# Optimizing a Trainium2 kernel written in Bass

```python
import numpy as np
import jax
import jax.numpy as jnp

def _softmax(x, axis=-1):
    return jax.nn.softmax(x, axis=axis)

def _gelu(x):
    return jax.nn.gelu(x, approximate=True)

def _silu(x):
    return jax.nn.silu(x)

def _sigmoid(x):
    return jax.nn.sigmoid(x)

def _layernorm(x, axis=-1, eps=1e-05):
    m = jnp.mean(x, axis=axis, keepdims=True)
    v = jnp.var(x, axis=axis, keepdims=True)
    return (x - m) / jnp.sqrt(v + eps)

def _scatter_add(tgt, idx, src, axis=0):
    return tgt.at[idx].add(src)

def _segment_sum(src, seg, n):
    return jax.ops.segment_sum(src, seg, n)
kernel_name = 'mk_decoder_postln_d2_seqx_r8_e9dd71'

def setup_inputs(seed: int=0):
    np.random.seed(seed)
    _w = jnp.asarray

    def _rec_inputs():
        import jax
        import jax.numpy as jnp
        _rk = jax.random.key(seed)
        x = 4.136e-05 + 0.9999 * jax.random.normal(jax.random.fold_in(_rk, 1), (4, 256, 256), jnp.float32)
        _lenS = 256 - jax.random.randint(jax.random.fold_in(_rk, 7), (4,), 0, max(1, 256 // 4) + 1, jnp.int32)
        _lenS2 = 256 - jax.random.randint(jax.random.fold_in(_rk, 8), (4,), 0, max(1, 256 // 4) + 1, jnp.int32)
        _ctx_1024P = jax.random.normal(jax.random.fold_in(_rk, 11), (4, 16, 128), jnp.float32)
        _ctx_1024c = jax.random.dirichlet(jax.random.fold_in(_rk, 511), 0.3 * jnp.ones((16,), jnp.float32), (4, 256))
        _ctx_1024t = jnp.einsum('bsk,bkd->bsd', _ctx_1024c, _ctx_1024P)
        _ctx_1024t = _ctx_1024t * jax.lax.rsqrt(jnp.mean(jnp.square(_ctx_1024t)) + 1e-12) * 0.953939
        ctx_1024 = -0.000292821 + 1.00034 * (_ctx_1024t + 0.3 * jax.random.normal(jax.random.fold_in(_rk, 611), (4, 256, 128), jnp.float32))
        fside_BxSx2_0 = jax.random.uniform(jax.random.fold_in(_rk, 12), (4, 256, 2), jnp.float32, 0.0, 0.999707)
        return (x, ctx_1024, fside_BxSx2_0)
    x, ctx_1024, fside_BxSx2_0 = _rec_inputs()

    def _L0_attn_setup():
        import jax, jax.numpy as jnp
        import numpy as np
        B, T, D = (1, 256, 256)
        H, DK, DV, M = (16, 64, 128, 64)
        KEY_DIM, VALUE_DIM = (H * DK, H * DV)
        EPS = 1e-05
        CLAMP_MIN, CLAMP_MAX = (-32.0, 32.0)
        XAVIER_GAIN = 2.0 ** (-2.5)

        def _chunk_abc(q, k, v, s):
            scale = q.shape[-1] ** (-0.5)
            z = jax.lax.cumlogsumexp(s, axis=2)
            g = jnp.exp(jnp.concatenate([z[:, :, :1], z[:, :, :-1]], axis=2) - z)
            p = jnp.exp(s - z)
            tfirst = lambda x: jnp.moveaxis(x, 2, 0)
            qT, kT, vT, pT, gT = map(tfirst, (q * scale, k, v, p, g))
            b, h = (q.shape[0], q.shape[1])
            hk0 = jnp.zeros((b, h, q.shape[-1], s.shape[-1]), q.dtype)

            def step_k(hk, x):
                q_t, k_t, p_t, g_t = x
                hk = hk * g_t[:, :, None, :] + k_t[..., None] * p_t[:, :, None, :]
                return (hk, jnp.einsum('bhk,bhkm->bhm', q_t, hk))
            _, okT = jax.lax.scan(step_k, hk0, (qT, kT, pT, gT))
            pvT = jax.nn.softmax(okT, axis=-1)
            hv0 = jnp.zeros((b, h, s.shape[-1], v.shape[-1]), q.dtype)

            def step_v(hv, x):
                pv_t, v_t, p_t, g_t = x
                hv = hv * g_t[..., None] + p_t[..., None] * v_t[:, :, None, :]
                return (hv, jnp.einsum('bhm,bhmv->bhv', pv_t, hv))
            _, ovT = jax.lax.scan(step_v, hv0, (pvT, vT, pT, gT))
            return jnp.moveaxis(ovT, 0, 2)
        key = jax.random.key(seed)
        ks = jax.random.split(key, 8)

        def w(k, fan_in, fan_out):
            std = XAVIER_GAIN * np.sqrt(2.0 / (fan_in + fan_out))
            return jax.random.normal(k, (fan_in, fan_out), jnp.float32) * std
        return {'hidden_states': jax.random.normal(ks[0], (B, T, D), jnp.float32), 'Wq': w(ks[1], D, KEY_DIM), 'Wk': w(ks[2], D, KEY_DIM), 'Wv': w(ks[3], D, VALUE_DIM), 'Wg': w(ks[4], D, VALUE_DIM), 'Ws': w(ks[5], D, H * M), 'Wo': w(ks[6], VALUE_DIM, D), 'g_norm_weight': jnp.ones((DV,), jnp.float32)}
    _L0_attn_all = _L0_attn_setup()
    _L0_attn_in = {k: v for k, v in _L0_attn_all.items() if k in ('Wq', 'Wk', 'Wv', 'Wg', 'Ws', 'Wo', 'g_norm_weight')}
    del _L0_attn_all

    def _L0_xattn_setup():
        import jax, jax.numpy as jnp
        import numpy as np
        import math
        B, L, DM = (2, 256, 128)
        DS, DC, EXP = (16, 4, 2)
        DI = EXP * DM
        DR = math.ceil(DM / 16)
        DT_MIN, DT_MAX, DT_FLOOR = (0.001, 0.1, 0.0001)

        def _ssm_forward(hidden_states, z, in_proj_w, conv_w, conv_b, x_proj_w, dt_proj_w, dt_proj_b, A_log, D):
            b = hidden_states.shape[0]
            x = jnp.einsum('ed,bld->bel', in_proj_w, hidden_states)
            xp = jnp.pad(x, ((0, 0), (0, 0), (DC - 1, 0)))
            xc = jax.lax.conv_general_dilated(xp, conv_w[:, None, :], window_strides=(1,), padding='VALID', dimension_numbers=('NCH', 'OIH', 'NCH'), feature_group_count=DI)
            u = jax.nn.silu(xc + conv_b[None, :, None])
            x_dbl = jnp.einsum('ke,bel->bkl', x_proj_w, u)
            dt_lo = x_dbl[:, :DR]
            Bm = x_dbl[:, DR:DR + DS]
            Cm = x_dbl[:, DR + DS:]
            delta = jax.nn.softplus(jnp.einsum('er,brl->bel', dt_proj_w, dt_lo) + dt_proj_b[None, :, None])
            A = -jnp.exp(A_log)

            def step(state, xs):
                d_t, B_t, C_t, u_t = xs
                dA = jnp.exp(d_t[..., None] * A)
                state = state * dA + (d_t * u_t)[..., None] * B_t[:, None, :]
                y_t = jnp.einsum('ben,bn->be', state, C_t)
                return (state, y_t)
            xs = (jnp.moveaxis(delta, -1, 0), jnp.moveaxis(Bm, -1, 0), jnp.moveaxis(Cm, -1, 0), jnp.moveaxis(u, -1, 0))
            state0 = jnp.zeros((b, DI, DS), delta.dtype)
            _, ys = jax.lax.scan(step, state0, xs)
            y = jnp.moveaxis(ys, 0, -1)
            y = y + D[None, :, None] * u
            y = y * jax.nn.silu(z)
            return jnp.swapaxes(y, 1, 2)
        key = jax.random.key(seed)
        ks = jax.random.split(key, 8)
        hidden_states = jax.random.normal(ks[0], (B, L, DM), jnp.float32)
        z = jax.random.normal(ks[1], (B, DI, L), jnp.float32)
        in_proj_w = jax.random.normal(ks[2], (DI, DM), jnp.float32) * DM ** (-0.5)
        conv_w = jax.random.normal(ks[3], (DI, DC), jnp.float32) * DC ** (-0.5)
        conv_b = jnp.zeros((DI,), jnp.float32)
        x_proj_w = jax.random.normal(ks[4], (DR + 2 * DS, DI), jnp.float32) * DI ** (-0.5)
        dt_std = DR ** (-0.5)
        dt_proj_w = jax.random.uniform(ks[5], (DI, DR), jnp.float32, -dt_std, dt_std)
        dt = jnp.exp(jax.random.uniform(ks[6], (DI,), jnp.float32) * (math.log(DT_MAX) - math.log(DT_MIN)) + math.log(DT_MIN))
        dt = jnp.clip(dt, DT_FLOOR)
        dt_proj_b = dt + jnp.log(-jnp.expm1(-dt))
        A_log = jnp.log(jnp.broadcast_to(jnp.arange(1, DS + 1, dtype=jnp.float32), (DI, DS)))
        D = jnp.ones((DI,), jnp.float32)
        return dict(hidden_states=hidden_states, z=z, in_proj_w=in_proj_w, conv_w=conv_w, conv_b=conv_b, x_proj_w=x_proj_w, dt_proj_w=dt_proj_w, dt_proj_b=dt_proj_b, A_log=A_log, D=D)
    _L0_xattn_all = _L0_xattn_setup()
    _L0_xattn_in = {k: v for k, v in _L0_xattn_all.items() if k in ('in_proj_w', 'conv_w', 'conv_b', 'x_proj_w', 'dt_proj_w', 'dt_proj_b', 'A_log', 'D')}
    del _L0_xattn_all

    def _L0_ffn_setup():
        import jax, jax.numpy as jnp
        import numpy as np
        E, K, H, F_EXP = (64, 6, 256, 176)
        B, S = (1, 64)

        def _swiglu(x, g, v, o):
            return jax.nn.silu(x @ g) * (x @ v) @ o
        key = jax.random.key(seed)
        ks = jax.random.split(key, 8)
        s_h = 1.0 / np.sqrt(H)
        s_f = 1.0 / np.sqrt(F_EXP)
        return {'hidden_states': jax.random.normal(ks[0], (B, S, H), jnp.float32), 'w_router': jax.random.normal(ks[1], (E, H), jnp.float32) * s_h, 'wg': jax.random.normal(ks[2], (E, H, F_EXP), jnp.float32) * s_h, 'wv': jax.random.normal(ks[3], (E, H, F_EXP), jnp.float32) * s_h, 'wo': jax.random.normal(ks[4], (E, F_EXP, H), jnp.float32) * s_f, 'swg': jax.random.normal(ks[5], (H, F_EXP), jnp.float32) * s_h, 'swv': jax.random.normal(ks[6], (H, F_EXP), jnp.float32) * s_h, 'swo': jax.random.normal(ks[7], (F_EXP, H), jnp.float32) * s_f}
    _L0_ffn_all = _L0_ffn_setup()
    _L0_ffn_in = {k: v for k, v in _L0_ffn_all.items() if k in ('w_router', 'wg', 'wv', 'wo', 'swg', 'swv', 'swo')}
    del _L0_ffn_all

    def _L1_attn_setup():
        import jax, jax.numpy as jnp
        import numpy as np
        D_MODEL = 256
        NUM_HEADS = 16
        D_K = D_MODEL // NUM_HEADS

        def _heads(t, B, S):
            return t.reshape(B, S, NUM_HEADS, D_K).transpose(0, 2, 1, 3)
        key = jax.random.key(seed)
        ks = jax.random.split(key, 9)
        s = 1.0 / np.sqrt(D_MODEL)
        x = jax.random.normal(ks[0], (4, 512, D_MODEL), dtype=jnp.float32)
        wq = jax.random.uniform(ks[1], (D_MODEL, D_MODEL), jnp.float32, -s, s)
        bq = jax.random.uniform(ks[2], (D_MODEL,), jnp.float32, -s, s)
        wk = jax.random.uniform(ks[3], (D_MODEL, D_MODEL), jnp.float32, -s, s)
        bk = jax.random.uniform(ks[4], (D_MODEL,), jnp.float32, -s, s)
        wv = jax.random.uniform(ks[5], (D_MODEL, D_MODEL), jnp.float32, -s, s)
        bv = jax.random.uniform(ks[6], (D_MODEL,), jnp.float32, -s, s)
        wo = jax.random.uniform(ks[7], (D_MODEL, D_MODEL), jnp.float32, -s, s)
        bo = jax.random.uniform(ks[8], (D_MODEL,), jnp.float32, -s, s)
        return {'x': x, 'wq': wq, 'bq': bq, 'wk': wk, 'bk': bk, 'wv': wv, 'bv': bv, 'wo': wo, 'bo': bo}
    _L1_attn_all = _L1_attn_setup()
    _L1_attn_in = {k: v for k, v in _L1_attn_all.items() if k in ('wq', 'bq', 'wk', 'bk', 'wv', 'bv', 'wo', 'bo')}
    del _L1_attn_all

    def _L1_xattn_setup():
        import jax, jax.numpy as jnp
        import numpy as np
        DIM = 256
        CTX_DIM = 128
        N_HEADS = 32
        HEAD_DIM = DIM // N_HEADS
        POS_DIM = 2
        B, N, CTXN = (2, 256, 256)
        ROPE_BASE = 10000.0

        def apply_axial_rope(x, pos):
            b, n, h, d = x.shape
            p = pos.shape[-1]
            dpa = d // p
            half = dpa // 2
            freqs = ROPE_BASE ** (-jnp.arange(half, dtype=x.dtype) / half)
            ang = pos[..., :, None] * freqs
            cos = jnp.cos(ang)[:, :, None, :, :]
            sin = jnp.sin(ang)[:, :, None, :, :]
            xr = x.reshape(b, n, h, p, half, 2)
            x1, x2 = (xr[..., 0], xr[..., 1])
            out = jnp.stack([x1 * cos - x2 * sin, x1 * sin + x2 * cos], axis=-1)
            return out.reshape(b, n, h, d)
        key = jax.random.key(seed)
        ks = jax.random.split(key, 8)
        x = jax.random.normal(ks[0], (B, N, DIM), jnp.float32)
        ctx = jax.random.normal(ks[1], (B, CTXN, CTX_DIM), jnp.float32)
        pos_map = jax.random.uniform(ks[2], (B, N, POS_DIM), jnp.float32)
        ctx_pos_map = jax.random.uniform(ks[3], (B, CTXN, POS_DIM), jnp.float32)
        Wq = jax.random.normal(ks[4], (DIM, DIM), jnp.float32) / np.sqrt(DIM)
        Wkv = jax.random.normal(ks[5], (CTX_DIM, 2 * DIM), jnp.float32) / np.sqrt(CTX_DIM)
        Wout = jax.random.normal(ks[6], (DIM, DIM), jnp.float32) / np.sqrt(DIM)
        bout = jnp.zeros((DIM,), jnp.float32)
        return {'x': x, 'ctx': ctx, 'pos_map': pos_map, 'ctx_pos_map': ctx_pos_map, 'Wq': Wq, 'Wkv': Wkv, 'Wout': Wout, 'bout': bout}
    _L1_xattn_all = _L1_xattn_setup()
    _L1_xattn_in = {k: v for k, v in _L1_xattn_all.items() if k in ('Wq', 'Wkv', 'Wout', 'bout')}
    del _L1_xattn_all

    def _L1_ffn_setup():
        import jax, jax.numpy as jnp
        import numpy as np
        EPS = 1e-05
        NUM_BITS = 8

        def _round_ste(x):
            return x + jax.lax.stop_gradient(jnp.round(x) - x)

        def _clamp_ste(x, lo=-1.0, hi=1.0):
            return x + jax.lax.stop_gradient(jnp.clip(x, lo, hi) - x)

        def ternary_quantize(w):
            scale = jnp.maximum(jnp.mean(jnp.abs(w)), EPS)
            q = _clamp_ste(_round_ste(w / scale))
            return scale * q

        def quantized_relu2(x, num_bits=NUM_BITS, eps=EPS):
            x = jnp.square(jax.nn.relu(x))
            xmax = jnp.maximum(jnp.max(x, axis=-1, keepdims=True), eps)
            num_steps = 2 ** num_bits - 1
            return _round_ste(x / xmax * num_steps) / num_steps * xmax
        key = jax.random.key(seed)
        k1, k2, k3 = jax.random.split(key, 3)
        B, S, D = (4, 256, 256)
        H = 4 * D
        std = 0.5 * D ** (-0.5)
        x = jax.random.normal(k1, (B, S, D), dtype=jnp.float32)
        c_fc = jax.random.normal(k2, (D, H), dtype=jnp.float32) * std
        c_proj = jax.random.normal(k3, (D, H), dtype=jnp.float32) * std
        return {'x': x, 'c_fc': c_fc, 'c_proj': c_proj}
    _L1_ffn_all = _L1_ffn_setup()
    _L1_ffn_in = {k: v for k, v in _L1_ffn_all.items() if k in ('c_fc', 'c_proj')}
    del _L1_ffn_all
    return {'x': x, 'ctx_1024': ctx_1024, 'fside_BxSx2_0': fside_BxSx2_0, 'L0_attn_Wq': _L0_attn_in['Wq'], 'L0_attn_Wk': _L0_attn_in['Wk'], 'L0_attn_Wv': _L0_attn_in['Wv'], 'L0_attn_Wg': _L0_attn_in['Wg'], 'L0_attn_Ws': _L0_attn_in['Ws'], 'L0_attn_Wo': _L0_attn_in['Wo'], 'L0_attn_g_norm_weight': _L0_attn_in['g_norm_weight'], 'L0_xattn_in_proj_w': _L0_xattn_in['in_proj_w'], 'L0_xattn_conv_w': _L0_xattn_in['conv_w'], 'L0_xattn_conv_b': _L0_xattn_in['conv_b'], 'L0_xattn_x_proj_w': _L0_xattn_in['x_proj_w'], 'L0_xattn_dt_proj_w': _L0_xattn_in['dt_proj_w'], 'L0_xattn_dt_proj_b': _L0_xattn_in['dt_proj_b'], 'L0_xattn_A_log': _L0_xattn_in['A_log'], 'L0_xattn_D': _L0_xattn_in['D'], 'L0_ffn_w_router': _L0_ffn_in['w_router'], 'L0_ffn_wg': _L0_ffn_in['wg'], 'L0_ffn_wv': _L0_ffn_in['wv'], 'L0_ffn_wo': _L0_ffn_in['wo'], 'L0_ffn_swg': _L0_ffn_in['swg'], 'L0_ffn_swv': _L0_ffn_in['swv'], 'L0_ffn_swo': _L0_ffn_in['swo'], 'L1_attn_wq': _L1_attn_in['wq'], 'L1_attn_bq': _L1_attn_in['bq'], 'L1_attn_wk': _L1_attn_in['wk'], 'L1_attn_bk': _L1_attn_in['bk'], 'L1_attn_wv': _L1_attn_in['wv'], 'L1_attn_bv': _L1_attn_in['bv'], 'L1_attn_wo': _L1_attn_in['wo'], 'L1_attn_bo': _L1_attn_in['bo'], 'L1_xattn_Wq': _L1_xattn_in['Wq'], 'L1_xattn_Wkv': _L1_xattn_in['Wkv'], 'L1_xattn_Wout': _L1_xattn_in['Wout'], 'L1_xattn_bout': _L1_xattn_in['bout'], 'L1_ffn_c_fc': _L1_ffn_in['c_fc'], 'L1_ffn_c_proj': _L1_ffn_in['c_proj']}

def reference(x, ctx_1024, fside_BxSx2_0, L0_attn_Wq, L0_attn_Wk, L0_attn_Wv, L0_attn_Wg, L0_attn_Ws, L0_attn_Wo, L0_attn_g_norm_weight, L0_xattn_in_proj_w, L0_xattn_conv_w, L0_xattn_conv_b, L0_xattn_x_proj_w, L0_xattn_dt_proj_w, L0_xattn_dt_proj_b, L0_xattn_A_log, L0_xattn_D, L0_ffn_w_router, L0_ffn_wg, L0_ffn_wv, L0_ffn_wo, L0_ffn_swg, L0_ffn_swv, L0_ffn_swo, L1_attn_wq, L1_attn_bq, L1_attn_wk, L1_attn_bk, L1_attn_wv, L1_attn_bv, L1_attn_wo, L1_attn_bo, L1_xattn_Wq, L1_xattn_Wkv, L1_xattn_Wout, L1_xattn_bout, L1_ffn_c_fc, L1_ffn_c_proj):
    import jax
    import jax.numpy as jnp

    def _L0_attn_ref(hidden_states, Wq, Wk, Wv, Wg, Ws, Wo, g_norm_weight):
        import jax, jax.numpy as jnp
        import numpy as np
        B, T, D = (1, 256, 256)
        H, DK, DV, M = (16, 64, 128, 64)
        KEY_DIM, VALUE_DIM = (H * DK, H * DV)
        EPS = 1e-05
        CLAMP_MIN, CLAMP_MAX = (-32.0, 32.0)
        XAVIER_GAIN = 2.0 ** (-2.5)

        def _chunk_abc(q, k, v, s):
            scale = q.shape[-1] ** (-0.5)
            z = jax.lax.cumlogsumexp(s, axis=2)
            g = jnp.exp(jnp.concatenate([z[:, :, :1], z[:, :, :-1]], axis=2) - z)
            p = jnp.exp(s - z)
            tfirst = lambda x: jnp.moveaxis(x, 2, 0)
            qT, kT, vT, pT, gT = map(tfirst, (q * scale, k, v, p, g))
            b, h = (q.shape[0], q.shape[1])
            hk0 = jnp.zeros((b, h, q.shape[-1], s.shape[-1]), q.dtype)

            def step_k(hk, x):
                q_t, k_t, p_t, g_t = x
                hk = hk * g_t[:, :, None, :] + k_t[..., None] * p_t[:, :, None, :]
                return (hk, jnp.einsum('bhk,bhkm->bhm', q_t, hk))
            _, okT = jax.lax.scan(step_k, hk0, (qT, kT, pT, gT))
            pvT = jax.nn.softmax(okT, axis=-1)
            hv0 = jnp.zeros((b, h, s.shape[-1], v.shape[-1]), q.dtype)

            def step_v(hv, x):
                pv_t, v_t, p_t, g_t = x
                hv = hv * g_t[..., None] + p_t[..., None] * v_t[:, :, None, :]
                return (hv, jnp.einsum('bhm,bhmv->bhv', pv_t, hv))
            _, ovT = jax.lax.scan(step_v, hv0, (pvT, vT, pT, gT))
            return jnp.moveaxis(ovT, 0, 2)
        b, t, _ = hidden_states.shape
        to_heads = lambda x, d: jnp.transpose(x.reshape(b, t, H, d), (0, 2, 1, 3))
        q = to_heads(hidden_states @ Wq, DK)
        k = to_heads(hidden_states @ Wk, DK)
        v = to_heads(hidden_states @ Wv, DV)
        s = jnp.clip(to_heads(hidden_states @ Ws, M), CLAMP_MIN, CLAMP_MAX)
        o = jnp.transpose(_chunk_abc(q, k, v, s), (0, 2, 1, 3))
        g = (hidden_states @ Wg).reshape(b, t, H, DV)
        o = o * jax.lax.rsqrt(jnp.mean(jnp.square(o), axis=-1, keepdims=True) + EPS) * g_norm_weight
        o = o * (g * jax.nn.sigmoid(g))
        return o.reshape(b, t, VALUE_DIM) @ Wo

    def _L0_xattn_ref(hidden_states, z, in_proj_w, conv_w, conv_b, x_proj_w, dt_proj_w, dt_proj_b, A_log, D):
        import jax, jax.numpy as jnp
        import numpy as np
        import math
        B, L, DM = (2, 256, 128)
        DS, DC, EXP = (16, 4, 2)
        DI = EXP * DM
        DR = math.ceil(DM / 16)
        DT_MIN, DT_MAX, DT_FLOOR = (0.001, 0.1, 0.0001)

        def _ssm_forward(hidden_states, z, in_proj_w, conv_w, conv_b, x_proj_w, dt_proj_w, dt_proj_b, A_log, D):
            b = hidden_states.shape[0]
            x = jnp.einsum('ed,bld->bel', in_proj_w, hidden_states)
            xp = jnp.pad(x, ((0, 0), (0, 0), (DC - 1, 0)))
            xc = jax.lax.conv_general_dilated(xp, conv_w[:, None, :], window_strides=(1,), padding='VALID', dimension_numbers=('NCH', 'OIH', 'NCH'), feature_group_count=DI)
            u = jax.nn.silu(xc + conv_b[None, :, None])
            x_dbl = jnp.einsum('ke,bel->bkl', x_proj_w, u)
            dt_lo = x_dbl[:, :DR]
            Bm = x_dbl[:, DR:DR + DS]
            Cm = x_dbl[:, DR + DS:]
            delta = jax.nn.softplus(jnp.einsum('er,brl->bel', dt_proj_w, dt_lo) + dt_proj_b[None, :, None])
            A = -jnp.exp(A_log)

            def step(state, xs):
                d_t, B_t, C_t, u_t = xs
                dA = jnp.exp(d_t[..., None] * A)
                state = state * dA + (d_t * u_t)[..., None] * B_t[:, None, :]
                y_t = jnp.einsum('ben,bn->be', state, C_t)
                return (state, y_t)
            xs = (jnp.moveaxis(delta, -1, 0), jnp.moveaxis(Bm, -1, 0), jnp.moveaxis(Cm, -1, 0), jnp.moveaxis(u, -1, 0))
            state0 = jnp.zeros((b, DI, DS), delta.dtype)
            _, ys = jax.lax.scan(step, state0, xs)
            y = jnp.moveaxis(ys, 0, -1)
            y = y + D[None, :, None] * u
            y = y * jax.nn.silu(z)
            return jnp.swapaxes(y, 1, 2)
        return _ssm_forward(hidden_states, z, in_proj_w, conv_w, conv_b, x_proj_w, dt_proj_w, dt_proj_b, A_log, D)

    def _L0_ffn_ref(hidden_states, w_router, wg, wv, wo, swg, swv, swo):
        import jax, jax.numpy as jnp
        import numpy as np
        E, K, H, F_EXP = (64, 6, 256, 176)
        B, S = (1, 64)

        def _swiglu(x, g, v, o):
            return jax.nn.silu(x @ g) * (x @ v) @ o
        b, s, h = hidden_states.shape
        x = hidden_states.reshape(-1, h)
        T = x.shape[0]
        scores = jax.nn.softmax(x @ w_router.T, axis=-1)
        topw, topi = jax.lax.top_k(scores, K)
        combine = jnp.zeros((T, E), x.dtype).at[jnp.arange(T)[:, None], topi].add(topw)

        def body(acc, ws):
            g, v, o, cw = ws
            return (acc + cw[:, None] * _swiglu(x, g, v, o), None)
        routed, _ = jax.lax.scan(body, jnp.zeros_like(x), (wg, wv, wo, combine.T))
        shared = _swiglu(x, swg, swv, swo)
        return (routed + shared).reshape(b, s, h)

    def _L1_attn_ref(x, wq, bq, wk, bk, wv, bv, wo, bo):
        import jax, jax.numpy as jnp
        import numpy as np
        D_MODEL = 256
        NUM_HEADS = 16
        D_K = D_MODEL // NUM_HEADS

        def _heads(t, B, S):
            return t.reshape(B, S, NUM_HEADS, D_K).transpose(0, 2, 1, 3)
        B, S, _ = x.shape
        Q = _heads(x @ wq.T + bq, B, S)
        K = _heads(x @ wk.T + bk, B, S)
        V = _heads(x @ wv.T + bv, B, S)
        Q = jax.nn.elu(Q) + 1.0
        K = jax.nn.elu(K) + 1.0
        KV = jnp.einsum('bhsd,bhse->bhde', K, V)
        QKV = jnp.einsum('bhsd,bhde->bhse', Q, KV)
        K_sum = jnp.sum(K, axis=-2)
        QK_sum = jnp.einsum('bhsd,bhd->bhs', Q, K_sum)
        out = QKV / (QK_sum[..., None] + 1e-08)
        out = out.transpose(0, 2, 1, 3).reshape(B, S, D_MODEL)
        return out @ wo.T + bo

    def _L1_xattn_ref(x, ctx, pos_map, ctx_pos_map, Wq, Wkv, Wout, bout):
        import jax, jax.numpy as jnp
        import numpy as np
        DIM = 256
        CTX_DIM = 128
        N_HEADS = 32
        HEAD_DIM = DIM // N_HEADS
        POS_DIM = 2
        B, N, CTXN = (2, 256, 256)
        ROPE_BASE = 10000.0

        def apply_axial_rope(x, pos):
            b, n, h, d = x.shape
            p = pos.shape[-1]
            dpa = d // p
            half = dpa // 2
            freqs = ROPE_BASE ** (-jnp.arange(half, dtype=x.dtype) / half)
            ang = pos[..., :, None] * freqs
            cos = jnp.cos(ang)[:, :, None, :, :]
            sin = jnp.sin(ang)[:, :, None, :, :]
            xr = x.reshape(b, n, h, p, half, 2)
            x1, x2 = (xr[..., 0], xr[..., 1])
            out = jnp.stack([x1 * cos - x2 * sin, x1 * sin + x2 * cos], axis=-1)
            return out.reshape(b, n, h, d)
        b, n, _ = x.shape
        ctx_n = ctx.shape[1]
        q = (x @ Wq).reshape(b, n, N_HEADS, HEAD_DIM)
        k, v = jnp.split(ctx @ Wkv, 2, axis=-1)
        k = k.reshape(b, ctx_n, N_HEADS, HEAD_DIM)
        v = v.reshape(b, ctx_n, N_HEADS, HEAD_DIM)
        q = apply_axial_rope(q, pos_map)
        k = apply_axial_rope(k, ctx_pos_map)
        scale = 1.0 / np.sqrt(HEAD_DIM).astype(np.float32)
        logits = jnp.einsum('bqhd,bkhd->bhqk', q, k) * scale
        w = jax.nn.softmax(logits, axis=-1)
        attn = jnp.einsum('bhqk,bkhd->bqhd', w, v)
        attn = attn.reshape(b, n, N_HEADS * HEAD_DIM)
        return attn @ Wout + bout

    def _L1_ffn_ref(x, c_fc, c_proj):
        import jax, jax.numpy as jnp
        import numpy as np
        EPS = 1e-05
        NUM_BITS = 8

        def _round_ste(x):
            return x + jax.lax.stop_gradient(jnp.round(x) - x)

        def _clamp_ste(x, lo=-1.0, hi=1.0):
            return x + jax.lax.stop_gradient(jnp.clip(x, lo, hi) - x)

        def ternary_quantize(w):
            scale = jnp.maximum(jnp.mean(jnp.abs(w)), EPS)
            q = _clamp_ste(_round_ste(w / scale))
            return scale * q

        def quantized_relu2(x, num_bits=NUM_BITS, eps=EPS):
            x = jnp.square(jax.nn.relu(x))
            xmax = jnp.maximum(jnp.max(x, axis=-1, keepdims=True), eps)
            num_steps = 2 ** num_bits - 1
            return _round_ste(x / xmax * num_steps) / num_steps * xmax
        w1 = ternary_quantize(c_fc)
        h = jnp.einsum('bsd,dh->bsh', x, w1)
        h = quantized_relu2(h, num_bits=NUM_BITS)
        w2 = ternary_quantize(c_proj)
        out = jnp.einsum('bsh,dh->bsd', h, w2)
        return out
    x = _layernorm(x + _L0_attn_ref(x, L0_attn_Wq, L0_attn_Wk, L0_attn_Wv, L0_attn_Wg, L0_attn_Ws, L0_attn_Wo, L0_attn_g_norm_weight), axis=-1)
    x = _layernorm(x + _L0_xattn_ref(ctx_1024, x, L0_xattn_in_proj_w, L0_xattn_conv_w, L0_xattn_conv_b, L0_xattn_x_proj_w, L0_xattn_dt_proj_w, L0_xattn_dt_proj_b, L0_xattn_A_log, L0_xattn_D), axis=-1)
    x = _layernorm(x + _L0_ffn_ref(x, L0_ffn_w_router, L0_ffn_wg, L0_ffn_wv, L0_ffn_wo, L0_ffn_swg, L0_ffn_swv, L0_ffn_swo), axis=-1)
    x = _layernorm(x + _L1_attn_ref(x, L1_attn_wq, L1_attn_bq, L1_attn_wk, L1_attn_bk, L1_attn_wv, L1_attn_bv, L1_attn_wo, L1_attn_bo), axis=-1)
    x = _layernorm(x + _L1_xattn_ref(x, ctx_1024, fside_BxSx2_0, fside_BxSx2_0, L1_xattn_Wq, L1_xattn_Wkv, L1_xattn_Wout, L1_xattn_bout), axis=-1)
    x = _layernorm(x + _L1_ffn_ref(x, L1_ffn_c_fc, L1_ffn_c_proj), axis=-1)
    return x

_drawn_inputs = setup_inputs


def setup_inputs(seed=0):
    import zlib

    import numpy as np

    out = dict(_drawn_inputs(seed))
    spreads = {'L0_attn_g_norm_weight': (1.0, 0.6),
     'L0_xattn_conv_b': (0.0, 0.1),
     'L0_xattn_D': (1.0, 0.2),
     'L1_xattn_bout': (0.0, 0.1)}
    factors = {'L0_attn_Wq': 32.436,
     'L0_attn_Wk': 32.538,
     'L0_attn_Wv': 5.406,
     'L0_attn_Wg': 5.367,
     'L0_attn_Ws': 8.0,
     'L0_attn_Wo': 5.381,
     'L0_xattn_dt_proj_w': 5.756,
     'L1_attn_wq': 45.623,
     'L1_attn_bq': 64.0,
     'L1_attn_wk': 34.851,
     'L1_attn_bk': 64.0,
     'L1_attn_bv': 3.202}
    for name, (base, spread) in spreads.items():
        noise = np.random.default_rng([zlib.crc32(name.encode()), seed]).standard_normal(out[name].shape)
        drawn = base * np.exp(spread * noise) if base else spread * noise
        out[name] = jnp.asarray(drawn.astype(out[name].dtype))
    for name, factor in factors.items():
        out[name] = (out[name] * factor).astype(out[name].dtype)
    return out
```

```python
from contextlib import ExitStack

import numpy as np

import concourse.bass as bass
from concourse import mybir

F32 = mybir.dt.float32
BF16 = mybir.dt.bfloat16
ALU = mybir.AluOpType
ACT = mybir.ActivationFunctionType
AX = mybir.AxisListType

P = 128
B, T, D = 4, 256, 256
TOK = B * T
TILES = TOK // P
KD = D // P
LN_EPS = 1e-5
H, DK, DV, M = 16, 64, 128, 64
PAIRS = H // 2
CLAMP = 32.0
CTX = 128
DI, DS, DR, DC = 256, 16, 8, 4
ET = DI // P
XD = DR + 2 * DS
E, TOPK, F = 64, 6, 176
FH = F // 2
SC = E + 2
NJ = 4
NBLK = -(-((TOK * TOPK + E * (P - 1)) // P) // NJ) * NJ
ROUND = 1.5 * 2.0 ** 23
LH = 16
LB = P // (D // LH)
KVW = P + LB
XH, XD_H = 32, 8
XPAIRS = XH // 2
SLOT = 64
VA = XD_H + 1
HF = 4 * D
KH = HF // P


TURN = dict(x1=0, x2=1, att0=2, x3=3, att1=4, x4=5)


def at(i, per, c):
    return i * per + c


def build(nc, a, out):
    with ExitStack() as ctx:
        mem = [ctx]

        def sb(name, shape, dt=F32):
            return mem[-1].enter_context(nc.sbuf_tensor(name, shape, dt))

        def sem(name):
            return ctx.enter_context(nc.semaphore(name))

        ps = ctx.enter_context(nc.psum_tensor("ps", [P, 8, 512], F32))
        PJ, AB, X, Y = 0, 2, 4, 6

        xres = sb("xres", [P, TILES, D])
        xT = sb("xT", [P, KD, TOK])
        ident = sb("ident", [P, P])
        tri = sb("tri", [P, 384])
        ones = sb("ones", [P, 256])
        ctxT = sb("ctxT", [P, TOK])
        stats = sb("stats", [P, TILES, 6])
        moments = sb("moments", [P, TILES, 2])
        ln_var = sb("ln_var", [P, TILES])
        ln_rstd = sb("ln_rstd", [P, TILES])
        ln_shift = sb("ln_shift", [P, TILES])
        eps_col = sb("eps_col", [P, 1])
        attn_mem = ExitStack()
        mem.append(attn_mem)
        w_qks = sb("w_qks", [P, KD, 384])
        w_vg = sb("w_vg", [P, KD, 512])
        w_o = sb("w_o", [P, 2, D])
        gn_half = sb("gn_half", [P, 1])
        qT = sb("qT", [P, TOK])
        kT = sb("kT", [P, TOK])
        sT = sb("sT", [P, TOK])
        eT = sb("eT", [P, TOK])
        e_tok = sb("e_tok", [P, TILES, P])
        zT = sb("zT", [P, TOK])
        zi = sb("zi", [P, TILES, P])
        aT = sb("aT", [P, 8, 384])
        okn = sb("okn", [P, TILES * 2, M])
        pe_ = sb("pexp", [P, TILES * 2, M])
        okmax = sb("okmax", [P, TILES * 2])
        psum_ = sb("psum_", [P, TILES * 2])
        wT = sb("wT", [P, TOK])
        v = sb("v", [P, TILES, 256])
        th = sb("th", [P, TILES, 256])
        on = sb("on", [P, TILES * 2, DV])
        sq = sb("sq", [P, 2, 4, DV])
        ss = sb("ss", [P, TILES * 2])
        lnv = sb("lnv", [P, TILES * 2])
        rstd = sb("rstd", [P, TILES * 2])
        oT = sb("oT", [P, 2, TOK])
        w_in = sb("w_in", [P, DI])
        xp_w = sb("xp_w", [P, ET, XD])
        dt_w = sb("dt_w", [DR, DI])
        s_cols = sb("s_cols", [P, ET, DC + 3])
        a_neg = sb("a_neg", [P, ET, DS])
        a_cur = sb("a_cur", [P, ET, 2])
        x_dbl = sb("x_dbl", [XD, TOK])
        u = sb("u", [P, ET, TOK])
        delta = sb("delta", [P, ET, TOK])
        du = sb("du", [P, ET, TOK])
        y = sb("y", [P, ET, TOK])
        b_row = sb("b_row", [P, 2, TOK])
        c_row = sb("c_row", [P, 2, TOK])
        decay = sb("decay", [P, 2, TOK])
        drive = sb("drive", [P, 2, TOK])
        state = sb("state", [P, 2, TOK])
        x_pad = aT[:].rearrange("p a b -> p (a b)")[:, 0:ET * B * (T + 3)].rearrange(
            "p (e b t) -> p e b t", e=ET, b=B)
        conv = v[:].rearrange("p a b -> p (a b)").rearrange("p (e n) -> p e n", e=ET)
        aux = th[:].rearrange("p a b -> p (a b)").rearrange("p (e n) -> p e n", e=ET)
        aux2 = on[:].rearrange("p a b -> p (a b)").rearrange("p (e n) -> p e n", e=ET)
        mem.pop()
        attn_mem.close()

        moe_mem = ExitStack()
        mem.append(moe_mem)
        U32 = mybir.dt.uint32
        w_router = sb("w_router", [P, KD, E])
        iota = sb("iota", [P, P])
        tok_id = sb("tok_id", [P, TILES])
        tri_bf = sb("tri_bf", [P, P], BF16)
        ones_bf = sb("ones_bf", [P, P], BF16)
        top_logit = sb("top_logit", [P, TILES])
        score_sum = sb("score_sum", [P, TILES])
        score = sb("score", [P, TILES, SC])
        score_rest = sb("score_rest", [P, TILES, SC])
        top8 = sb("top8", [P, TILES, 8])
        chosen = sb("chosen", [P, TILES, E])
        chosen_bf = sb("chosen_bf", [P, TILES, E], BF16)
        blocks = sb("blocks", [P, E])
        blk_end = sb("blk_end", [P, E])
        blk_row = sb("blk_row", [P, E])
        place = sb("place", [P, TILES, E])
        place8 = sb("place8", [P, TILES, 8])
        slot = sb("slot", [P, TILES, TOPK])
        slot_blk = sb("slot_blk", [P, TILES, TOPK])
        slot_row = sb("slot_row", [P, TILES, TOPK])
        slot_idx = sb("slot_idx", [P, TILES, TOPK], U32)
        pick = sb("pick", [P, TOPK, E])
        pick_w = sb("pick_w", [P, TILES, TOPK])
        late = sb("late", [P, E])
        blk_expert = sb("blk_expert", [P, 1])
        expert_row = sb("expert_row", [1, P], mybir.dt.int32)
        row_hot = sb("row_hot", [P, 4, P])
        blk_hot = sb("blk_hot", [P, 4, NBLK])
        tok_of = sb("tok_of", [P, NBLK], U32)
        tok_cur = sb("tok_cur", [P, NJ], U32)
        xg = sb("xg", [P, NJ, D])
        xgT = sb("xgT", [P, NJ, KD * P])
        w_gv = sb("w_gv", [P, NJ, KD, 2 * F])
        w_dn = sb("w_dn", [FH, NJ, 2, D])
        sh_gv = sb("sh_gv", [P, KD, 2 * F])
        sh_dn = sb("sh_dn", [FH, 2, D])
        g_th = sb("g_th", [P, NJ, F])
        hid = sb("hid", [P, NJ, F])
        hidT = sb("hidT", [FH, NJ, 2 * P])
        y_out = sb("y_out", [P, NJ, D])
        yg = sb("yg", [P, 8, D])
        l_wq = sb("l_wq", [P, KD, D])
        l_wkv = sb("l_wkv", [P, KD, 2 * D])
        l_wo = sb("l_wo", [P, KD, D])
        l_bq = sb("l_bq", [P, KD])
        l_bkv = sb("l_bkv", [P, 2 * D])
        l_bo = sb("l_bo", [P, D])
        head_mask = sb("head_mask", [P, KVW])
        lqT = sb("lqT", [P, KD, TOK])
        lq_low = sb("lq_low", [P, 2, 512])
        lk = sb("lk", [P, TILES, D])
        lk_low = sb("lk_low", [P, 2, D])
        lv = sb("lv", [P, TILES, D])
        kv = sb("kv", [P, B * KD, KVW])
        l_den = sb("l_den", [P, TILES, KD, LB])
        l_out = sb("l_out", [P, TILES, D])
        mem.pop()
        moe_mem.close()
        last_mem = ExitStack()
        mem.append(last_mem)
        x_wq = sb("x_wq", [P, KD, D])
        x_wkv = sb("x_wkv", [P, 2 * D])
        x_wo = sb("x_wo", [P, KD, D])
        x_bo = sb("x_bo", [P, D])
        ident_bf = sb("ident_bf", [P, P], BF16)
        shift_sel = sb("shift_sel", [P, 8, P], BF16)
        pos = sb("pos", [P, TILES, 2])
        ang = sb("ang", [P, TILES, 2, 4])
        turns = sb("turns", [P, TILES, 2, 4])
        cos_sin = sb("cos_sin", [P, TILES, 2, 4])
        rot = sb("rot", [P, 2, 2, 512])
        q_rot = sb("q_rot", [P, TILES, D])
        k_rot = sb("k_rot", [P, TILES, D])
        v_aug = sb("v_aug", [P, TILES, XH, VA])
        part = sb("part", [P, 3, TILES, D], BF16)
        q_st = sb("q_st", [P, TILES, XH, SLOT], BF16)
        k_st = sb("k_st", [P, TILES, XH, SLOT], BF16)
        qsT = sb("qsT", [P, TOK], BF16)
        ksT = sb("ksT", [P, TOK], BF16)
        va_cur = sb("va_cur", [P, TILES, 2, VA])
        row_max = sb("row_max", [P, 16])
        shift = sb("shift", [P, 2, SLOT], BF16)
        shiftT = sb("shiftT", [P, P], BF16)
        probT = sb("probT", [P, 4, 2, 2 * P])
        x_den = sb("x_den", [P, 16])
        x_att = sb("x_att", [P, TILES, D])
        f_in = sb("f_in", [P, KD, HF])
        f_out = sb("f_out", [P, KH, D])
        f_sum = sb("f_sum", [P, 2])
        f_scale = sb("f_scale", [P, 2])
        f_inv = sb("f_inv", [P, 2])
        q_in = sb("q_in", [P, KD, HF], BF16)
        q_out = sb("q_out", [P, KH, D], BF16)
        x_part = part[:].rearrange("p a b c -> p a (b c)").rearrange("p a (k n) -> p a k n", k=KD)
        hid_f = q_rot[:].rearrange("p a b -> p (a b)").rearrange("p (a b) -> p a b", a=2)
        hid_q = k_rot[:].rearrange("p a b -> p (a b)").bitcast(BF16).rearrange("p (a b) -> p a b", a=4)
        f_max = sb("f_max", [P, 2])
        f_rmax = sb("f_rmax", [P, 2])
        f_back = sb("f_back", [P, 2])
        mem.pop()
        last_mem.close()

        x_dram = nc.dram_tensor("x_dram", (TOK, D), F32).ap()
        y_dram = nc.dram_tensor("y_dram", (NBLK * P, D), F32).ap()
        x_dbl_dram = nc.dram_tensor("x_dbl_dram", (XD, TOK), F32).ap()

        x_loaded = sem("x_loaded")
        const_loaded = sem("const_loaded")
        const_set = sem("const_set")
        qks_loaded = sem("qks_loaded")
        vg_loaded = sem("vg_loaded")
        wo_loaded = sem("wo_loaded")
        proj_ready = sem("proj_ready")
        qk_copied = sem("qk_copied")
        s_clipped = sem("s_clipped")
        eT_ready = sem("eT_ready")
        zT_ready = sem("zT_ready")
        lnz_ready = sem("lnz_ready")
        scores_ready = sem("scores_ready")
        scores_masked = sem("scores_masked")
        e_turned = sem("e_turned")
        e_copied = sem("e_copied")
        z_turned = sem("z_turned")
        zi_ready = sem("zi_ready")
        slots_ready = sem("slots_ready")
        slots_shifted = sem("slots_shifted")
        slots_exp = sem("slots_exp")
        w_ready = sem("w_ready")
        tanh_ready = sem("tanh_ready")
        gate_ready = sem("gate_ready")
        w_turned = sem("w_turned")
        wT_copied = sem("wT_copied")
        read_ready = sem("read_ready")
        read_masked = sem("read_masked")
        o_ready = sem("o_ready")
        squares_ready = sem("squares_ready")
        squares_read = sem("squares_read")
        rstd_ready = sem("rstd_ready")
        o_gated = sem("o_gated")
        o_turned = sem("o_turned")
        oT_copied = sem("oT_copied")
        mixed_ready = sem("mixed_ready")
        mixed_added = sem("mixed_added")
        vec_step = sem("vec_step")
        chain = sem("chain")
        act_step = sem("act_step")
        stored = sem("stored")
        scan_consts = sem("scan_consts")
        scan_mm = sem("scan_mm")
        inner_copied = sem("inner_copied")
        pool_set = sem("pool_set")
        conv_step = sem("conv_step")
        u_ready = sem("u_ready")
        x_dbl_copied = sem("x_dbl_copied")
        x_dbl_stored = sem("x_dbl_stored")
        scan_act = sem("scan_act")
        softplus_step = sem("softplus_step")
        a_ready = sem("a_ready")
        bc_loaded = [sem(f"bc_loaded{j}") for j in range(2)]
        a_picked = sem("a_picked")
        decay_ready = sem("decay_ready")
        drive_ready = sem("drive_ready")
        scanned = sem("scanned")
        read_out = sem("read_out")
        y_added = sem("y_added")
        ln_moments = sem("ln_moments")
        ln_scale = sem("ln_scale")
        normed = sem("normed")
        x_turned = sem("x_turned")
        xT_copied = sem("xT_copied")
        y_gated = sem("y_gated")
        y_turned = sem("y_turned")
        y_residual = sem("y_residual")
        moe_consts = sem("moe_consts")
        route_mm = sem("route_mm")
        route_vec = sem("route_vec")
        scores_exp = sem("scores_exp")
        expert_known = sem("expert_known")
        hot_ready = sem("hot_ready")
        hot_used = sem("hot_used")
        tok_known = sem("tok_known")
        tok_picked = sem("tok_picked")
        gather_due = sem("gather_due")
        x_stored = sem("x_stored")
        gathered = [sem(f"gathered{j}") for j in range(NJ)]
        w_loaded = [sem(f"w_loaded{j}") for j in range(NJ)]
        y_stored = [sem(f"y_stored{j}") for j in range(NJ)]
        xg_turned = sem("xg_turned")
        xgT_copied = sem("xgT_copied")
        gv_ready = sem("gv_ready")
        g_tanh = sem("g_tanh")
        g_silu = sem("g_silu")
        hid_ready = sem("hid_ready")
        hid_turned = sem("hid_turned")
        hidT_copied = sem("hidT_copied")
        down_ready = sem("down_ready")
        down_copied = sem("down_copied")
        combined = sem("combined")
        lq_ready = sem("lq_ready")
        elu_split = sem("elu_split")
        elu_exp = sem("elu_exp")
        elu_done = sem("elu_done")
        lkv_ready = sem("lkv_ready")
        lkv_added = sem("lkv_added")
        kv_ready = sem("kv_ready")
        kv_masked = sem("kv_masked")
        num_ready = sem("num_ready")
        att_ready = sem("att_ready")
        proj_out_ready = sem("proj_out_ready")
        bias_added = sem("bias_added")
        attended = sem("attended")
        layer_loaded = sem("layer_loaded")
        angle = sem("angle")
        cos_sin_ready = sem("cos_sin_ready")
        xkv_ready = sem("xkv_ready")
        xv_copied = sem("xv_copied")
        turns_done = sem("turns_done")
        rotated = sem("rotated")
        xq_ready = sem("xq_ready")
        part_cast = sem("part_cast")
        part_rest = sem("part_rest")
        stacked = sem("stacked")
        heads_turned = sem("heads_turned")
        qsT_copied = sem("qsT_copied")
        ksT_copied = sem("ksT_copied")
        v_picked = sem("v_picked")
        rows_ready = sem("rows_ready")
        rows_maxed = sem("rows_maxed")
        shift_step = sem("shift_step")
        shift_ready = sem("shift_ready")
        shift_turned = sem("shift_turned")
        shiftT_copied = sem("shiftT_copied")
        cols_ready = sem("cols_ready")
        prob_ready = sem("prob_ready")
        pv_ready = sem("pv_ready")
        den_inv = sem("den_inv")
        head_out = sem("head_out")
        f_summed = sem("f_summed")
        f_total = sem("f_total")
        ternary = sem("ternary")
        h_ready = sem("h_ready")
        h_relu = sem("h_relu")
        h_square = sem("h_square")
        hq_ready = sem("hq_ready")
        hq_turned = sem("hq_turned")
        hqT_copied = sem("hqT_copied")
        f_out_ready = sem("f_out_ready")
        f_added = sem("f_added")

        back = [(s, 16 * NBLK // NJ) for s in gathered] + [(sem(f"back{j}"), 0) for j in range(4)]

        block = ctx.enter_context(nc.Block())

        def bank(n, a=0, b=512):
            return ps[:, n, a:b]

        def pair(n):
            return ps[:, n:n + 2, :].rearrange("p a b -> p (a b)")

        @block.sync
        def _(sp):
            sp.dma_start(xT[:], a["xT"]).then_inc(x_loaded, 16)
            sp.dma_start(w_qks[:], a["wqks"][0]).then_inc(qks_loaded, 16)
            sp.dma_start(ident[:], a["ident"]).then_inc(const_loaded, 16)
            sp.dma_start(w_vg[:], a["wvg"][0]).then_inc(vg_loaded, 16)
            sp.wait_ge(const_loaded, 16)
            sp.dma_start(tri[:], a["tri"]).then_inc(const_loaded, 16)
            sp.wait_ge(const_loaded, 32)
            sp.dma_start(gn_half[:], a["gnorm"]).then_inc(const_loaded, 16)
            sp.dma_start(w_o[:], a["wo"][0]).then_inc(wo_loaded, 16)
            sp.wait_ge(x_loaded, 16)
            sp.dma_start(xres[:], a["x_tok"]).then_inc(x_loaded, 16)
            for dst, src in ((ctxT, "ctxT"), (w_in, "w_in"), (xp_w, "xp_w"), (dt_w, "dt_w"), (s_cols, "s_cols"),
                             (a_neg, "a_log")):
                sp.dma_start(dst[:], a[src]).then_inc(scan_consts, 16)
            sp.wait_ge(proj_ready, 6)
            sp.dma_start(w_qks[:], a["wqks"][1]).then_inc(qks_loaded, 16)
            sp.wait_ge(x_dbl_copied, 2)
            sp.dma_start(x_dbl_dram, x_dbl[:]).then_inc(x_dbl_stored, 16)
            sp.wait_ge(x_dbl_stored, 16)

            def scan_rows(i, j):
                row = DR + 2 * i + j
                for dst, r in ((b_row, row), (c_row, row + DS)):
                    src = x_dbl_dram[bass.ds(r, 1), :].to_broadcast([P, TOK])
                    sp.dma_start(dst[:, j, :], src).then_inc(bc_loaded[j], 16)

            for j in range(2):
                scan_rows(0, j)

            def loads(i, last):
                sp.wait_ge(proj_ready, at(i, 14, 14))
                sp.dma_start(w_vg[:], a["wvg"][bass.ds(i + 1, 1)].rearrange("a p k n -> (a p) k n")).then_inc(vg_loaded, 16)
                if not last:
                    sp.wait_ge(proj_ready, at(i, 14, 20))
                    sp.dma_start(w_qks[:], a["wqks"][bass.ds(i + 2, 1)].rearrange("a p k n -> (a p) k n")).then_inc(qks_loaded, 16)
                sp.wait_ge(mixed_ready, at(i, 4, 4))
                sp.dma_start(w_o[:], a["wo"][bass.ds(i + 1, 1)].rearrange("a p k n -> (a p) k n")).then_inc(wo_loaded, 16)
                for j in range(2):
                    sp.wait_ge(read_out, at(i, 4, 2 * j + 2))
                    scan_rows(i + 1, j)

            with sp.Fori(0, PAIRS - 2) as i:
                loads(i, False)
            loads(PAIRS - 2, True)
            sp.wait_ge(y_turned, 4)
            for dst, src in ((w_router, "w_router"), (iota, "iota"), (tok_id, "tok_id"), (tri_bf, "tri_bf")):
                sp.dma_start(dst[:], a[src]).then_inc(moe_consts, 16)
            sp.dma_start(sh_gv[:], a["sh_gv"]).then_inc(layer_loaded, 16)
            sp.dma_start(sh_dn[:], a["sh_dn"]).then_inc(layer_loaded, 16)
            sp.wait_ge(normed, 16)
            sp.dma_start(x_dram.rearrange("(t p) d -> p t d", p=P), xres[:]).then_inc(x_stored, 16)
            sp.wait_ge(expert_known, 1)
            for j in range(NJ):
                sp.sem_inc(y_stored[j], 16)

            def store_y(i, j):
                sp.wait_ge(down_copied, at(i, NJ, j + 1) + TILES)
                rows = y_dram[bass.ds((i * NJ + j) * P, P), :]
                sp.dma_start(rows, y_out[:, j, :]).then_inc(y_stored[j], 16)

            def load_w(i, j):
                e = sp.value_load(expert_row[0:1, bass.ds(i * NJ + j, 1)], min_val=0, max_val=E - 1)
                sp.dma_start(w_gv[:, j], a["w_gv"][bass.ds(e, 1)].rearrange("a p k n -> (a p) k n")).then_inc(w_loaded[j], 16)
                sp.dma_start(w_dn[:, j], a["w_dn"][bass.ds(e, 1)].rearrange("a p k n -> (a p) k n")).then_inc(w_loaded[j], 16)

            for j in range(NJ):
                load_w(0, j)
            with sp.Fori(1, NBLK // NJ) as i:
                for j in range(NJ):
                    store_y(i - 1, j)
                    load_w(i, j)
            for j in range(NJ):
                store_y(NBLK // NJ - 1, j)
            sp.wait_ge(normed, 24)
            for dst, src in ((l_wq, "l_wq"), (l_wkv, "l_wkv"), (l_wo, "l_wo"), (l_bq, "l_bq"), (head_mask, "head_mask")):
                sp.dma_start(dst[:], a[src]).then_inc(layer_loaded, 16)
            sp.dma_start(l_bkv[:], a["l_bkv"].to_broadcast([P, 2 * D])).then_inc(layer_loaded, 16)
            sp.dma_start(l_bo[:], a["l_bo"].to_broadcast([P, D])).then_inc(layer_loaded, 16)
            sp.wait_ge(normed, 32)
            for dst, src in ((x_wkv, "x_wkv"), (pos, "pos"), (x_wq, "x_wq"), (ident_bf, "ident_bf"),
                             (shift_sel, "shift_sel"), (x_wo, "x_wo"), (f_in, "f_in"), (f_out, "f_out")):
                sp.dma_start(dst[:], a[src]).then_inc(layer_loaded, 16)
            sp.dma_start(x_bo[:], a["x_bo"].to_broadcast([P, D])).then_inc(layer_loaded, 16)
            sp.wait_ge(normed, 48)
            sp.dma_start(out.rearrange("b (t p) d -> p (b t) d", p=P), xres[:]).then_inc(stored, 16)
            sp.wait_ge(stored, 16)

        @block.tensor
        def _(pe):
            mm = nc.tensor.matmul

            def project_qks(i, first):
                pe.wait_ge(qks_loaded, at(i, 16, 16))
                for n in range(6):
                    part, half = n // 2, n % 2
                    if n < 2:
                        if not first:
                            pe.wait_ge(gate_ready, at(i - 1, 8, 7 + n))
                    elif n < 4:
                        pe.wait_ge(qk_copied, at(i, 4, n - 1))
                    else:
                        pe.wait_ge(qk_copied, at(i, 4, n - 1))
                    for k in range(KD):
                        last = mm(bank(PJ + n % 2), w_qks[:, k, part * P:(part + 1) * P],
                                  xT[:, k, half * 512:(half + 1) * 512], start=(k == 0), stop=(k == KD - 1))
                    last.then_inc(proj_ready, 1)

            def step(i, last_pair):
                pe.wait_ge(qk_copied, at(i, 4, 4))
                for n in range(8):
                    b, h = n // 2, n % 2
                    if n >= 2:
                        pe.wait_ge(scores_masked, at(i, 8, n - 1))
                    r = slice(64 * h, 64 * h + 64)
                    c = b * T
                    mm(ps[:, AB + n % 2, 0:256], kT[r, c:c + P], qT[r, c:c + 256], start=True, stop=True)
                    mm(ps[:, AB + n % 2, 256:384], kT[r, c + P:c + 256], qT[r, c + P:c + 256],
                       start=True, stop=True).then_inc(scores_ready, 1)
                pe.wait_ge(eT_ready, at(i, 2, 2))
                pe.wait_ge(const_loaded, 48)
                pe.wait_ge(mixed_added, at(i, 4, 1))
                for n in range(2):
                    for t in range(4):
                        c = (4 * n + t) * P
                        last = nc.tensor.transpose(ps[:, X + n, t * P:(t + 1) * P], eT[:, c:c + P], ident[:])
                    last.then_inc(e_turned, 1)
                pe.wait_ge(e_copied, at(i, 2, 2))
                pe.wait_ge(scores_masked, at(i, 8, 8))
                for b in range(B):
                    for h in range(2):
                        n = 2 * b + h
                        m = slice(M * h, M * h + M)
                        o0 = ps[:, X + b // 2, (b % 2) * 256 + M * h:(b % 2) * 256 + M * h + M]
                        o1 = ps[:, X + b // 2, (b % 2) * 256 + P + M * h:(b % 2) * 256 + P + M * h + M]
                        mm(o0, aT[:, n, 0:P], e_tok[:, 2 * b, m], start=True, stop=True)
                        mm(o1, aT[:, n, P:256], e_tok[:, 2 * b, m], start=True, stop=False)
                        last = mm(o1, aT[:, n, 256:384], e_tok[:, 2 * b + 1, m], start=False, stop=True)
                last.then_inc(slots_ready, 1)
                pe.wait_ge(lnz_ready, at(i, 1, 1))
                for n in range(2):
                    for t in range(4):
                        c = (4 * n + t) * P
                        last = nc.tensor.transpose(ps[:, Y + n, t * P:(t + 1) * P], zT[:, c:c + P], ident[:])
                    last.then_inc(z_turned, 1)
                pe.wait_ge(vg_loaded, at(i, 16, 16))
                for t in range(TILES):
                    if t < 2:
                        pe.wait_ge(s_clipped, at(i, 2, t + 1))
                    else:
                        pe.wait_ge(gate_ready, at(i, 8, t - 1))
                    for k in range(KD):
                        last = mm(bank(PJ + t % 2), xT[:, k, t * P:(t + 1) * P], w_vg[:, k, :],
                                  start=(k == 0), stop=(k == KD - 1))
                    last.then_inc(proj_ready, 1)
                pe.wait_ge(w_ready, at(i, 1, 1))
                pe.wait_ge(zi_ready, at(i, 2, 2))
                for n in range(2):
                    for t in range(4):
                        r = 4 * n + t
                        last = nc.tensor.transpose(ps[:, Y + n, t * P:(t + 1) * P],
                                                   okn[:, 2 * r:2 * r + 2, :].rearrange("p a b -> p (a b)"), ident[:])
                    last.then_inc(w_turned, 1)
                def read(n):
                    b, h = n // 2, n % 2
                    if n >= 2:
                        pe.wait_ge(read_masked, at(i, 8, n - 1))
                    r = slice(64 * h, 64 * h + 64)
                    c = b * T
                    mm(ps[:, AB + n % 2, 0:256], eT[r, c:c + P], wT[r, c:c + 256], start=True, stop=True)
                    mm(ps[:, AB + n % 2, 256:384], eT[r, c + P:c + 256], wT[r, c + P:c + 256],
                       start=True, stop=True).then_inc(read_ready, 1)

                def mix(n):
                    b, h = n // 2, n % 2
                    pe.wait_ge(read_masked, at(i, 8, n + 1))
                    vh = slice(DV * h, DV * h + DV)
                    o0 = ps[:, X + b, DV * h:DV * h + DV]
                    o1 = ps[:, X + b, 256 + DV * h:256 + DV * h + DV]
                    mm(o0, aT[:, n, 0:P], v[:, 2 * b, vh], start=True, stop=True)
                    mm(o1, aT[:, n, P:256], v[:, 2 * b, vh], start=True, stop=False)
                    last = mm(o1, aT[:, n, 256:384], v[:, 2 * b + 1, vh], start=False, stop=True)
                    if h == 1:
                        last.then_inc(o_ready, 1)

                pe.wait_ge(wT_copied, at(i, 2, 2))
                read(0)
                for n in range(8):
                    if n < 7:
                        read(n + 1)
                    mix(n)
                if not last_pair:
                    project_qks(i + 1, False)
                pe.wait_ge(wo_loaded, at(i, 16, 16))

                def turn(b):
                    pe.wait_ge(o_gated, at(i, 4, b + 1))
                    if b >= 2:
                        pe.wait_ge(oT_copied, at(i, 4, b - 1))
                    for h in range(2):
                        for t in range(2):
                            last = nc.tensor.transpose(ps[:, AB + b % 2, (2 * h + t) * P:(2 * h + t + 1) * P],
                                                       on[:, 2 * (2 * b + t) + h, :], ident[:])
                    last.then_inc(o_turned, 1)

                def project_out(b):
                    pe.wait_ge(oT_copied, at(i, 4, b + 1))
                    if b >= 2:
                        pe.wait_ge(mixed_added, at(i, 4, b))
                    for t in range(2):
                        for h in range(2):
                            c = (2 * b + t) * P
                            last = mm(ps[:, X + b % 2, 256 * t:256 * t + 256], oT[:, h, c:c + P], w_o[:, h, :],
                                      start=(h == 0), stop=(h == 1))
                    last.then_inc(mixed_ready, 1)

                turn(0)
                for b in range(B):
                    if b < 3:
                        turn(b + 1)
                    project_out(b)

            pe.wait_ge(x_loaded, 16)
            project_qks(0, True)
            pe.wait_ge(scan_consts, 96)
            for e in range(ET):
                for half in range(2):
                    mm(bank(X + 2 * e + half), w_in[:, e * P:(e + 1) * P], ctxT[:, half * 512:(half + 1) * 512],
                       start=True, stop=True).then_inc(scan_mm, 1)
            pe.wait_ge(u_ready, 2)
            for half in range(2):
                for e in range(ET):
                    last = mm(ps[0:XD, X + half, :], xp_w[:, e, :], u[:, e, half * 512:(half + 1) * 512],
                              start=(e == 0), stop=(e == ET - 1))
                last.then_inc(scan_mm, 1)
            pe.wait_ge(x_dbl_copied, 2)
            for e in range(ET):
                for half in range(2):
                    mm(bank(X + 2 * e + half), dt_w[:, e * P:(e + 1) * P], x_dbl[0:DR, half * 512:(half + 1) * 512],
                       start=True, stop=True).then_inc(scan_mm, 1)
            pe.wait_ge(scan_act, 10)
            with pe.Fori(0, PAIRS - 1) as i:
                step(i, False)
            step(PAIRS - 1, True)

            def turn_x(n):
                for b in range(B):
                    pe.wait_ge(normed, 8 * n + 2 * b + 2)
                    for k in range(KD):
                        for t in range(2):
                            last = nc.tensor.transpose(ps[:, b, k * 256 + t * P:k * 256 + (t + 1) * P],
                                                       xres[:, 2 * b + t, k * P:(k + 1) * P], ident[:])
                    last.then_inc(x_turned, 1)

            for b in range(B):
                pe.wait_ge(y_gated, b + 1)
                for t in range(2):
                    for e in range(ET):
                        last = nc.tensor.transpose(ps[:, X + b, t * 256 + e * P:t * 256 + (e + 1) * P],
                                                   v[:, 2 * b + e, t * P:(t + 1) * P], ident[:])
                last.then_inc(y_turned, 1)
            turn_x(1)
            pe.wait_ge(moe_consts, 64)
            for t in range(TILES):
                if t % 2 == 0:
                    pe.wait_ge(xT_copied, t // 2 + 1)
                if t == 0:
                    pe.wait_ge(y_residual, 1)
                for k in range(KD):
                    last = mm(ps[:, X, t * E:(t + 1) * E], xT[:, k, t * P:(t + 1) * P], w_router[:, k, :],
                              start=(k == 0), stop=(k == KD - 1))
            last.then_inc(route_mm, 1)
            pe.wait_ge(route_vec, 2)
            pe.wait_ge(pool_set, 2)
            for t in range(TILES):
                for q in range(t + 1):
                    last = mm(ps[:, X + 1, t * E:(t + 1) * E], ones_bf[:] if q < t else tri_bf[:], chosen_bf[:, q, :],
                              start=(q == 0), stop=(q == t))
            for t in range(TILES):
                last = mm(ps[:, Y, 0:E], ones_bf[:], chosen_bf[:, t, :], start=(t == 0), stop=(t == TILES - 1))
            last.then_inc(route_mm, 1)
            pe.wait_ge(route_vec, 3)
            nc.tensor.transpose(ps[0:1, Y, 0:P], blk_expert[:], ident[:]).then_inc(route_mm, 1)
            for n in range(TILES * TOPK):
                pe.wait_ge(hot_ready, 2 * n + 2)
                mm(ps[:, Y + 1, 0:NBLK], row_hot[:, n % 4, :], blk_hot[:, n % 4, :], start=(n == 0),
                   stop=(n == TILES * TOPK - 1)).then_inc(hot_used, 1)

            def gate_up(n, j, x_of, w):
                for k in range(KD):
                    last = mm(ps[:, 2 * j + 1, 0:2 * F], x_of(k), w[:, k, :], start=(k == 0), stop=(k == KD - 1))
                last.then_inc(gv_ready, 1)

            def turn_hid(n, j):
                pe.wait_ge(hid_ready, n + 1)
                for f in range(2):
                    last = nc.tensor.transpose(ps[0:FH, 2 * j, f * P:(f + 1) * P], hid[:, j, f * FH:(f + 1) * FH], ident[:])
                last.then_inc(hid_turned, 1)

            def down(n, j, w):
                pe.wait_ge(hidT_copied, n + 1)
                for f in range(2):
                    last = mm(ps[:, 2 * j, 256:512], hidT[:, j, f * P:(f + 1) * P], w[:, f, :], start=(f == 0),
                              stop=(f == 1))
                last.then_inc(down_ready, 1)

            pe.wait_ge(layer_loaded, 32)
            pe.wait_ge(tok_known, 1)
            for r in range(TILES // NJ):
                for j in range(NJ):
                    n = r * NJ + j
                    if r:
                        pe.wait_ge(down_copied, n - NJ + 1)
                    gate_up(n, j, lambda k: xT[:, k, n * P:(n + 1) * P], sh_gv)
                for j in range(NJ):
                    turn_hid(r * NJ + j, j)
                for j in range(NJ):
                    down(r * NJ + j, j, sh_dn)
            with pe.Fori(0, NBLK // NJ) as i:
                for j in range(NJ):
                    n = i * NJ + j
                    pe.wait_ge(gathered[j], at(i, 16, 16))
                    pe.wait_ge(down_copied, n + TILES - NJ + 1)
                    for k in range(KD):
                        last = nc.tensor.transpose(ps[:, 2 * j, k * P:(k + 1) * P], xg[:, j, k * P:(k + 1) * P], ident[:])
                    last.then_inc(xg_turned, 1)
                for j in range(NJ):
                    n = i * NJ + j
                    pe.wait_ge(xgT_copied, n + 1)
                    pe.wait_ge(w_loaded[j], at(i, 32, 32))
                    gate_up(n + TILES, j, lambda k: xgT[:, j, k * P:(k + 1) * P], w_gv[:, j])
                for j in range(NJ):
                    turn_hid(i * NJ + j + TILES, j)
                for j in range(NJ):
                    down(i * NJ + j + TILES, j, w_dn[:, j])

            def copy_x_wait(n):
                pe.wait_ge(xT_copied, 4 * TURN[f"x{n}"] + 4)

            turn_x(2)
            copy_x_wait(2)
            pe.wait_ge(layer_loaded, 144)
            for n in range(4):
                m, half = n // 2, n % 2
                for k in range(KD):
                    last = mm(bank(4 + n), l_wq[:, k, m * P:(m + 1) * P], xT[:, k, half * 512:(half + 1) * 512],
                              start=(k == 0), stop=(k == KD - 1))
                last.then_inc(lq_ready, 1)
            for t in range(TILES):
                if t >= 4:
                    pe.wait_ge(lkv_added, 2 * (t - 3))
                for k in range(KD):
                    last = mm(bank(t % 4), xT[:, k, t * P:(t + 1) * P], l_wkv[:, k, :], start=(k == 0), stop=(k == KD - 1))
                last.then_inc(lkv_ready, 1)
            pe.wait_ge(elu_split, 8)
            for n in range(B * KD):
                b, m = n // KD, n % KD
                pe.wait_ge(elu_done, 4 + 2 * b + 2)
                if n >= 4:
                    pe.wait_ge(kv_masked, n - 3)
                c = slice(m * P, (m + 1) * P)
                for t in range(2):
                    mm(ps[:, 4 + n % 4, 0:P], lk[:, 2 * b + t, c], lv[:, 2 * b + t, c], start=(t == 0), stop=(t == 1))
                for t in range(2):
                    last = mm(ps[:, 4 + n % 4, P:KVW], lk[:, 2 * b + t, c], ones[:, 0:LB], start=(t == 0), stop=(t == 1))
                last.then_inc(kv_ready, 1)
            pe.wait_ge(elu_done, 4)
            for t in range(TILES):
                b = t // 2
                pe.wait_ge(kv_masked, KD * (b + 1))
                if t < 4:
                    pe.wait_ge(lkv_added, 2 * TILES)
                else:
                    pe.wait_ge(att_ready, t - 3)
                for m in range(KD):
                    last = mm(ps[:, t % 4, m * KVW:(m + 1) * KVW], lqT[:, m, t * P:(t + 1) * P], kv[:, KD * b + m, :],
                              start=True, stop=True)
                last.then_inc(num_ready, 1)

            def turn_att(src):
                for b in range(B):
                    if src is l_out:
                        pe.wait_ge(att_ready, 2 * b + 2)
                    for k in range(KD):
                        for t in range(2):
                            last = nc.tensor.transpose(ps[:, 4 + b, k * 256 + t * P:k * 256 + (t + 1) * P],
                                                       src[:, 2 * b + t, k * P:(k + 1) * P], ident[:])
                    last.then_inc(x_turned, 1)

            def project_att(n, w):
                for t in range(TILES):
                    pe.wait_ge(xT_copied, 4 * TURN[f"att{n}"] + t // 2 + 1)
                    if t >= 4:
                        pe.wait_ge(attended, 8 * n + t - 3)
                    for k in range(KD):
                        last = mm(ps[:, t % 4, 0:D], xT[:, k, t * P:(t + 1) * P], w[:, k, :], start=(k == 0),
                                  stop=(k == KD - 1))
                    last.then_inc(proj_out_ready, 1)

            pe.wait_ge(kv_masked, B * KD)
            turn_att(l_out)
            project_att(0, l_wo)

            pe.wait_ge(layer_loaded, 288)
            pe.wait_ge(attended, 8)
            for t in range(TILES):
                if t >= 4:
                    pe.wait_ge(turns_done, 4 * (t - 3))
                mm(bank(t % 4), ctxT[:, t * P:(t + 1) * P], x_wkv[:], start=True, stop=True).then_inc(xkv_ready, 1)
            pe.wait_ge(turns_done, 4 * TILES)
            turn_x(3)
            copy_x_wait(3)
            for b in range(B):
                for t in range(2):
                    for k in range(KD):
                        c = (2 * b + t) * P
                        last = mm(ps[:, 4 + b, t * 256:(t + 1) * 256], xT[:, k, c:c + P], x_wq[:, k, :], start=(k == 0),
                                  stop=(k == KD - 1))
                last.then_inc(xq_ready, 1)
            pe.wait_ge(stacked, 12)
            pe.wait_ge(pool_set, 6)
            pe.wait_ge(turns_done, 48)
            with pe.Fori(0, XPAIRS) as i:
                pe.wait_ge(head_out, at(i, 1, 1))
                for n, src in enumerate((q_st, k_st)):
                    for t in range(TILES):
                        last = mm(ps[:, 2 * n + t // 4, t % 4 * P:(t % 4 + 1) * P],
                                  src[:, t, bass.ds(2 * i, 2), :].rearrange("p a b -> p (a b)"), ident_bf[:],
                                  start=True, stop=True)
                        if t % 4 == 3:
                            last.then_inc(heads_turned, 1)
                pe.wait_ge(qsT_copied, at(i, 2, 2))
                pe.wait_ge(ksT_copied, at(i, 2, 2))
                for b in range(B):
                    if b >= 2:
                        pe.wait_ge(rows_maxed, at(i, 4, b - 1))
                    for h in range(2):
                        r = slice(SLOT * h, SLOT * h + SLOT)
                        for q in range(2):
                            c = b * T + q * P
                            last = mm(ps[:, 4 + 2 * (b % 2) + h, q * 256:(q + 1) * 256], qsT[r, c:c + P],
                                      ksT[r, b * T:(b + 1) * T], start=True, stop=True)
                    last.then_inc(rows_ready, 1)
                pe.wait_ge(shift_ready, at(i, 1, 1))
                mm(ps[:, 0, 0:P], shift[:].rearrange("p a b -> p (a b)"), ident_bf[:], start=True,
                   stop=True).then_inc(shift_turned, 1)
                pe.wait_ge(shiftT_copied, at(i, 1, 1))
                pe.wait_ge(v_picked, at(i, 1, 1))

                def columns(b):
                    if b >= 2:
                        pe.wait_ge(prob_ready, at(i, 4, b - 1))
                    for h in range(2):
                        r = slice(SLOT * h, SLOT * h + SLOT)
                        for k in range(2):
                            out = ps[:, 4 + 2 * (b % 2) + h, k * 256:(k + 1) * 256]
                            for q in range(2):
                                mm(out[:, q * P:(q + 1) * P], ksT[r, b * T + k * P:b * T + (k + 1) * P],
                                   qsT[r, b * T + q * P:b * T + (q + 1) * P], start=True, stop=False)
                                last = mm(out[:, q * P:(q + 1) * P], shift_sel[r, 2 * b + q, :], shiftT[r, :],
                                          start=False, stop=True)
                    last.then_inc(cols_ready, 1)

                def values(b):
                    pe.wait_ge(prob_ready, at(i, 4, b + 1))
                    for h in range(2):
                        for q in range(2):
                            c = ((2 * b + q) * 2 + h) * VA
                            for k in range(2):
                                last = mm(ps[:, 1, c:c + VA], probT[:, 2 * (b % 2) + h, k, q * P:(q + 1) * P],
                                          va_cur[:, 2 * b + k, h, :], start=(k == 0), stop=(k == 1))
                    if b == B - 1:
                        last.then_inc(pv_ready, 1)

                pe.wait_ge(rows_maxed, at(i, 4, 4))
                columns(0)
                for b in range(B):
                    if b < B - 1:
                        columns(b + 1)
                    values(b)
            pe.wait_ge(head_out, XPAIRS + 1)
            turn_att(x_att)
            project_att(1, x_wo)

            pe.wait_ge(f_summed, 2)
            mm(ps[:, 7, 0:2], ones[:, 0:P], f_sum[:], start=True, stop=True).then_inc(f_total, 1)
            turn_x(4)
            pe.wait_ge(ternary, 2)
            pe.wait_ge(part_cast, 9)

            def up(t):
                if t >= 2:
                    pe.wait_ge(h_relu, t - 1)
                for n in range(2):
                    for j in range(3):
                        for k in range(KD):
                            last = mm(bank(2 * (t % 2) + n), x_part[:, j, k, t * P:(t + 1) * P],
                                      q_in[:, k, n * 512:(n + 1) * 512], start=(j == 0 and k == 0),
                                      stop=(j == 2 and k == KD - 1))
                last.then_inc(h_ready, 1)

            def turn_h(t):
                pe.wait_ge(hq_ready, t + 1)
                if t >= 2:
                    pe.wait_ge(hqT_copied, t - 1)
                for k in range(KH):
                    last = nc.tensor.transpose(ps[:, 4 + t % 2, :].bitcast(BF16)[:, k * P:(k + 1) * P],
                                               hid_q[:, t % 2, k * P:(k + 1) * P], ident_bf[:])
                last.then_inc(hq_turned, 1)

            def down_f(t):
                pe.wait_ge(hqT_copied, t + 1)
                if t >= 2:
                    pe.wait_ge(f_added, t - 1)
                for k in range(KH):
                    last = mm(ps[:, 6 + t % 2, 0:D], hid_q[:, 2 + t % 2, k * P:(k + 1) * P], q_out[:, k, :],
                              start=(k == 0), stop=(k == KH - 1))
                last.then_inc(f_out_ready, 1)

            up(0)
            for t in range(TILES):
                if t < TILES - 1:
                    up(t + 1)
                turn_h(t)
                down_f(t)

        @block.gpsimd
        def _(pool):
            nc.gpsimd.memset(x_pad[:, :, :, 0:DC - 1], 0.0).then_inc(pool_set, 1)
            G = nc.gpsimd
            pool.sem_inc(y_added, 2)
            pool.wait_ge(u_ready, 4)

            def steps(i):
                def drive_of(n):
                    j, e = n // 2, n % 2
                    pool.wait_ge(bc_loaded[j], at(i, 32, 32))
                    pool.wait_ge(scanned, at(i, 4, n + 1))
                    G.tensor_tensor(drive[:, n % 2], du[:, e], b_row[:, j], ALU.mult).then_inc(drive_ready, 1)

                def read_of(n):
                    j, e = n // 2, n % 2
                    pool.wait_ge(scanned, at(i, 4, n + 3))
                    G.tensor_tensor(state[:, n % 2], state[:, n % 2], c_row[:, j], ALU.mult).then_inc(read_out, 1)
                    pool.wait_ge(read_out, at(i, 4, n + 1))
                    pool.wait_ge(y_added, at(i, 4, n + 1))
                    G.tensor_tensor(y[:, e], y[:, e], state[:, n % 2], ALU.add).then_inc(y_added, 1)

                drive_of(0)
                drive_of(1)
                read_of(0)
                drive_of(2)
                read_of(1)
                drive_of(3)
                read_of(2)
                read_of(3)

            steps(0)
            with pool.Fori(1, PAIRS) as i:
                steps(i)
            pool.wait_ge(y_turned, 4)
            G.memset(ones_bf[:], 1.0).then_inc(pool_set, 1)
            pool.wait_ge(tok_known, 1)
            pool.wait_ge(x_stored, 16)

            def gather(i, j, first):
                if not first:
                    pool.wait_ge(xg_turned, at(i - 1, NJ, j + 1))
                    pool.wait_ge(gathered[j], at(i, 16, 0))
                G.tensor_copy(tok_cur[:, j:j + 1], tok_of[:, bass.ds(i * NJ + j, 1)]).then_inc(tok_picked, 1)
                pool.wait_ge(tok_picked, at(i, NJ, j + 1))
                pool.sem_inc(gather_due, 1)
                G.indirect_dma_start(xg[:, j, :], None, x_dram, bass.IndirectOffsetOnAxis(ap=tok_cur[:, j:j + 1], axis=0)
                                     ).then_inc(gathered[j], 16)

            for j in range(NJ):
                gather(0, j, True)
            with pool.Fori(1, NBLK // NJ) as i:
                for j in range(NJ):
                    gather(i, j, False)
            for j in range(NJ):
                pool.wait_ge(y_stored[j], NBLK // NJ * 16 + 16)
            for n in range(TILES * TOPK):
                if n >= 8:
                    pool.wait_ge(combined, n - 7)
                G.indirect_dma_start(yg[:, n % 8, :], None, y_dram,
                                     bass.IndirectOffsetOnAxis(ap=slot_idx[:, n // TOPK, n % TOPK:n % TOPK + 1], axis=0)
                                     ).then_inc(back[n % 8][0], 16)
            pool.wait_ge(normed, 32)
            G.memset(q_st[:, :, :, 6 * XD_H:SLOT], 0.0).then_inc(pool_set, 1)
            G.memset(k_st[:, :, :, 6 * XD_H:SLOT], 0.0).then_inc(pool_set, 1)
            G.memset(v_aug[:, :, :, XD_H:VA], 1.0).then_inc(pool_set, 1)
            G.memset(shift[:, :, 3 * 8:SLOT], 0.0).then_inc(pool_set, 1)
            pool.wait_ge(xv_copied, TILES)
            pool.wait_ge(pool_set, 6)

            def pick_v(i):
                G.tensor_copy(va_cur[:], v_aug[:, :, bass.ds(2 * i, 2), :]).then_inc(v_picked, 1)

            pick_v(0)
            with pool.Fori(1, XPAIRS) as i:
                pool.wait_ge(pv_ready, i)
                pick_v(i)

        @block.scalar
        def _(act):
            def f(out, in_, func, **kw):
                return nc.scalar.activation(out, in_, func, **kw)

            act.wait_ge(const_loaded, 48)
            nc.scalar.mul(gn_half[:], gn_half[:], 0.5).then_inc(act_step, 1)

            def head(i, rms_of):
                for n in range(4):
                    act.wait_ge(proj_ready, at(i, 14, n + 1))
                    dst = (qT, kT)[n // 2]
                    f(dst[:, (n % 2) * 512:(n % 2) * 512 + 512], bank(PJ + n % 2), ACT.Copy).then_inc(qk_copied, 1)
                nc.scalar.preload_act_table_set("natural_log_exp_and_others")
                if rms_of is not None:
                    rms(rms_of)
                for n in range(2):
                    act.wait_ge(s_clipped, at(i, 2, n + 1))
                    f(eT[:, n * 512:(n + 1) * 512], sT[:, n * 512:(n + 1) * 512], ACT.Exp).then_inc(eT_ready, 1)
                act.wait_ge(zT_ready, at(i, 1, 1))
                f(zT[:], zT[:], ACT.Ln).then_inc(lnz_ready, 1)

            def rms(i):
                act.wait_ge(squares_read, at(i, 4, 4))
                f(lnv[:], ss[:], ACT.Ln, scale=1.0 / DV, bias=eps_col[:]).then_inc(act_step, 1)
                act.wait_ge(act_step, at(i, 1, 2))
                f(rstd[:], lnv[:], ACT.Exp, scale=-0.5).then_inc(rstd_ready, 1)

            def decay_of(i, n):
                j, e = n // 2, n % 2
                act.wait_ge(a_picked, at(i, 1, 1))
                act.wait_ge(scanned, at(i, 4, n + 1))
                f(decay[:, n % 2], delta[:, e], ACT.Exp, scale=a_cur[:, e, j:j + 1]).then_inc(decay_ready, 1)

            def step(i, last_pair):
                for n in range(2):
                    act.wait_ge(e_turned, at(i, 2, n + 1))
                    f(e_tok[:, 4 * n:4 * n + 4, :].rearrange("p a b -> p (a b)"), bank(X + n),
                      ACT.Copy).then_inc(e_copied, 1)
                for n in range(2):
                    act.wait_ge(z_turned, at(i, 2, n + 1))
                    f(zi[:, 4 * n:4 * n + 4, :].rearrange("p a b -> p (a b)"), bank(Y + n), ACT.Exp,
                      scale=-1.0).then_inc(zi_ready, 1)

                def values_and_gate(t):
                    act.wait_ge(proj_ready, at(i, 14, 7 + t))
                    f(v[:, t, :], bank(PJ + t % 2, 0, 256), ACT.Copy)
                    f(th[:, t, :], bank(PJ + t % 2, 256, 512), ACT.Tanh, scale=0.5).then_inc(tanh_ready, 1)

                decay_of(i, 0)
                for t in range(2):
                    values_and_gate(t)
                act.wait_ge(slots_shifted, at(i, 1, 1))
                f(pe_[:], okn[:], ACT.Exp, scale=DK ** -0.5).then_inc(slots_exp, 1)
                for t in range(2, 4):
                    values_and_gate(t)
                decay_of(i, 1)
                for t in range(4, TILES):
                    values_and_gate(t)
                decay_of(i, 2)
                for n in range(2):
                    act.wait_ge(w_turned, at(i, 2, n + 1))
                    f(wT[:, n * 512:(n + 1) * 512], bank(Y + n), ACT.Copy).then_inc(wT_copied, 1)
                for b in range(B):
                    act.wait_ge(o_ready, at(i, 4, b + 1))
                    if b >= 2:
                        act.wait_ge(squares_read, at(i, 4, b - 1))
                    f(sq[:, b % 2].rearrange("p a b -> p (a b)"), bank(X + b), ACT.Square).then_inc(squares_ready, 1)
                decay_of(i, 3)
                if last_pair:
                    nc.scalar.preload_act_table_set("natural_log_exp_and_others")
                    rms(i)
                else:
                    head(i + 1, i)
                for b in range(B):
                    act.wait_ge(o_turned, at(i, 4, b + 1))
                    f(oT[:, :, 2 * b * P:(2 * b + 2) * P], bank(AB + b % 2).rearrange("p (h t) -> p h t", h=2), ACT.Copy,
                      scale=gn_half[:]).then_inc(oT_copied, 1)

            act.wait_ge(act_step, 1)
            act.wait_ge(const_set, 2)
            head(0, None)
            act.wait_ge(scan_consts, 96)
            f(a_neg[:], a_neg[:], ACT.Exp).then_inc(a_ready, 1)
            act.wait_ge(a_ready, 1)
            nc.scalar.mul(a_neg[:], a_neg[:], -1.0).then_inc(a_ready, 1)
            for e in range(ET):
                for half in range(2):
                    act.wait_ge(scan_mm, 2 * e + half + 1)
                    f(x_pad[:, e, 2 * half:2 * half + 2, DC - 1:DC - 1 + T],
                      bank(X + 2 * e + half).rearrange("p (b t) -> p b t", b=2), ACT.Copy).then_inc(inner_copied, 1)
            for e in range(ET):
                act.wait_ge(conv_step, 4 * e + 4)
                f(aux[:, e], conv[:, e], ACT.Tanh, scale=0.5).then_inc(scan_act, 1)
            for half in range(2):
                act.wait_ge(scan_mm, 4 + half + 1)
                f(x_dbl[:, half * 512:(half + 1) * 512], ps[0:XD, X + half, :], ACT.Copy).then_inc(x_dbl_copied, 1)
            act.wait_ge(u_ready, 2)
            for e in range(ET):
                for half in range(2):
                    c = slice(half * 512, (half + 1) * 512)
                    act.wait_ge(scan_mm, 6 + 2 * e + half + 1)
                    f(delta[:, e, c], bank(X + 2 * e + half), ACT.Relu, bias=s_cols[:, e, DC + 1:DC + 2]).then_inc(scan_act, 1)
                    f(conv[:, e, c], bank(X + 2 * e + half), ACT.Abs, bias=s_cols[:, e, DC + 1:DC + 2]).then_inc(scan_act, 1)
            act.wait_ge(scan_act, 10)
            f(conv[:], conv[:], ACT.Exp, scale=-1.0).then_inc(scan_act, 1)
            nc.scalar.preload_act_table_set("natural_log_exp_and_others")
            act.wait_ge(softplus_step, 1)
            f(aux2[:], aux[:], ACT.Ln).then_inc(scan_act, 1)
            act.wait_ge(u_ready, 4)
            with act.Fori(0, PAIRS - 1) as i:
                step(i, False)
            step(PAIRS - 1, True)

            def norm_scale(n):
                nc.scalar.preload_act_table_set("natural_log_exp_and_others")
                act.wait_ge(ln_moments, n + 1)
                f(ln_var[:], moments[:, :, 1], ACT.Ln, bias=eps_col[:]).then_inc(ln_scale, 1)
                act.wait_ge(ln_scale, 2 * n + 1)
                f(ln_rstd[:], ln_var[:], ACT.Exp, scale=-0.5).then_inc(ln_scale, 1)

            def copy_xT(n):
                for b in range(B):
                    act.wait_ge(x_turned, 4 * TURN[f"x{n}"] + b + 1)
                    f(xT[:, :, b * 256:(b + 1) * 256], bank(b).rearrange("p (k t) -> p k t", k=KD),
                      ACT.Copy).then_inc(xT_copied, 1)

            norm_scale(0)
            act.wait_ge(normed, 8)
            f(th[:], xres[:], ACT.Tanh, scale=0.5).then_inc(tanh_ready, 1)
            norm_scale(1)
            copy_xT(1)
            act.wait_ge(route_vec, 1)
            f(score[:, :, 0:E], score[:, :, 0:E], ACT.Exp).then_inc(scores_exp, 1)
            act.wait_ge(route_mm, 3)
            f(expert_row[:], ps[0:1, Y, 0:P], ACT.Copy).then_inc(expert_known, 1)

            def g_tanh_of(n, j):
                act.wait_ge(gv_ready, n + 1)
                f(g_th[:, j, :], ps[:, 2 * j + 1, 0:F], ACT.Tanh, scale=0.5).then_inc(g_tanh, 1)

            def hidT_of(n, j):
                act.wait_ge(hid_turned, n + 1)
                f(hidT[:, j, :], ps[0:FH, 2 * j, 0:2 * P], ACT.Copy).then_inc(hidT_copied, 1)

            for r in range(TILES // NJ):
                for j in range(NJ):
                    g_tanh_of(r * NJ + j, j)
                for j in range(NJ):
                    hidT_of(r * NJ + j, j)
            with act.Fori(0, NBLK // NJ) as i:
                for j in range(NJ):
                    act.wait_ge(xg_turned, at(i, NJ, j + 1))
                    f(xgT[:, j, :], ps[:, 2 * j, 0:KD * P], ACT.Copy).then_inc(xgT_copied, 1)
                for j in range(NJ):
                    g_tanh_of(i * NJ + j + TILES, j)
                for j in range(NJ):
                    hidT_of(i * NJ + j + TILES, j)

            def hqT_of(t):
                act.wait_ge(hq_turned, t + 1)
                if t >= 2:
                    act.wait_ge(f_out_ready, t - 1)
                f(hid_q[:, 2 + t % 2], ps[:, 4 + t % 2, :].bitcast(BF16), ACT.Copy).then_inc(hqT_copied, 1)

            norm_scale(2)
            copy_xT(2)
            for n in range(4):
                act.wait_ge(elu_split, 2 * n + 2)
                f(lq_low[:, n % 2, :], lq_low[:, n % 2, :], ACT.Exp).then_inc(elu_exp, 1)
            for t in range(TILES):
                act.wait_ge(elu_split, 8 + t + 1)
                f(lk_low[:, t % 2, :], lk_low[:, t % 2, :], ACT.Exp).then_inc(elu_exp, 1)

            def copy_attT(n):
                for b in range(B):
                    act.wait_ge(x_turned, 4 * TURN[f"att{n}"] + b + 1)
                    f(xT[:, :, b * 256:(b + 1) * 256], bank(4 + b).rearrange("p (k t) -> p k t", k=KD),
                      ACT.Copy).then_inc(xT_copied, 1)

            copy_attT(0)
            norm_scale(3)
            act.wait_ge(angle, 6)
            f(cos_sin[:], ang[:], ACT.Sin).then_inc(cos_sin_ready, 1)
            for t in range(TILES):
                act.wait_ge(xkv_ready, t + 1)
                f(v_aug[:, t, :, 0:XD_H], bank(t % 4, 256, 512).rearrange("p (h d) -> p h d", h=XH),
                  ACT.Copy).then_inc(xv_copied, 1)
            copy_xT(3)

            def cast_parts(n, src, count):
                act.wait_ge(rotated, count)
                for j in range(3):
                    if j:
                        act.wait_ge(part_rest, 2 * n + j)
                    elif n:
                        act.wait_ge(stacked, 6)
                    f(part[:, j], src[:], ACT.Copy).then_inc(part_cast, 1)

            cast_parts(0, k_rot, 2 * TILES)
            cast_parts(1, q_rot, 2 * TILES + 2 * B)
            with act.Fori(0, XPAIRS) as i:
                for n in range(2):
                    act.wait_ge(heads_turned, at(i, 4, n + 1))
                    f(qsT[:, n * 512:(n + 1) * 512], bank(n), ACT.Copy).then_inc(qsT_copied, 1)
                act.wait_ge(shift_turned, at(i, 1, 1))
                f(shiftT[:], ps[:, 0, 0:P], ACT.Copy).then_inc(shiftT_copied, 1)
                for b in range(B):
                    act.wait_ge(cols_ready, at(i, 4, b + 1))
                    f(probT[:, 2 * (b % 2):2 * (b % 2) + 2].rearrange("p a k n -> p (a k n)"), pair(4 + 2 * (b % 2)),
                      ACT.Exp, scale=XD_H ** -0.5).then_inc(prob_ready, 1)
            copy_attT(1)
            norm_scale(4)
            copy_xT(4)
            act.wait_ge(xT_copied, 4 * TURN["x4"] + 4)
            for j in range(3):
                if j:
                    act.wait_ge(part_rest, 4 + j)
                f(x_part[:, j], xT[:], ACT.Copy).then_inc(part_cast, 1)
            for t in range(TILES):
                act.wait_ge(h_ready, t + 1)
                if t >= 2:
                    act.wait_ge(hq_ready, t - 1)
                for n in range(2):
                    last = f(hid_f[:, t % 2, n * 512:(n + 1) * 512], bank(2 * (t % 2) + n), ACT.Relu, scale=f_scale[:, 0:1])
                last.then_inc(h_relu, 1)
                act.wait_ge(h_relu, t + 1)
                f(hid_f[:, t % 2], hid_f[:, t % 2], ACT.Square).then_inc(h_square, 1)
                if t:
                    hqT_of(t - 1)
            hqT_of(TILES - 1)
            norm_scale(5)

        @block.vector
        def _(dve):
            V = nc.vector
            V.memset(ones[:], 1.0).then_inc(const_set, 1)
            V.memset(eps_col[:], LN_EPS).then_inc(const_set, 1)
            dve.wait_ge(const_set, 2)
            CHAIN = 5
            dve.sem_inc(scanned, 2)
            dve.sem_inc(mixed_added, 1)
            dve.sem_inc(head_out, 1)
            steps = [0]

            def then(ins):
                steps[0] += 1
                ins.then_inc(chain, 1)
                dve.wait_ge(chain, steps[0])

            def head(i):
                for n in range(2):
                    dve.wait_ge(proj_ready, at(i, 14, 5 + n))
                    V.tensor_scalar(sT[:, n * 512:(n + 1) * 512], bank(PJ + n % 2), CLAMP, -CLAMP,
                                    ALU.min, ALU.max).then_inc(s_clipped, 1)
                dve.wait_ge(eT_ready, at(i, 2, 2))
                for b in range(B):
                    last = V.tensor_tensor_scan(zT[:, b * T:(b + 1) * T], ones[:], eT[:, b * T:(b + 1) * T], 0.0,
                                                ALU.mult, ALU.add)
                last.then_inc(zT_ready, 1)

            def scan(i, n):
                j, e = n // 2, n % 2
                dve.wait_ge(decay_ready, at(i, 4, n + 1))
                dve.wait_ge(drive_ready, at(i, 4, n + 1))
                dve.wait_ge(y_added, at(i, 4, n + 1))
                for b in range(B):
                    c = slice(b * T, (b + 1) * T)
                    last = V.tensor_tensor_scan(state[:, n % 2, c], decay[:, n % 2, c], drive[:, n % 2, c], 0.0,
                                                ALU.mult, ALU.add)
                last.then_inc(scanned, 1)

            def step(i, last_pair):
                for n in range(8):
                    dve.wait_ge(scores_ready, at(i, 8, n + 1))
                    V.tensor_tensor(aT[:, n, :], ps[:, AB + n % 2, 0:384], tri[:], ALU.mult).then_inc(scores_masked, 1)
                dve.wait_ge(slots_ready, at(i, 1, 1))
                dve.wait_ge(zi_ready, at(i, 2, 2))
                okf = okn[:].rearrange("p a b -> p (a b)")
                zif = zi[:].rearrange("p a b -> p (a b)")
                V.tensor_tensor(okf, pair(X), zif, ALU.mult).then_inc(vec_step, 1)
                dve.wait_ge(vec_step, at(i, CHAIN, 1))
                V.tensor_reduce(okmax[:], okn[:], AX.X, ALU.max).then_inc(vec_step, 1)
                dve.wait_ge(vec_step, at(i, CHAIN, 2))
                V.tensor_tensor(okn[:], okn[:], okmax[:].unsqueeze(2).to_broadcast([P, TILES * 2, M]),
                                ALU.subtract).then_inc(slots_shifted, 1)

                def gate(t):
                    dve.wait_ge(tanh_ready, at(i, 8, t + 1))
                    V.scalar_tensor_tensor(out=th[:, t, :], in0=th[:, t, :], scalar=1.0,
                                           in1=bank(PJ + t % 2, 256, 512), op0=ALU.add,
                                           op1=ALU.mult).then_inc(gate_ready, 1)

                for t in range(3):
                    gate(t)
                dve.wait_ge(slots_exp, at(i, 1, 1))
                V.tensor_reduce(psum_[:], pe_[:], AX.X, ALU.add).then_inc(vec_step, 1)
                gate(3)
                dve.wait_ge(vec_step, at(i, CHAIN, 3))
                V.reciprocal(psum_[:], psum_[:]).then_inc(vec_step, 1)
                V.tensor_tensor(pe_[:].rearrange("p a b -> p (a b)"), pe_[:].rearrange("p a b -> p (a b)"), zif,
                                ALU.mult).then_inc(vec_step, 1)
                gate(4)
                dve.wait_ge(vec_step, at(i, CHAIN, 5))
                V.tensor_tensor(okn[:], pe_[:], psum_[:].unsqueeze(2).to_broadcast([P, TILES * 2, M]),
                                ALU.mult).then_inc(w_ready, 1)
                scan(i, 0)
                for t in range(5, TILES):
                    gate(t)
                scan(i, 1)
                for n in range(8):
                    dve.wait_ge(read_ready, at(i, 8, n + 1))
                    V.tensor_tensor(aT[:, n, :], ps[:, AB + n % 2, 0:384], tri[:], ALU.mult).then_inc(read_masked, 1)
                scan(i, 2)
                for b in range(B):
                    dve.wait_ge(squares_ready, at(i, 4, b + 1))
                    V.tensor_reduce(ss[:, 4 * b:4 * b + 4], sq[:, b % 2], AX.X, ALU.add).then_inc(squares_read, 1)
                dve.wait_ge(rstd_ready, at(i, 1, 1))
                for b in range(B):
                    r = slice(4 * b, 4 * b + 4)
                    V.tensor_tensor(on[:, r, :], bank(X + b).rearrange("p (a b) -> p a b", a=4),
                                    rstd[:, r].unsqueeze(2).to_broadcast([P, 4, DV]), ALU.mult).then_inc(o_scaled, 1)
                for b in range(B):
                    r = slice(4 * b, 4 * b + 4)
                    dve.wait_ge(o_scaled, at(i, 4, b + 1))
                    V.tensor_tensor(on[:, r, :].rearrange("p a b -> p (a b)"), on[:, r, :].rearrange("p a b -> p (a b)"),
                                    th[:, 2 * b:2 * b + 2, :].rearrange("p a b -> p (a b)"),
                                    ALU.mult).then_inc(o_gated, 1)
                if not last_pair:
                    dve.wait_ge(decay_ready, at(i, 4, 4))
                    V.tensor_copy(a_cur[:], a_neg[:, :, bass.ds(2 * i + 2, 2)]).then_inc(a_picked, 1)
                    head(i + 1)
                scan(i, 3)
                for b in range(B):
                    dve.wait_ge(mixed_ready, at(i, 4, b + 1))
                    r = xres[:, 2 * b:2 * b + 2, :].rearrange("p a b -> p (a b)")
                    if b == 0:
                        dve.wait_ge(mixed_added, at(i, 4, 1))
                    V.tensor_tensor(r, r, bank(X + b % 2), ALU.add).then_inc(mixed_added, 1)

            o_scaled = sem("o_scaled")
            head(0)
            dve.wait_ge(pool_set, 1)
            dve.wait_ge(scan_consts, 96)
            for e in range(ET):
                dve.wait_ge(inner_copied, 2 * e + 2)
                out = conv[:, e].rearrange("p (b t) -> p b t", b=B)
                for tap in range(DC):
                    x_tap = x_pad[:, e, :, tap:tap + T]
                    if tap == 0:
                        ins = V.tensor_scalar(out, x_tap, s_cols[:, e, 0:1], s_cols[:, e, DC:DC + 1], ALU.mult, ALU.add)
                    else:
                        dve.wait_ge(conv_step, 4 * e + tap)
                        ins = V.scalar_tensor_tensor(out=out, in0=x_tap, scalar=s_cols[:, e, tap:tap + 1], in1=out,
                                                     op0=ALU.mult, op1=ALU.add)
                    ins.then_inc(conv_step, 1)
            for e in range(ET):
                dve.wait_ge(scan_act, e + 1)
                V.tensor_scalar(aux[:, e], aux[:, e], 0.5, 0.5, ALU.mult, ALU.add).then_inc(conv_step, 1)
                dve.wait_ge(conv_step, 9 + e)
                V.tensor_tensor(u[:, e], aux[:, e], conv[:, e], ALU.mult).then_inc(u_ready, 1)
            dve.wait_ge(scan_act, 11)
            V.tensor_scalar(aux[:], conv[:], 1.0, None, ALU.add).then_inc(softplus_step, 1)
            dve.wait_ge(softplus_step, 1)
            dve.wait_ge(scan_act, 12)
            V.scalar_tensor_tensor(out=conv[:], in0=aux[:], scalar=-1.0, in1=conv[:], op0=ALU.add,
                                   op1=ALU.subtract).then_inc(softplus_step, 1)
            V.tensor_tensor(delta[:], delta[:], aux2[:], ALU.add).then_inc(softplus_step, 1)
            dve.wait_ge(softplus_step, 3)
            V.tensor_tensor(delta[:], delta[:], conv[:], ALU.subtract).then_inc(softplus_step, 1)
            dve.wait_ge(softplus_step, 4)
            V.tensor_tensor(du[:], delta[:], u[:], ALU.mult).then_inc(u_ready, 1)
            for e in range(ET):
                last = V.tensor_scalar(y[:, e], u[:, e], s_cols[:, e, DC + 2:DC + 3], None, ALU.mult)
            last.then_inc(u_ready, 1)
            dve.wait_ge(a_ready, 2)
            V.tensor_copy(a_cur[:], a_neg[:, :, 0:2]).then_inc(a_picked, 1)
            dve.wait_ge(x_loaded, 32)
            with dve.Fori(0, PAIRS - 1) as i:
                step(i, False)
            step(PAIRS - 1, True)

            def norm(n):
                for t in range(TILES):
                    last = V.bn_stats(stats[:, t, :], xres[:, t, :])
                then(last)
                for t in range(TILES):
                    last = V.bn_aggr(moments[:, t, :], stats[:, t, :])
                last.then_inc(ln_moments, 1)
                dve.wait_ge(ln_scale, 2 * n + 2)
                then(V.scalar_tensor_tensor(out=ln_shift[:], in0=moments[:, :, 0], scalar=-1.0, in1=ln_rstd[:],
                                            op0=ALU.mult, op1=ALU.mult))
                for t in range(TILES):
                    V.tensor_scalar(xres[:, t, :], xres[:, t, :], ln_rstd[:, t:t + 1], ln_shift[:, t:t + 1],
                                    ALU.mult, ALU.add).then_inc(normed, 1)

            dve.wait_ge(mixed_added, 4 * PAIRS + 1)
            norm(0)
            dve.wait_ge(tanh_ready, TILES * PAIRS + 1)
            dve.wait_ge(y_added, 4 * PAIRS + 2)
            then(V.scalar_tensor_tensor(out=v[:], in0=th[:], scalar=1.0, in1=xres[:], op0=ALU.add, op1=ALU.mult))
            for b in range(B):
                V.tensor_tensor(v[:, 2 * b:2 * b + 2, :], v[:, 2 * b:2 * b + 2, :], y[:, :, b * T:(b + 1) * T],
                                ALU.mult).then_inc(y_gated, 1)
            for b in range(B):
                dve.wait_ge(y_turned, b + 1)
                r = xres[:, 2 * b:2 * b + 2, :].rearrange("p a b -> p (a b)")
                V.scalar_tensor_tensor(out=r, in0=bank(X + b), scalar=0.5, in1=r, op0=ALU.mult,
                                       op1=ALU.add).then_inc(y_residual, 1)
            dve.wait_ge(y_residual, 4)
            norm(1)
            dve.wait_ge(route_mm, 1)
            logits = bank(X).rearrange("p (t e) -> p t e", t=TILES)
            def per_tile(col, n):
                return col.unsqueeze(2).to_broadcast([P, TILES, n])

            then(V.tensor_reduce(top_logit[:], logits, AX.X, ALU.max))
            V.memset(score[:, :, E:SC], -7.0)
            V.tensor_tensor(score[:, :, 0:E], logits, per_tile(top_logit[:], E), ALU.subtract).then_inc(route_vec, 1)
            dve.wait_ge(scores_exp, 1)
            then(V.tensor_reduce(score_sum[:], score[:, :, 0:E], AX.X, ALU.add))
            then(V.reciprocal(score_sum[:], score_sum[:]))
            then(V.tensor_tensor(score[:, :, 0:E], score[:, :, 0:E], per_tile(score_sum[:], E), ALU.mult))
            for t in range(TILES):
                last = V.max(top8[:, t, :], score[:, t, 0:E])
            then(last)
            then(V.memset(top8[:, :, TOPK:8], -7.0))
            for t in range(TILES):
                last = V.match_replace(score_rest[:, t, :], top8[:, t, :], score[:, t, :], -9.0)
            then(last)
            then(V.tensor_tensor(chosen[:], score[:, :, 0:E], score_rest[:, :, 0:E], ALU.not_equal))
            V.tensor_copy(chosen_bf[:], chosen[:]).then_inc(route_vec, 1)
            dve.wait_ge(route_mm, 2)
            then(V.tensor_scalar(blocks[:], ps[:, Y, 0:E], P - 1.0, 1.0 / P, ALU.add, ALU.mult))
            then(V.tensor_scalar(blocks[:], blocks[:], -0.498, ROUND, ALU.add, ALU.add))
            then(V.tensor_scalar(blocks[:], blocks[:], -ROUND, None, ALU.add))
            then(V.tensor_tensor_scan(blk_end[:], ones[:, 0:E], blocks[:], 0.0, ALU.mult, ALU.add))
            then(V.tensor_tensor(blk_row[:], blk_end[:], blocks[:], ALU.subtract))
            then(V.tensor_scalar(late[:], blk_end[:], tok_id[:, 0:1], None, ALU.is_le))
            then(V.tensor_reduce(blk_expert[:], late[:], AX.X, ALU.add))
            V.tensor_scalar(blk_expert[:], blk_expert[:], E - 1.0, None, ALU.min).then_inc(route_vec, 1)
            then(V.tensor_scalar(blk_row[:], blk_row[:], float(P), 1.0, ALU.mult, ALU.add))
            then(V.tensor_tensor(place[:], bank(X + 1).rearrange("p (t e) -> p t e", t=TILES),
                                 blk_row[:].unsqueeze(1).to_broadcast([P, TILES, E]), ALU.add))
            then(V.tensor_tensor(place[:], place[:], chosen[:], ALU.mult))
            for t in range(TILES):
                last = V.max(place8[:, t, :], place[:, t, :])
            then(last)
            then(V.tensor_scalar(slot[:], place8[:, :, 0:TOPK], -1.0, None, ALU.add))
            then(V.tensor_copy(slot_idx[:], slot[:]))
            then(V.tensor_scalar(slot_blk[:], slot[:], 1.0 / P, -0.498, ALU.mult, ALU.add))
            then(V.tensor_scalar(slot_blk[:], slot_blk[:], ROUND, None, ALU.add))
            then(V.tensor_scalar(slot_blk[:], slot_blk[:], -ROUND, None, ALU.add))
            then(V.scalar_tensor_tensor(out=slot_row[:], in0=slot_blk[:], scalar=-float(P), in1=slot[:], op0=ALU.mult,
                                        op1=ALU.add))
            for n in range(TILES * TOPK):
                t, k = n // TOPK, n % TOPK
                if n >= 4:
                    dve.wait_ge(hot_used, n - 3)
                V.tensor_scalar(row_hot[:, n % 4, :], iota[:], slot_row[:, t, k:k + 1], tok_id[:, t:t + 1], ALU.is_equal,
                                ALU.mult).then_inc(hot_ready, 1)
                V.tensor_scalar(blk_hot[:, n % 4, :], iota[:, 0:NBLK], slot_blk[:, t, k:k + 1], None,
                                ALU.is_equal).then_inc(hot_ready, 1)
            dve.wait_ge(hot_used, TILES * TOPK)
            V.tensor_copy(tok_of[:], ps[:, Y + 1, 0:NBLK]).then_inc(tok_known, 1)

            def hidden(n, j):
                dve.wait_ge(g_tanh, n + 1)
                V.scalar_tensor_tensor(out=g_th[:, j, :], in0=g_th[:, j, :], scalar=1.0, in1=ps[:, 2 * j + 1, 0:F],
                                       op0=ALU.add, op1=ALU.mult).then_inc(g_silu, 1)
                dve.wait_ge(g_silu, n + 1)
                V.tensor_tensor(hid[:, j, :], g_th[:, j, :], ps[:, 2 * j + 1, F:2 * F], ALU.mult).then_inc(hid_ready, 1)

            for r in range(TILES // NJ):
                for j in range(NJ):
                    hidden(r * NJ + j, j)
                for j in range(NJ):
                    n = r * NJ + j
                    dve.wait_ge(down_ready, n + 1)
                    if n == 0:
                        dve.wait_ge(x_stored, 16)
                    V.scalar_tensor_tensor(out=xres[:, n, :], in0=ps[:, 2 * j, 256:512], scalar=0.5, in1=xres[:, n, :],
                                           op0=ALU.mult, op1=ALU.add).then_inc(down_copied, 1)
            with dve.Fori(0, NBLK // NJ) as i:
                for j in range(NJ):
                    hidden(i * NJ + j + TILES, j)
                for j in range(NJ):
                    dve.wait_ge(down_ready, i * NJ + j + TILES + 1)
                    dve.wait_ge(y_stored[j], at(i, 16, 16))
                    V.tensor_scalar(y_out[:, j, :], ps[:, 2 * j, 256:512], 0.5, None, ALU.mult).then_inc(down_copied, 1)
            for t in range(TILES):
                then(V.tensor_tensor(pick[:], place[:, t, :].unsqueeze(1).to_broadcast([P, TOPK, E]),
                                     place8[:, t, 0:TOPK].unsqueeze(2).to_broadcast([P, TOPK, E]), ALU.is_equal))
                then(V.tensor_tensor(pick[:], pick[:], score[:, t, 0:E].unsqueeze(1).to_broadcast([P, TOPK, E]),
                                     ALU.mult))
                then(V.tensor_reduce(pick_w[:, t, :], pick[:], AX.X, ALU.add))
            for n in range(TILES * TOPK):
                t, k = n // TOPK, n % TOPK
                dve.wait_ge(back[n % 8][0], back[n % 8][1] + 16 * (n // 8 + 1))
                if n:
                    dve.wait_ge(combined, n)
                V.scalar_tensor_tensor(out=xres[:, t, :], in0=yg[:, n % 8, :], scalar=pick_w[:, t, k:k + 1],
                                       in1=xres[:, t, :], op0=ALU.mult, op1=ALU.add).then_inc(combined, 1)
            dve.wait_ge(combined, TILES * TOPK)
            norm(2)
            dve.wait_ge(layer_loaded, 144)
            for t in range(TILES):
                if t % 2 == 0:
                    dve.wait_ge(x_turned, 4 * TURN["x2"] + t // 2 + 1)
                V.tensor_tensor(xres[:, t, :], xres[:, t, :], l_bo[:], ALU.add).then_inc(bias_added, 1)

            def add_exp(n):
                m, c = n // 2, slice((n % 2) * 512, (n % 2) * 512 + 512)
                dve.wait_ge(elu_exp, n + 1)
                V.tensor_tensor(lqT[:, m, c], lqT[:, m, c], lq_low[:, n % 2, :], ALU.add).then_inc(elu_done, 1)

            for n in range(4):
                m, c = n // 2, slice((n % 2) * 512, (n % 2) * 512 + 512)
                dve.wait_ge(lq_ready, n + 1)
                if n >= 2:
                    dve.wait_ge(elu_done, n - 1)
                V.tensor_scalar(lq_low[:, n % 2, :], bank(4 + n), l_bq[:, m:m + 1], 0.0, ALU.add, ALU.min).then_inc(elu_split, 1)
                V.tensor_scalar(lqT[:, m, c], bank(4 + n), l_bq[:, m:m + 1], 0.0, ALU.add, ALU.max).then_inc(elu_split, 1)
                if n:
                    add_exp(n - 1)
            add_exp(3)

            def finish_k(t):
                dve.wait_ge(elu_exp, 4 + t + 1)
                V.scalar_tensor_tensor(out=lk[:, t, :], in0=lk[:, t, :], scalar=0.0, in1=lk_low[:, t % 2, :], op0=ALU.max,
                                       op1=ALU.add).then_inc(elu_done, 1)

            for t in range(TILES):
                dve.wait_ge(lkv_ready, t + 1)
                V.tensor_tensor(lk[:, t, :], bank(t % 4, 0, 256), l_bkv[:, 0:D], ALU.add).then_inc(lkv_added, 1)
                V.tensor_tensor(lv[:, t, :], bank(t % 4, 256, 512), l_bkv[:, D:2 * D], ALU.add).then_inc(lkv_added, 1)
                dve.wait_ge(lkv_added, 2 * t + 1)
                if t >= 2:
                    dve.wait_ge(elu_done, 4 + t - 1)
                V.tensor_scalar(lk_low[:, t % 2, :], lk[:, t, :], 0.0, None, ALU.min).then_inc(elu_split, 1)
                if t:
                    finish_k(t - 1)
            finish_k(TILES - 1)
            for n in range(B * KD):
                dve.wait_ge(kv_ready, n + 1)
                V.tensor_tensor(kv[:, n, :], ps[:, 4 + n % 4, 0:KVW], head_mask[:], ALU.mult).then_inc(kv_masked, 1)
            for t in range(TILES):
                dve.wait_ge(num_ready, t + 1)
                src = ps[:, t % 4, 0:KD * KVW].rearrange("p (k n) -> p k n", k=KD)
                then(V.tensor_scalar(l_den[:, t], src[:, :, P:KVW], 1e-8, None, ALU.add))
                then(V.reciprocal(l_den[:, t], l_den[:, t]))
                for k in range(KD):
                    last = V.tensor_tensor(l_out[:, t, k * P:(k + 1) * P].rearrange("p (h d) -> p h d", h=LB),
                                           src[:, k, 0:P].rearrange("p (h d) -> p h d", h=LB),
                                           l_den[:, t, k, :].unsqueeze(2).to_broadcast([P, LB, P // LB]), ALU.mult)
                last.then_inc(att_ready, 1)

            def add_att(n):
                for t in range(TILES):
                    dve.wait_ge(proj_out_ready, 8 * n + t + 1)
                    dve.wait_ge(bias_added, 8 * n + t + 1)
                    V.tensor_tensor(xres[:, t, :], xres[:, t, :], ps[:, t % 4, 0:D], ALU.add).then_inc(attended, 1)
                dve.wait_ge(attended, 8 * n + 8)

            add_att(0)
            norm(3)
            dve.wait_ge(layer_loaded, 288)
            pi = float(np.pi)
            for half, freq in enumerate((1.0, 0.01)):
                for n in range(2):
                    out = ang[:, :, n, half::2]
                    last = V.tensor_scalar(out, pos[:], freq, (0.5 * pi, 0.0)[n], ALU.mult, ALU.add)
            last.then_inc(angle, 1)
            dve.wait_ge(angle, 1)
            V.tensor_scalar(turns[:], ang[:], 0.5 / pi, ROUND, ALU.mult, ALU.add).then_inc(angle, 1)
            dve.wait_ge(angle, 2)
            V.tensor_scalar(turns[:], turns[:], -ROUND, None, ALU.add).then_inc(angle, 1)
            dve.wait_ge(angle, 3)
            V.scalar_tensor_tensor(out=ang[:], in0=turns[:], scalar=-2.0 * pi, in1=ang[:], op0=ALU.mult,
                                   op1=ALU.add).then_inc(angle, 1)
            dve.wait_ge(angle, 4)
            in_pi = 3.1415925
            V.tensor_scalar(ang[:], ang[:], in_pi, -in_pi, ALU.min, ALU.max).then_inc(angle, 2)
            dve.wait_ge(cos_sin_ready, 1)

            def rotate(src, dst, tiles, n, size):
                pairs = src.rearrange("p (t h c two) -> p t h c two", t=tiles.stop - tiles.start, h=XH, two=2)
                out = dst[:, tiles, :].rearrange("p t (h c two) -> p t h c two", h=XH, two=2)
                shape = [P, tiles.stop - tiles.start, XH, 4]
                for turn in range(2):
                    for two in range(2):
                        w = cos_sin[:, tiles, turn ^ two, :].unsqueeze(2).to_broadcast(shape)
                        prod = rot[:, turn, two, 0:size].rearrange("p (t h c) -> p t h c", t=shape[1], h=XH)
                        V.tensor_tensor(prod, pairs[:, :, :, :, two], w, ALU.mult).then_inc(turns_done, 1)
                dve.wait_ge(turns_done, 4 * n + 4)
                for turn in range(2):
                    o = out[:, :, :, :, turn]
                    p0, p1 = (rot[:, turn, two, 0:size].rearrange("p (t h c) -> p t h c", t=shape[1], h=XH) for two in range(2))
                    V.tensor_tensor(o, p0, p1, (ALU.subtract, ALU.add)[turn]).then_inc(rotated, 1)
                dve.wait_ge(rotated, 2 * n + 2)

            for t in range(TILES):
                dve.wait_ge(xv_copied, t + 1)
                rotate(bank(t % 4, 0, 256), k_rot, slice(t, t + 1), t, P)

            def stack(n, src, dst, order):
                for j in range(2):
                    dve.wait_ge(part_cast, 3 * n + j + 1)
                    V.tensor_tensor(src[:], src[:], part[:, j], ALU.subtract).then_inc(part_rest, 1)
                    dve.wait_ge(part_rest, 2 * n + j + 1)
                dve.wait_ge(part_cast, 3 * n + 3)
                for slot_n, j in enumerate(order):
                    V.tensor_copy(dst[:, :, :, slot_n * XD_H:(slot_n + 1) * XD_H],
                                  part[:, j].rearrange("p t (h d) -> p t h d", h=XH)).then_inc(stacked, 1)

            stack(0, k_rot, k_st, (0, 1, 0, 2, 1, 0))
            for t in range(TILES):
                if t % 2 == 0:
                    dve.wait_ge(x_turned, 4 * TURN["x3"] + t // 2 + 1)
                V.tensor_tensor(xres[:, t, :], xres[:, t, :], x_bo[:], ALU.add).then_inc(bias_added, 1)
            for b in range(B):
                dve.wait_ge(xq_ready, b + 1)
                rotate(bank(4 + b), q_rot, slice(2 * b, 2 * b + 2), TILES + b, 256)
            stack(1, q_rot, q_st, (0, 0, 1, 0, 1, 2))
            with dve.Fori(0, XPAIRS) as i:
                for n in range(2):
                    dve.wait_ge(heads_turned, at(i, 4, n + 3))
                    V.tensor_copy(ksT[:, n * 512:(n + 1) * 512], bank(2 + n)).then_inc(ksT_copied, 1)
                for b in range(B):
                    dve.wait_ge(rows_ready, at(i, 4, b + 1))
                    V.tensor_reduce(row_max[:, 4 * b:4 * b + 4],
                                    pair(4 + 2 * (b % 2)).rearrange("p (a k) -> p a k", a=4), AX.X,
                                    ALU.max).then_inc(rows_maxed, 1)
                dve.wait_ge(rows_maxed, at(i, 4, 4))
                V.tensor_scalar(row_max[:], row_max[:], -1.0, None, ALU.mult).then_inc(shift_step, 1)
                dve.wait_ge(shift_step, at(i, 5, 1))
                maxima = row_max[:].rearrange("p (b h q) -> p h b q", b=B, h=2)
                for j in range(3):
                    part_j = shift[:, :, 8 * j:8 * j + 8].rearrange("p h (b q) -> p h b q", b=B)
                    V.tensor_copy(part_j, maxima).then_inc(shift_ready if j == 2 else shift_step, 1)
                    if j < 2:
                        dve.wait_ge(shift_step, at(i, 5, 2 + 2 * j))
                        V.tensor_tensor(maxima, maxima, part_j, ALU.subtract).then_inc(shift_step, 1)
                        dve.wait_ge(shift_step, at(i, 5, 3 + 2 * j))
                dve.wait_ge(pv_ready, at(i, 1, 1))
                o = ps[:, 1, 0:16 * VA].rearrange("p (t h d) -> p t h d", t=TILES, h=2)
                V.reciprocal(x_den[:].rearrange("p (t h) -> p t h", h=2), o[:, :, :, XD_H]).then_inc(den_inv, 1)
                dve.wait_ge(den_inv, at(i, 1, 1))
                V.tensor_tensor(x_att[:, :, bass.ds(2 * XD_H * i, 2 * XD_H)].rearrange("p t (h d) -> p t h d", h=2),
                                o[:, :, :, 0:XD_H],
                                x_den[:].rearrange("p (t h) -> p t h", h=2).unsqueeze(3).to_broadcast([P, TILES, 2, XD_H]),
                                ALU.mult).then_inc(head_out, 1)
            dve.wait_ge(head_out, XPAIRS + 1)
            add_att(1)
            norm(4)
            dve.wait_ge(x_turned, 4 * TURN["att1"] + 4)
            for n, w in enumerate((f_in, f_out)):
                V.tensor_reduce(f_sum[:, n:n + 1], w[:].rearrange("p a b -> p (a b)"), AX.X, ALU.add,
                                apply_absolute_value=True).then_inc(f_summed, 1)
            dve.wait_ge(f_total, 1)
            then(V.tensor_scalar(f_scale[:], ps[:, 7, 0:2], 1.0 / (D * HF), 1e-5, ALU.mult, ALU.max))
            then(V.reciprocal(f_inv[:], f_scale[:]))
            for n, (w, q) in enumerate(((f_in, q_in), (f_out, q_out))):
                then(V.tensor_scalar(w[:], w[:], f_inv[:, n:n + 1], ROUND, ALU.mult, ALU.add))
                then(V.tensor_scalar(w[:], w[:], -ROUND, 1.0, ALU.add, ALU.min))
                V.tensor_scalar(q[:], w[:], -1.0, None, ALU.max).then_inc(ternary, 1)
            dve.wait_ge(xT_copied, 4 * TURN["x4"] + 4)
            for j in range(2):
                dve.wait_ge(part_cast, 6 + j + 1)
                V.tensor_tensor(xT[:], xT[:], x_part[:, j], ALU.subtract).then_inc(part_rest, 1)
                dve.wait_ge(part_rest, 4 + j + 1)

            def quantize(t):
                j = t % 2
                dve.wait_ge(h_square, t + 1)
                then(V.tensor_reduce(f_max[:, j:j + 1], hid_f[:, j], AX.X, ALU.max))
                then(V.tensor_scalar(f_max[:, j:j + 1], f_max[:, j:j + 1], 1e-5, None, ALU.max))
                V.reciprocal(f_rmax[:, j:j + 1], f_max[:, j:j + 1])
                then(V.tensor_scalar(f_back[:, j:j + 1], f_max[:, j:j + 1], f_scale[:, 1:2], 1.0 / 255, ALU.mult,
                                     ALU.mult))
                then(V.tensor_scalar(hid_f[:, j], hid_f[:, j], f_rmax[:, j:j + 1], 255.0, ALU.mult, ALU.mult))
                if t >= 2:
                    dve.wait_ge(hq_turned, t - 1)
                V.tensor_scalar(hid_q[:, j], hid_f[:, j], ROUND, -ROUND, ALU.add, ALU.add).then_inc(hq_ready, 1)

            def add_ffn(t):
                dve.wait_ge(f_out_ready, t + 1)
                V.scalar_tensor_tensor(out=xres[:, t, :], in0=ps[:, 6 + t % 2, 0:D], scalar=f_back[:, t % 2:t % 2 + 1],
                                       in1=xres[:, t, :], op0=ALU.mult, op1=ALU.add).then_inc(f_added, 1)

            for t in range(TILES):
                quantize(t)
                if t:
                    add_ffn(t - 1)
            add_ffn(TILES - 1)
            dve.wait_ge(f_added, TILES)
            norm(5)


def host_layout(inp):
    g = {k: np.asarray(v) for k, v in inp.items()}
    x = g["x"].reshape(TOK, D)

    def kp(w):
        return w.reshape(-1, P, w.shape[-1]).transpose(1, 0, 2)

    q, k, s = (kp(g["L0_attn_W" + n]).reshape(P, KD, PAIRS, P) for n in "qks")
    v, w = (kp(g["L0_attn_W" + n]).reshape(P, KD, PAIRS, 256) for n in "vg")
    t = np.triu(np.ones((P, P), np.float32))
    col = {n: g["L0_xattn_" + n].reshape(ET, P, -1) for n in ("conv_w", "conv_b", "dt_proj_b", "D", "A_log")}
    out = dict(
        x_tok=x.reshape(TILES, P, D).transpose(1, 0, 2), xT=kp(x.T),
        wqks=np.concatenate([q, k, s], 3).transpose(2, 0, 1, 3), wvg=np.concatenate([v, w], 3).transpose(2, 0, 1, 3),
        wo=g["L0_attn_Wo"].reshape(PAIRS, 2, DV, D).transpose(0, 2, 1, 3),
        gnorm=g["L0_attn_g_norm_weight"].reshape(P, 1),
        ident=np.eye(P, dtype=np.float32), tri=np.concatenate([t, np.ones((P, P), np.float32), t], 1),
        ctxT=g["ctx_1024"].reshape(TOK, CTX).T, w_in=g["L0_xattn_in_proj_w"].T, xp_w=kp(g["L0_xattn_x_proj_w"].T),
        dt_w=g["L0_xattn_dt_proj_w"].T,
        s_cols=np.concatenate([col[n] for n in ("conv_w", "conv_b", "dt_proj_b", "D")], 2).transpose(1, 0, 2),
        a_log=col["A_log"].transpose(1, 0, 2),
    )
    def ffn(gate, value, down):
        lead = gate.shape[:-2]
        gv = np.concatenate([gate, value], -1).reshape(*lead, KD, P, 2 * F)
        return np.moveaxis(gv, -3, -2), np.moveaxis(down.reshape(*lead, 2, FH, D), -3, -2)

    out["w_router"] = kp(g["L0_ffn_w_router"].T)
    out["w_gv"], out["w_dn"] = ffn(g["L0_ffn_wg"], g["L0_ffn_wv"], g["L0_ffn_wo"])
    out["sh_gv"], out["sh_dn"] = ffn(g["L0_ffn_swg"], g["L0_ffn_swv"], g["L0_ffn_swo"])
    bf16 = mybir.dt.np(BF16)
    out["iota"] = np.tile(np.arange(P, dtype=np.float32), (P, 1))
    out["tok_id"] = np.arange(TOK, dtype=np.float32).reshape(TILES, P).T
    out["tri_bf"] = np.triu(np.ones((P, P), np.float32), 1).astype(bf16)
    out["l_wq"], out["l_wo"] = kp(g["L1_attn_wq"].T), kp(g["L1_attn_wo"].T)
    out["l_wkv"] = np.concatenate([kp(g["L1_attn_wk"].T), kp(g["L1_attn_wv"].T)], 2)
    out["l_bq"] = g["L1_attn_bq"].reshape(KD, P).T
    out["l_bkv"] = np.concatenate([g["L1_attn_bk"], g["L1_attn_bv"]]).reshape(1, 2 * D)
    out["l_bo"] = g["L1_attn_bo"].reshape(1, D)
    same = np.arange(P)[:, None] // (P // LB)
    out["head_mask"] = np.concatenate([same == same.T, same == np.arange(LB)], 1).astype(np.float32)
    out["x_wq"], out["x_wo"] = kp(g["L1_xattn_Wq"]), kp(g["L1_xattn_Wout"])
    out["x_wkv"], out["x_bo"] = g["L1_xattn_Wkv"], g["L1_xattn_bout"].reshape(1, D)
    out["pos"] = kp(g["fside_BxSx2_0"].reshape(TOK, 2))
    out["ident_bf"] = np.eye(P, dtype=np.float32).astype(bf16)
    row = np.arange(P) % SLOT
    sel = (row[:, None] % 8 == np.arange(8)) & (row[:, None] < 3 * 8)
    out["shift_sel"] = np.repeat(sel.astype(bf16)[:, :, None], P, 2)
    out["f_in"], out["f_out"] = kp(g["L1_ffn_c_fc"]), kp(g["L1_ffn_c_proj"].T)
    return {n: np.ascontiguousarray(m) for n, m in out.items()}


def kernel(**inputs):
    from concourse import bacc
    from concourse.bass_utils import run_bass_kernel_spmd

    nc = bacc.Bacc("TRN2", target_bir_lowering=False, num_devices=1)
    arrays = {"in_" + name: array for name, array in host_layout(inputs).items()}
    args = {name[3:]: nc.dram_tensor(name, m.shape, mybir.dt.from_np(m.dtype), kind="ExternalInput").ap()
            for name, m in arrays.items()}
    out = nc.dram_tensor("out", (B, T, D), F32, kind="ExternalOutput").ap()
    build(nc, args, out)
    return run_bass_kernel_spmd(nc, [arrays], core_ids=[0]).results[0]["out"]
```

```python
from contextlib import ExitStack

import numpy as np

import concourse.bass as bass
from concourse import mybir

F32 = mybir.dt.float32
BF16 = mybir.dt.bfloat16
ALU = mybir.AluOpType
ACT = mybir.ActivationFunctionType
AX = mybir.AxisListType

P = 128
B, T, D = 4, 256, 256
TOK = B * T
TILES = TOK // P
KD = D // P
LN_EPS = 1e-5
H, DK, DV, M = 16, 64, 128, 64
PAIRS = H // 2
CLAMP = 32.0
CTX = 128
DI, DS, DR, DC = 256, 16, 8, 4
ET = DI // P
XD = DR + 2 * DS
E, TOPK, F = 64, 6, 176
FH = F // 2
SC = E + 2
NJ = 4
NBLK = -(-((TOK * TOPK + E * (P - 1)) // P) // NJ) * NJ
LEAST_GROUPS = TOK * TOPK // P // NJ
ROUND = 1.5 * 2.0 ** 23
LH = 16
LB = P // (D // LH)
KVW = P + LB
XH, XD_H = 32, 8
XPAIRS = XH // 2
SLOT = 64
SHIFT = 6 * XD_H
GH = P // (2 * XD_H)
GAP = P // 2 - XD_H
VW = 3 * GAP + 2 * XD_H
XGROUPS = XH // GH
GP = GH // 2
ITEMS = B * GP
HF = 4 * D
KH = HF // P


TURN = dict(x1=0, x2=1, att0=2, x3=3, x4=4)


def at(i, per, c):
    return i * per + c


def build(nc, a, out):
    with ExitStack() as ctx:
        mem = [ctx]

        def sb(name, shape, dt=F32):
            return mem[-1].enter_context(nc.sbuf_tensor(name, shape, dt))

        def sem(name):
            return ctx.enter_context(nc.semaphore(name))

        ps = ctx.enter_context(nc.psum_tensor("ps", [P, 8, 512], F32))
        PJ, AB, X, Y = 0, 2, 4, 6

        xres = sb("xres", [P, TILES, D])
        xT = sb("xT", [P, KD, TOK])
        ident = sb("ident", [P, P])
        tri = sb("tri", [P, 384])
        ones = sb("ones", [P, 256])
        ctxT = sb("ctxT", [P, TOK])
        stats = sb("stats", [P, TILES, 6])
        moments = sb("moments", [P, TILES, 2])
        ln_var = sb("ln_var", [P, TILES])
        ln_rstd = sb("ln_rstd", [P, TILES])
        ln_shift = sb("ln_shift", [P, TILES])
        blank = sb("blank", [P, D])
        eps_col = sb("eps_col", [P, 1])
        attn_mem = ExitStack()
        mem.append(attn_mem)
        w_qks = sb("w_qks", [P, KD, 384])
        w_vg = sb("w_vg", [P, KD, 512])
        w_o = sb("w_o", [P, 2, D])
        gn_half = sb("gn_half", [P, 1])
        qT = sb("qT", [P, TOK])
        kT = sb("kT", [P, TOK])
        sT = sb("sT", [P, TOK])
        eT = sb("eT", [P, TOK])
        e_tok = sb("e_tok", [P, TILES, P])
        zT = sb("zT", [P, TOK])
        zi = sb("zi", [P, TILES, P])
        aT = sb("aT", [P, 8, 384])
        okn = sb("okn", [P, TILES * 2, M])
        pe_ = sb("pexp", [P, TILES * 2, M])
        okmax = sb("okmax", [P, TILES * 2])
        psum_ = sb("psum_", [P, TILES * 2])
        wT = sb("wT", [P, TOK])
        v = sb("v", [P, TILES, 256])
        th = sb("th", [P, TILES, 256])
        on = sb("on", [P, TILES * 2, DV])
        sq = sb("sq", [P, 2, 4, DV])
        ss = sb("ss", [P, TILES * 2])
        lnv = sb("lnv", [P, TILES * 2])
        rstd = sb("rstd", [P, TILES * 2])
        oT = sb("oT", [P, 2, TOK])
        w_in = sb("w_in", [P, DI])
        xp_w = sb("xp_w", [P, ET, XD])
        dt_w = sb("dt_w", [DR, DI])
        s_cols = sb("s_cols", [P, ET, DC + 3])
        a_neg = sb("a_neg", [P, ET, DS])
        a_cur = sb("a_cur", [P, ET, 2])
        x_dbl = sb("x_dbl", [XD, TOK])
        u = sb("u", [P, ET, TOK])
        delta = sb("delta", [P, ET, TOK])
        du = sb("du", [P, ET, TOK])
        y = sb("y", [P, ET, TOK])
        b_row = sb("b_row", [P, 2, TOK])
        c_row = sb("c_row", [P, 2, TOK])
        decay = sb("decay", [P, 2, TOK])
        drive = sb("drive", [P, 2, TOK])
        state = sb("state", [P, 2, TOK])
        x_pad = aT[:].rearrange("p a b -> p (a b)")[:, 0:ET * B * (T + 3)].rearrange(
            "p (e b t) -> p e b t", e=ET, b=B)
        conv = v[:].rearrange("p a b -> p (a b)").rearrange("p (e n) -> p e n", e=ET)
        aux = th[:].rearrange("p a b -> p (a b)").rearrange("p (e n) -> p e n", e=ET)
        aux2 = on[:].rearrange("p a b -> p (a b)").rearrange("p (e n) -> p e n", e=ET)
        mem.pop()
        attn_mem.close()

        moe_mem = ExitStack()
        mem.append(moe_mem)
        U32 = mybir.dt.uint32
        w_router = sb("w_router", [P, KD, E])
        iota = sb("iota", [P, P])
        tok_id = sb("tok_id", [P, TILES])
        tri_bf = sb("tri_bf", [P, P], BF16)
        ones_bf = sb("ones_bf", [P, P], BF16)
        top_logit = sb("top_logit", [P, TILES])
        score_sum = sb("score_sum", [P, TILES])
        score = sb("score", [P, TILES, SC])
        score_rest = sb("score_rest", [P, TILES, SC])
        top8 = sb("top8", [P, TILES, 8])
        chosen = sb("chosen", [P, TILES, E])
        chosen_bf = sb("chosen_bf", [P, TILES, E], BF16)
        blocks = sb("blocks", [P, E])
        blk_end = sb("blk_end", [P, E])
        blk_row = sb("blk_row", [P, E])
        place = sb("place", [P, TILES, E])
        place8 = sb("place8", [P, TILES, 8])
        slot = sb("slot", [P, TILES, TOPK])
        slot_blk = sb("slot_blk", [P, TILES, TOPK])
        slot_row = sb("slot_row", [P, TILES, TOPK])
        slot_idx = sb("slot_idx", [P, TILES, TOPK], U32)
        pick = sb("pick", [P, TOPK, E])
        pick_w = sb("pick_w", [P, TILES, TOPK])
        late = sb("late", [P, E])
        blk_expert = sb("blk_expert", [P, 1])
        expert_row = sb("expert_row", [1, P], mybir.dt.int32)
        groups_f = sb("groups_f", [1, 1])
        groups = sb("groups", [1, 1], mybir.dt.int32)
        row_hot = sb("row_hot", [P, 4, P])
        blk_hot = sb("blk_hot", [P, 4, NBLK])
        tok_of = sb("tok_of", [P, NBLK], U32)
        tok_cur = sb("tok_cur", [P, NJ], U32)
        xg = sb("xg", [P, NJ, D])
        xgT = sb("xgT", [P, NJ, KD * P])
        w_gv = sb("w_gv", [P, NJ, KD, 2 * F])
        w_dn = sb("w_dn", [FH, NJ, 2, D])
        sh_gv = sb("sh_gv", [P, KD, 2 * F])
        sh_dn = sb("sh_dn", [FH, 2, D])
        g_th = sb("g_th", [P, NJ, F])
        hid = sb("hid", [P, NJ, F])
        hidT = sb("hidT", [FH, NJ, 2 * P])
        y_out = sb("y_out", [P, NJ, D])
        yg = sb("yg", [P, 8, D])
        l_wq = sb("l_wq", [P, KD, D])
        l_wkv = sb("l_wkv", [P, KD, 2 * D])
        l_wo = sb("l_wo", [P, KD, D])
        l_bq = sb("l_bq", [P, KD])
        l_bkv = sb("l_bkv", [P, 2 * D])
        l_bo = sb("l_bo", [P, D])
        head_mask = sb("head_mask", [P, KVW])
        lqT = sb("lqT", [P, KD, TOK])
        lq_low = sb("lq_low", [P, 2, 512])
        lk = sb("lk", [P, TILES, D])
        lk_low = sb("lk_low", [P, 2, D])
        lv = sb("lv", [P, TILES, D])
        kv = sb("kv", [P, B * KD, KVW])
        l_den = sb("l_den", [P, TILES, KD, LB])
        l_out = sb("l_out", [P, TILES, D])
        mem.pop()
        moe_mem.close()
        last_mem = ExitStack()
        mem.append(last_mem)
        x_wq = sb("x_wq", [P, KD, D])
        x_wkv = sb("x_wkv", [P, 2 * D])
        x_wo = sb("x_wo", [P, KD, D])
        x_bo = sb("x_bo", [P, D])
        ident_bf = sb("ident_bf", [P, P], BF16)
        pos = sb("pos", [P, TILES, 2])
        ang = sb("ang", [P, TILES, 2, 4])
        turns = sb("turns", [P, TILES, 2, 4])
        cos_sin = sb("cos_sin", [P, TILES, 2, 4])
        rot = sb("rot", [P, 2, 2, 512])
        q_rot = sb("q_rot", [P, TILES, D])
        k_rot = sb("k_rot", [P, TILES, D])
        x_v = sb("x_v", [P, TILES, D])
        v_win = sb("v_win", [P, 2, 2, 2, VW])
        part = sb("part", [P, 3, TILES, D], BF16)
        q_st = sb("q_st", [P, TILES, XH, SLOT], BF16)
        k_st = sb("k_st", [P, TILES, XH, SLOT], BF16)
        qsT = sb("qsT", [P, GP, TOK], BF16)
        ksT = sb("ksT", [P, GP, TOK], BF16)
        row_max = sb("row_max", [P, XPAIRS * 16])
        shift = sb("shift", [P, 3, XPAIRS * 16], BF16)
        probT = sb("probT", [P, 4, 2, 2 * P])
        x_den = sb("x_den", [P // 2, 2, 256])
        f_in = sb("f_in", [P, KD, HF])
        f_out = sb("f_out", [P, KH, D])
        f_sum = sb("f_sum", [P, 2])
        f_scale = sb("f_scale", [P, 2])
        f_inv = sb("f_inv", [P, 2])
        q_in = sb("q_in", [P, KD, HF], BF16)
        q_out = sb("q_out", [P, KH, D], BF16)
        x_part = part[:].rearrange("p a b c -> p a (b c)").rearrange("p a (k n) -> p a k n", k=KD)
        hid_f = q_rot[:].rearrange("p a b -> p (a b)").rearrange("p (a b) -> p a b", a=2)
        hid_q = k_rot[:].rearrange("p a b -> p (a b)").bitcast(BF16).rearrange("p (a b) -> p a b", a=4)
        f_max = sb("f_max", [P, 2])
        f_rmax = sb("f_rmax", [P, 2])
        f_back = sb("f_back", [P, 2])
        mem.pop()
        last_mem.close()

        x_dram = nc.dram_tensor("x_dram", (TOK, D), F32).ap()
        y_dram = nc.dram_tensor("y_dram", (NBLK * P, D), F32).ap()
        x_dbl_dram = nc.dram_tensor("x_dbl_dram", (XD, TOK), F32).ap()

        x_loaded = sem("x_loaded")
        const_loaded = sem("const_loaded")
        const_set = sem("const_set")
        qks_loaded = sem("qks_loaded")
        vg_loaded = sem("vg_loaded")
        wo_loaded = sem("wo_loaded")
        proj_ready = sem("proj_ready")
        qk_copied = sem("qk_copied")
        s_clipped = sem("s_clipped")
        eT_ready = sem("eT_ready")
        zT_ready = sem("zT_ready")
        lnz_ready = sem("lnz_ready")
        scores_ready = sem("scores_ready")
        scores_masked = sem("scores_masked")
        e_turned = sem("e_turned")
        e_copied = sem("e_copied")
        z_turned = sem("z_turned")
        zi_ready = sem("zi_ready")
        slots_ready = sem("slots_ready")
        slots_shifted = sem("slots_shifted")
        slots_exp = sem("slots_exp")
        w_ready = sem("w_ready")
        tanh_ready = sem("tanh_ready")
        gate_ready = sem("gate_ready")
        w_turned = sem("w_turned")
        wT_copied = sem("wT_copied")
        read_ready = sem("read_ready")
        read_masked = sem("read_masked")
        o_ready = sem("o_ready")
        squares_ready = sem("squares_ready")
        squares_read = sem("squares_read")
        rstd_ready = sem("rstd_ready")
        o_scaled = sem("o_scaled")
        o_gated = sem("o_gated")
        o_turned = sem("o_turned")
        oT_copied = sem("oT_copied")
        mixed_ready = sem("mixed_ready")
        mixed_added = sem("mixed_added")
        vec_step = sem("vec_step")
        chain = sem("chain")
        act_step = sem("act_step")
        scan_consts = sem("scan_consts")
        scan_mm = sem("scan_mm")
        inner_copied = sem("inner_copied")
        pool_set = sem("pool_set")
        conv_step = sem("conv_step")
        u_ready = sem("u_ready")
        x_dbl_copied = sem("x_dbl_copied")
        x_dbl_stored = sem("x_dbl_stored")
        scan_act = sem("scan_act")
        softplus_step = sem("softplus_step")
        a_ready = sem("a_ready")
        bc_loaded = [sem(f"bc_loaded{j}") for j in range(2)]
        a_picked = sem("a_picked")
        decay_ready = sem("decay_ready")
        drive_ready = sem("drive_ready")
        scanned = sem("scanned")
        read_out = sem("read_out")
        y_added = sem("y_added")
        ln_moments = sem("ln_moments")
        ln_scale = sem("ln_scale")
        normed = sem("normed")
        x_turned = sem("x_turned")
        xT_copied = sem("xT_copied")
        y_gated = sem("y_gated")
        y_turned = sem("y_turned")
        y_residual = sem("y_residual")
        moe_consts = sem("moe_consts")
        route_mm = sem("route_mm")
        groups_known = sem("groups_known")
        route_vec = sem("route_vec")
        route_act = sem("route_act")
        hot_ready = sem("hot_ready")
        hot_used = sem("hot_used")
        tok_known = sem("tok_known")
        tok_picked = sem("tok_picked")
        gather_due = sem("gather_due")
        x_stored = sem("x_stored")
        gathered = [sem(f"gathered{j}") for j in range(NJ)]
        w_loaded = [sem(f"w_loaded{j}") for j in range(NJ)]
        y_stored = [sem(f"y_stored{j}") for j in range(NJ)]
        xg_turned = sem("xg_turned")
        xgT_copied = sem("xgT_copied")
        gv_ready = sem("gv_ready")
        g_tanh = sem("g_tanh")
        g_silu = sem("g_silu")
        hid_ready = sem("hid_ready")
        hid_turned = sem("hid_turned")
        hidT_copied = sem("hidT_copied")
        down_ready = sem("down_ready")
        down_copied = sem("down_copied")
        y_blank = sem("y_blank")
        back = [sem(f"back{j}") for j in range(8)]
        combined = sem("combined")
        lq_ready = sem("lq_ready")
        elu_split = sem("elu_split")
        elu_exp = sem("elu_exp")
        elu_done = sem("elu_done")
        lkv_ready = sem("lkv_ready")
        lkv_added = sem("lkv_added")
        kv_ready = sem("kv_ready")
        kv_masked = sem("kv_masked")
        num_ready = sem("num_ready")
        att_ready = sem("att_ready")
        proj_out_ready = sem("proj_out_ready")
        bias_added = sem("bias_added")
        attended = sem("attended")
        layer_loaded = sem("layer_loaded")
        angle = sem("angle")
        cos_sin_ready = sem("cos_sin_ready")
        xkv_ready = sem("xkv_ready")
        xv_copied = sem("xv_copied")
        turns_done = sem("turns_done")
        rotated = sem("rotated")
        xq_ready = sem("xq_ready")
        part_cast = sem("part_cast")
        part_rest = sem("part_rest")
        stacked = sem("stacked")
        heads_turned = sem("heads_turned")
        qsT_copied = sem("qsT_copied")
        ksT_copied = sem("ksT_copied")
        rows_ready = sem("rows_ready")
        rows_maxed = sem("rows_maxed")
        shifted = sem("shifted")
        cols_ready = sem("cols_ready")
        prob_ready = sem("prob_ready")
        pv_ready = sem("pv_ready")
        acc_free = sem("acc_free")
        v_placed = sem("v_placed")
        f_total = sem("f_total")
        ternary = sem("ternary")
        h_ready = sem("h_ready")
        h_relu = sem("h_relu")
        h_square = sem("h_square")
        hq_ready = sem("hq_ready")
        hq_turned = sem("hq_turned")
        hqT_copied = sem("hqT_copied")
        f_out_ready = sem("f_out_ready")
        f_added = sem("f_added")

        block = ctx.enter_context(nc.Block())

        def bank(n, a=0, b=512):
            return ps[:, n, a:b]

        def pair(n):
            return ps[:, n:n + 2, :].rearrange("p a b -> p (a b)")

        def used_groups(engine):
            engine.wait_ge(groups_known, 1)
            return engine.value_load(groups[0:1, 0:1], min_val=LEAST_GROUPS, max_val=NBLK // NJ)

        @block.sync
        def _(sp):
            sp.dma_start(xT[:], a["xT"]).then_inc(x_loaded, 16)
            sp.dma_start(w_qks[:], a["wqks"][0]).then_inc(qks_loaded, 16)
            sp.dma_start(ident[:], a["ident"]).then_inc(const_loaded, 16)
            sp.dma_start(w_vg[:], a["wvg"][0]).then_inc(vg_loaded, 16)
            sp.wait_ge(const_loaded, 16)
            sp.dma_start(tri[:], a["tri"]).then_inc(const_loaded, 16)
            sp.wait_ge(const_loaded, 32)
            sp.dma_start(gn_half[:], a["gnorm"]).then_inc(const_loaded, 16)
            sp.dma_start(w_o[:], a["wo"][0]).then_inc(wo_loaded, 16)
            sp.wait_ge(x_loaded, 16)
            sp.dma_start(xres[:], a["x_tok"]).then_inc(x_loaded, 16)
            for dst, src in ((ctxT, "ctxT"), (w_in, "w_in"), (xp_w, "xp_w"), (dt_w, "dt_w"), (s_cols, "s_cols"),
                             (a_neg, "a_log")):
                sp.dma_start(dst[:], a[src]).then_inc(scan_consts, 16)
            sp.wait_ge(pool_set, 2)
            step_rows = NBLK // NJ
            for r in range(LEAST_GROUPS * NJ, NBLK, step_rows):
                n = min(step_rows, NBLK - r)
                sp.dma_start(y_dram[r * P:(r + n) * P, :].rearrange("(n p) d -> p n d", p=P),
                             blank[:].unsqueeze(1).to_broadcast([P, n, D])).then_inc(y_blank, 16)
            sp.wait_ge(proj_ready, 6)
            sp.dma_start(w_qks[:], a["wqks"][1]).then_inc(qks_loaded, 16)
            sp.wait_ge(x_dbl_copied, 2)
            sp.dma_start(x_dbl_dram, x_dbl[:]).then_inc(x_dbl_stored, 16)
            sp.wait_ge(x_dbl_stored, 16)

            def scan_rows(i, j):
                row = DR + 2 * i + j
                for dst, r in ((b_row, row), (c_row, row + DS)):
                    src = x_dbl_dram[bass.ds(r, 1), :].to_broadcast([P, TOK])
                    sp.dma_start(dst[:, j, :], src).then_inc(bc_loaded[j], 16)

            for j in range(2):
                scan_rows(0, j)

            def loads(i, last):
                sp.wait_ge(proj_ready, at(i, 14, 14))
                sp.dma_start(w_vg[:], a["wvg"][bass.ds(i + 1, 1)].rearrange("a p k n -> (a p) k n")).then_inc(vg_loaded, 16)
                if not last:
                    sp.wait_ge(proj_ready, at(i, 14, 20))
                    sp.dma_start(w_qks[:], a["wqks"][bass.ds(i + 2, 1)].rearrange("a p k n -> (a p) k n")).then_inc(qks_loaded, 16)
                sp.wait_ge(mixed_ready, at(i, 4, 4))
                sp.dma_start(w_o[:], a["wo"][bass.ds(i + 1, 1)].rearrange("a p k n -> (a p) k n")).then_inc(wo_loaded, 16)
                for j in range(2):
                    sp.wait_ge(read_out, at(i, 4, 2 * j + 2))
                    scan_rows(i + 1, j)

            with sp.Fori(0, PAIRS - 2) as i:
                loads(i, False)
            loads(PAIRS - 2, True)
            sp.wait_ge(y_turned, 4)
            for dst, src in ((w_router, "w_router"), (iota, "iota"), (tok_id, "tok_id"), (tri_bf, "tri_bf")):
                sp.dma_start(dst[:], a[src]).then_inc(moe_consts, 16)
            sp.dma_start(sh_gv[:], a["sh_gv"]).then_inc(layer_loaded, 16)
            sp.dma_start(sh_dn[:], a["sh_dn"]).then_inc(layer_loaded, 16)
            sp.wait_ge(normed, 16)
            sp.dma_start(x_dram.rearrange("(t p) d -> p t d", p=P), xres[:]).then_inc(x_stored, 16)
            sp.wait_ge(route_act, 2)
            sp.wait_ge(y_blank, 16 * -(-(NBLK - LEAST_GROUPS * NJ) // (NBLK // NJ)))
            for j in range(NJ):
                sp.sem_inc(y_stored[j], 16)

            def store_y(i, j):
                sp.wait_ge(down_copied, at(i, NJ, j + 1) + TILES)
                rows = y_dram[bass.ds((i * NJ + j) * P, P), :]
                sp.dma_start(rows, y_out[:, j, :]).then_inc(y_stored[j], 16)

            def load_w(i, j):
                e = sp.value_load(expert_row[0:1, bass.ds(i * NJ + j, 1)], min_val=0, max_val=E - 1)
                sp.dma_start(w_gv[:, j], a["w_gv"][bass.ds(e, 1)].rearrange("a p k n -> (a p) k n")).then_inc(w_loaded[j], 16)
                sp.dma_start(w_dn[:, j], a["w_dn"][bass.ds(e, 1)].rearrange("a p k n -> (a p) k n")).then_inc(w_loaded[j], 16)

            for j in range(NJ):
                load_w(0, j)
            used = used_groups(sp)
            with sp.Fori(1, used) as i:
                for j in range(NJ):
                    store_y(i - 1, j)
                    load_w(i, j)
            for j in range(NJ):
                store_y(used - 1, j)
            sp.wait_ge(normed, 24)
            for dst, src in ((l_wq, "l_wq"), (l_wkv, "l_wkv"), (l_wo, "l_wo"), (l_bq, "l_bq"), (head_mask, "head_mask")):
                sp.dma_start(dst[:], a[src]).then_inc(layer_loaded, 16)
            sp.dma_start(l_bkv[:], a["l_bkv"].to_broadcast([P, 2 * D])).then_inc(layer_loaded, 16)
            sp.dma_start(l_bo[:], a["l_bo"].to_broadcast([P, D])).then_inc(layer_loaded, 16)
            sp.wait_ge(normed, 32)
            for dst, src in ((x_wkv, "x_wkv"), (pos, "pos"), (x_wq, "x_wq"), (ident_bf, "ident_bf"), (x_wo, "x_wo"), (f_in, "f_in"), (f_out, "f_out")):
                sp.dma_start(dst[:], a[src]).then_inc(layer_loaded, 16)
            sp.dma_start(x_bo[:], a["x_bo"].to_broadcast([P, D])).then_inc(layer_loaded, 16)
            sp.wait_ge(normed, 48)
            sp.dma_start(out.rearrange("b (t p) d -> p (b t) d", p=P), xres[:]).then_inc(x_stored, 16)
            sp.wait_ge(x_stored, 32)

        @block.tensor
        def _(pe):
            mm = nc.tensor.matmul

            def project_qks(i, first):
                pe.wait_ge(qks_loaded, at(i, 16, 16))
                for n in range(6):
                    part, half = n // 2, n % 2
                    if n < 2:
                        if not first:
                            pe.wait_ge(gate_ready, at(i - 1, 8, 7 + n))
                    elif n < 4:
                        pe.wait_ge(qk_copied, at(i, 4, n - 1))
                    else:
                        pe.wait_ge(qk_copied, at(i, 4, n - 1))
                    for k in range(KD):
                        last = mm(bank(PJ + n % 2), w_qks[:, k, part * P:(part + 1) * P],
                                  xT[:, k, half * 512:(half + 1) * 512], start=(k == 0), stop=(k == KD - 1))
                    last.then_inc(proj_ready, 1)

            def step(i, last_pair):
                pe.wait_ge(qk_copied, at(i, 4, 4))
                for n in range(8):
                    b, h = n // 2, n % 2
                    if n >= 2:
                        pe.wait_ge(scores_masked, at(i, 8, n - 1))
                    r = slice(64 * h, 64 * h + 64)
                    c = b * T
                    mm(ps[:, AB + n % 2, 0:256], kT[r, c:c + P], qT[r, c:c + 256], start=True, stop=True)
                    mm(ps[:, AB + n % 2, 256:384], kT[r, c + P:c + 256], qT[r, c + P:c + 256],
                       start=True, stop=True).then_inc(scores_ready, 1)
                pe.wait_ge(eT_ready, at(i, 2, 2))
                pe.wait_ge(const_loaded, 48)
                pe.wait_ge(mixed_added, at(i, 4, 1))
                for n in range(2):
                    for t in range(4):
                        c = (4 * n + t) * P
                        last = nc.tensor.transpose(ps[:, X + n, t * P:(t + 1) * P], eT[:, c:c + P], ident[:])
                    last.then_inc(e_turned, 1)
                pe.wait_ge(lnz_ready, at(i, 1, 1))
                for n in range(2):
                    for t in range(4):
                        c = (4 * n + t) * P
                        last = nc.tensor.transpose(ps[:, Y + n, t * P:(t + 1) * P], zT[:, c:c + P], ident[:])
                    last.then_inc(z_turned, 1)
                pe.wait_ge(vg_loaded, at(i, 16, 16))

                def project_vg(t):
                    if t < 2:
                        pe.wait_ge(s_clipped, at(i, 2, t + 1))
                    else:
                        pe.wait_ge(gate_ready, at(i, 8, t - 1))
                    for k in range(KD):
                        last = mm(bank(PJ + t % 2), xT[:, k, t * P:(t + 1) * P], w_vg[:, k, :],
                                  start=(k == 0), stop=(k == KD - 1))
                    last.then_inc(proj_ready, 1)

                project_vg(0)
                project_vg(1)
                pe.wait_ge(e_copied, at(i, 2, 2))
                pe.wait_ge(scores_masked, at(i, 8, 8))
                for b in range(B):
                    for h in range(2):
                        n = 2 * b + h
                        m = slice(M * h, M * h + M)
                        o0 = ps[:, X + b // 2, (b % 2) * 256 + M * h:(b % 2) * 256 + M * h + M]
                        o1 = ps[:, X + b // 2, (b % 2) * 256 + P + M * h:(b % 2) * 256 + P + M * h + M]
                        mm(o0, aT[:, n, 0:P], e_tok[:, 2 * b, m], start=True, stop=True)
                        mm(o1, aT[:, n, P:256], e_tok[:, 2 * b, m], start=True, stop=False)
                        last = mm(o1, aT[:, n, 256:384], e_tok[:, 2 * b + 1, m], start=False, stop=True)
                last.then_inc(slots_ready, 1)
                for t in range(2, TILES):
                    project_vg(t)
                pe.wait_ge(w_ready, at(i, 1, 1))
                pe.wait_ge(zi_ready, at(i, 2, 2))
                for n in range(2):
                    for t in range(4):
                        r = 4 * n + t
                        last = nc.tensor.transpose(ps[:, Y + n, t * P:(t + 1) * P],
                                                   okn[:, 2 * r:2 * r + 2, :].rearrange("p a b -> p (a b)"), ident[:])
                    last.then_inc(w_turned, 1)
                def read(n):
                    b, h = n // 2, n % 2
                    if n % 4 == 0:
                        pe.wait_ge(wT_copied, at(i, 2, n // 4 + 1))
                    if n >= 2:
                        pe.wait_ge(read_masked, at(i, 8, n - 1))
                    r = slice(64 * h, 64 * h + 64)
                    c = b * T
                    mm(ps[:, AB + n % 2, 0:256], eT[r, c:c + P], wT[r, c:c + 256], start=True, stop=True)
                    mm(ps[:, AB + n % 2, 256:384], eT[r, c + P:c + 256], wT[r, c + P:c + 256],
                       start=True, stop=True).then_inc(read_ready, 1)

                def mix(n):
                    b, h = n // 2, n % 2
                    pe.wait_ge(read_masked, at(i, 8, n + 1))
                    vh = slice(DV * h, DV * h + DV)
                    o0 = ps[:, X + b, DV * h:DV * h + DV]
                    o1 = ps[:, X + b, 256 + DV * h:256 + DV * h + DV]
                    mm(o0, aT[:, n, 0:P], v[:, 2 * b, vh], start=True, stop=True)
                    mm(o1, aT[:, n, P:256], v[:, 2 * b, vh], start=True, stop=False)
                    last = mm(o1, aT[:, n, 256:384], v[:, 2 * b + 1, vh], start=False, stop=True)
                    if h == 1:
                        last.then_inc(o_ready, 1)

                read(0)
                for n in range(8):
                    if n < 7:
                        read(n + 1)
                    mix(n)
                if not last_pair:
                    project_qks(i + 1, False)
                pe.wait_ge(wo_loaded, at(i, 16, 16))

                def turn(b):
                    pe.wait_ge(o_gated, at(i, 4, b + 1))
                    if b >= 2:
                        pe.wait_ge(oT_copied, at(i, 4, b - 1))
                    for h in range(2):
                        for t in range(2):
                            last = nc.tensor.transpose(ps[:, AB + b % 2, (2 * h + t) * P:(2 * h + t + 1) * P],
                                                       on[:, 2 * (2 * b + t) + h, :], ident[:])
                    last.then_inc(o_turned, 1)

                def project_out(b):
                    pe.wait_ge(oT_copied, at(i, 4, b + 1))
                    if b >= 2:
                        pe.wait_ge(mixed_added, at(i, 4, b))
                    for t in range(2):
                        for h in range(2):
                            c = (2 * b + t) * P
                            last = mm(ps[:, X + b % 2, 256 * t:256 * t + 256], oT[:, h, c:c + P], w_o[:, h, :],
                                      start=(h == 0), stop=(h == 1))
                    last.then_inc(mixed_ready, 1)

                turn(0)
                for b in range(B):
                    if b < 3:
                        turn(b + 1)
                    project_out(b)

            pe.wait_ge(x_loaded, 16)
            project_qks(0, True)
            pe.wait_ge(scan_consts, 96)
            for e in range(ET):
                for half in range(2):
                    mm(bank(X + 2 * e + half), w_in[:, e * P:(e + 1) * P], ctxT[:, half * 512:(half + 1) * 512],
                       start=True, stop=True).then_inc(scan_mm, 1)
            pe.wait_ge(u_ready, 2)
            for half in range(2):
                for e in range(ET):
                    last = mm(ps[0:XD, X + half, :], xp_w[:, e, :], u[:, e, half * 512:(half + 1) * 512],
                              start=(e == 0), stop=(e == ET - 1))
                last.then_inc(scan_mm, 1)
            pe.wait_ge(x_dbl_copied, 2)
            for e in range(ET):
                for half in range(2):
                    mm(bank(X + 2 * e + half), dt_w[:, e * P:(e + 1) * P], x_dbl[0:DR, half * 512:(half + 1) * 512],
                       start=True, stop=True).then_inc(scan_mm, 1)
            pe.wait_ge(scan_act, 10)
            with pe.Fori(0, PAIRS - 1) as i:
                step(i, False)
            step(PAIRS - 1, True)

            def turn_x(n):
                for b in range(B):
                    pe.wait_ge(normed, 8 * n + 2 * b + 2)
                    for k in range(KD):
                        for t in range(2):
                            last = nc.tensor.transpose(ps[:, b, k * 256 + t * P:k * 256 + (t + 1) * P],
                                                       xres[:, 2 * b + t, k * P:(k + 1) * P], ident[:])
                    last.then_inc(x_turned, 1)

            for b in range(B):
                pe.wait_ge(y_gated, b + 1)
                for t in range(2):
                    for e in range(ET):
                        last = nc.tensor.transpose(ps[:, X + b, t * 256 + e * P:t * 256 + (e + 1) * P],
                                                   v[:, 2 * b + e, t * P:(t + 1) * P], ident[:])
                last.then_inc(y_turned, 1)
            turn_x(1)
            pe.wait_ge(moe_consts, 64)
            for t in range(TILES):
                if t % 2 == 0:
                    pe.wait_ge(xT_copied, t // 2 + 1)
                if t == 0:
                    pe.wait_ge(y_residual, 1)
                for k in range(KD):
                    last = mm(ps[:, X, t * E:(t + 1) * E], xT[:, k, t * P:(t + 1) * P], w_router[:, k, :],
                              start=(k == 0), stop=(k == KD - 1))
            last.then_inc(route_mm, 1)
            pe.wait_ge(route_vec, 2)
            pe.wait_ge(pool_set, 3)
            for t in range(TILES):
                for q in range(t + 1):
                    last = mm(ps[:, X + 1, t * E:(t + 1) * E], ones_bf[:] if q < t else tri_bf[:], chosen_bf[:, q, :],
                              start=(q == 0), stop=(q == t))
            for t in range(TILES):
                last = mm(ps[:, Y, 0:E], ones_bf[:], chosen_bf[:, t, :], start=(t == 0), stop=(t == TILES - 1))
            last.then_inc(route_mm, 1)
            pe.wait_ge(route_vec, 3)
            nc.tensor.transpose(ps[0:1, Y, 0:P], blk_expert[:], ident[:]).then_inc(route_mm, 1)
            for n in range(TILES * TOPK):
                pe.wait_ge(hot_ready, 2 * n + 2)
                mm(ps[:, Y + 1, 0:NBLK], row_hot[:, n % 4, :], blk_hot[:, n % 4, :], start=(n == 0),
                   stop=(n == TILES * TOPK - 1)).then_inc(hot_used, 1)

            def gate_up(n, j, x_of, w):
                for k in range(KD):
                    last = mm(ps[:, 2 * j + 1, 0:2 * F], x_of(k), w[:, k, :], start=(k == 0), stop=(k == KD - 1))
                last.then_inc(gv_ready, 1)

            def turn_hid(n, j):
                pe.wait_ge(hid_ready, n + 1)
                for f in range(2):
                    last = nc.tensor.transpose(ps[0:FH, 2 * j, f * P:(f + 1) * P], hid[:, j, f * FH:(f + 1) * FH], ident[:])
                last.then_inc(hid_turned, 1)

            def down(n, j, w):
                pe.wait_ge(hidT_copied, n + 1)
                for f in range(2):
                    last = mm(ps[:, 2 * j, 256:512], hidT[:, j, f * P:(f + 1) * P], w[:, f, :], start=(f == 0),
                              stop=(f == 1))
                last.then_inc(down_ready, 1)

            pe.wait_ge(layer_loaded, 32)
            pe.wait_ge(tok_known, 1)
            for r in range(TILES // NJ):
                for j in range(NJ):
                    n = r * NJ + j
                    if r:
                        pe.wait_ge(down_copied, n - NJ + 1)
                    gate_up(n, j, lambda k: xT[:, k, n * P:(n + 1) * P], sh_gv)
                for j in range(NJ):
                    turn_hid(r * NJ + j, j)
                for j in range(NJ):
                    down(r * NJ + j, j, sh_dn)
            with pe.Fori(0, used_groups(pe)) as i:
                for j in range(NJ):
                    n = i * NJ + j
                    pe.wait_ge(gathered[j], at(i, 16, 16))
                    pe.wait_ge(down_copied, n + TILES - NJ + 1)
                    for k in range(KD):
                        last = nc.tensor.transpose(ps[:, 2 * j, k * P:(k + 1) * P], xg[:, j, k * P:(k + 1) * P], ident[:])
                    last.then_inc(xg_turned, 1)
                for j in range(NJ):
                    n = i * NJ + j
                    pe.wait_ge(xgT_copied, n + 1)
                    pe.wait_ge(w_loaded[j], at(i, 32, 32))
                    gate_up(n + TILES, j, lambda k: xgT[:, j, k * P:(k + 1) * P], w_gv[:, j])
                for j in range(NJ):
                    turn_hid(i * NJ + j + TILES, j)
                for j in range(NJ):
                    down(i * NJ + j + TILES, j, w_dn[:, j])

            def copy_x_wait(n):
                pe.wait_ge(xT_copied, 4 * TURN[f"x{n}"] + 4)

            turn_x(2)
            copy_x_wait(2)
            pe.wait_ge(layer_loaded, 144)
            for n in range(4):
                m, half = n // 2, n % 2
                for k in range(KD):
                    last = mm(bank(4 + n), l_wq[:, k, m * P:(m + 1) * P], xT[:, k, half * 512:(half + 1) * 512],
                              start=(k == 0), stop=(k == KD - 1))
                last.then_inc(lq_ready, 1)
            for t in range(TILES):
                if t >= 4:
                    pe.wait_ge(lkv_added, 2 * (t - 3))
                for k in range(KD):
                    last = mm(bank(t % 4), xT[:, k, t * P:(t + 1) * P], l_wkv[:, k, :], start=(k == 0), stop=(k == KD - 1))
                last.then_inc(lkv_ready, 1)
            pe.wait_ge(elu_split, 8)
            for n in range(B * KD):
                b, m = n // KD, n % KD
                pe.wait_ge(elu_done, 4 + 2 * b + 2)
                if n >= 4:
                    pe.wait_ge(kv_masked, n - 3)
                c = slice(m * P, (m + 1) * P)
                for t in range(2):
                    mm(ps[:, 4 + n % 4, 0:P], lk[:, 2 * b + t, c], lv[:, 2 * b + t, c], start=(t == 0), stop=(t == 1))
                for t in range(2):
                    last = mm(ps[:, 4 + n % 4, P:KVW], lk[:, 2 * b + t, c], ones[:, 0:LB], start=(t == 0), stop=(t == 1))
                last.then_inc(kv_ready, 1)
            pe.wait_ge(elu_done, 4)
            for t in range(TILES):
                b = t // 2
                pe.wait_ge(kv_masked, KD * (b + 1))
                if t < 4:
                    pe.wait_ge(lkv_added, 2 * TILES)
                else:
                    pe.wait_ge(att_ready, t - 3)
                for m in range(KD):
                    last = mm(ps[:, t % 4, m * KVW:(m + 1) * KVW], lqT[:, m, t * P:(t + 1) * P], kv[:, KD * b + m, :],
                              start=True, stop=True)
                last.then_inc(num_ready, 1)

            def turn_att(src):
                for b in range(B):
                    pe.wait_ge(att_ready, 2 * b + 2)
                    for k in range(KD):
                        for t in range(2):
                            last = nc.tensor.transpose(ps[:, 4 + b, k * 256 + t * P:k * 256 + (t + 1) * P],
                                                       src[:, 2 * b + t, k * P:(k + 1) * P], ident[:])
                    last.then_inc(x_turned, 1)

            def project_att(n, w):
                for t in range(TILES):
                    if n == 0:
                        pe.wait_ge(xT_copied, 4 * TURN["att0"] + t // 2 + 1)
                    if t >= 4:
                        pe.wait_ge(attended, 8 * n + t - 3)
                    for k in range(KD):
                        last = mm(ps[:, t % 4, 0:D], xT[:, k, t * P:(t + 1) * P], w[:, k, :], start=(k == 0),
                                  stop=(k == KD - 1))
                    last.then_inc(proj_out_ready, 1)

            pe.wait_ge(kv_masked, B * KD)
            turn_att(l_out)
            project_att(0, l_wo)

            pe.wait_ge(layer_loaded, 272)
            pe.wait_ge(attended, 8)
            for t in range(TILES):
                if t >= 4:
                    pe.wait_ge(turns_done, 4 * (t - 3))
                mm(bank(t % 4), ctxT[:, t * P:(t + 1) * P], x_wkv[:], start=True, stop=True).then_inc(xkv_ready, 1)
            pe.wait_ge(turns_done, 4 * TILES)
            turn_x(3)
            copy_x_wait(3)
            for b in range(B):
                for t in range(2):
                    for k in range(KD):
                        c = (2 * b + t) * P
                        last = mm(ps[:, 4 + b, t * 256:(t + 1) * 256], xT[:, k, c:c + P], x_wq[:, k, :], start=(k == 0),
                                  stop=(k == KD - 1))
                last.then_inc(xq_ready, 1)
            pe.wait_ge(stacked, 12)
            pe.wait_ge(pool_set, 9)
            pe.wait_ge(turns_done, 48)

            def turn_heads(n, m):
                for bank_n, src, copied in ((0, q_st, qsT_copied), (1, k_st, ksT_copied)):
                    pe.wait_ge(copied, at(m, 1, 1))
                    for t in range(TILES):
                        last = nc.tensor.transpose(bank(bank_n).bitcast(BF16)[:, t * P:(t + 1) * P],
                                                   src[:, t, bass.ds(n * 2, 2), :].rearrange("p a b -> p (a b)"),
                                                   ident_bf[:])
                    last.then_inc(heads_turned, 1)

            def rows(n, j):
                pe.wait_ge(qsT_copied, at(n, 1, 2))
                pe.wait_ge(ksT_copied, at(n, 1, 2))
                for b in range(B):
                    pe.wait_ge(rows_maxed, at(n, 4, b + 1))
                    for h in range(2):
                        r = slice(SLOT * h, SLOT * h + SLOT)
                        for q in range(2):
                            c = b * T + q * P
                            last = mm(ps[:, 4 + 2 * (b % 2) + h, q * 256:(q + 1) * 256], qsT[r, j, c:c + P],
                                      ksT[r, j, b * T:(b + 1) * T], start=True, stop=True)
                    last.then_inc(rows_ready, 1)

            def columns(g, it):
                b, jj = it // GP, it % GP
                if b == 0:
                    pe.wait_ge(qsT_copied, at(g, GP, jj + 2) + XPAIRS)
                    pe.wait_ge(ksT_copied, at(g, GP, jj + 2) + XPAIRS)
                pe.wait_ge(prob_ready, at(g, ITEMS, it + 1))
                for h in range(2):
                    r = slice(SLOT * h, SLOT * h + SLOT)
                    for k in range(2):
                        last = mm(ps[:, 4 + 2 * (it % 2) + h, k * 256:(k + 1) * 256],
                                  ksT[r, jj, b * T + k * P:b * T + (k + 1) * P], qsT[r, jj, b * T:(b + 1) * T],
                                  start=True, stop=True)
                last.then_inc(cols_ready, 1)

            def values(g, it):
                b, jj = it // GP, it % GP
                pe.wait_ge(prob_ready, at(g, ITEMS, it + 3))
                pe.wait_ge(v_placed, at(g, ITEMS, it + 1))
                if jj == 0:
                    pe.wait_ge(acc_free, at(g, B, b + 1))
                for h in range(2):
                    hh = 2 * jj + h
                    for k in range(2):
                        last = mm(ps[:, 2 + b % 2, 0:256],
                                  v_win[:, it % 2, k, h, GAP - XD_H * hh:GAP - XD_H * hh + P],
                                  probT[:, 2 * (it % 2) + h, k, :], start=(hh == 0 and k == 0),
                                  stop=(hh == GH - 1 and k == 1))
                last.then_inc(pv_ready, 1)

            def attend(g, last_group):
                for it in range(ITEMS):
                    if it < ITEMS - 1:
                        columns(g, it + 1)
                    elif not last_group:
                        columns(g + 1, 0)
                    values(g, it)
                    if it // GP == B - 1 and not last_group:
                        turn_heads((g + 1) * GP + it % GP, (g + 1) * GP + it % GP + XPAIRS)

            turn_heads(0, 0)
            with pe.Fori(0, XPAIRS // 2 - 1) as i:
                for j in range(2):
                    turn_heads(i * 2 + (j + 1), i * 2 + (j + 1))
                    rows(i * 2 + j, j)
            turn_heads(XPAIRS - 1, XPAIRS - 1)
            rows(XPAIRS - 2, 0)
            rows(XPAIRS - 1, 1)
            pe.wait_ge(shifted, 1)
            for jj in range(GP):
                turn_heads(jj, XPAIRS + jj)
            columns(0, 0)
            with pe.Fori(0, XGROUPS - 1) as g:
                attend(g, False)
            attend(XGROUPS - 1, True)
            pe.wait_ge(acc_free, XGROUPS * B + 2)
            project_att(1, x_wo)

            pe.wait_ge(ternary, 2)
            mm(ps[:, 7, 0:2], ones[:, 0:P], f_sum[:], start=True, stop=True).then_inc(f_total, 1)
            turn_x(4)
            pe.wait_ge(ternary, 4)
            pe.wait_ge(part_cast, 9)

            def up(t):
                if t >= 2:
                    pe.wait_ge(h_relu, t - 1)
                for n in range(2):
                    for j in range(3):
                        for k in range(KD):
                            last = mm(bank(2 * (t % 2) + n), x_part[:, j, k, t * P:(t + 1) * P],
                                      q_in[:, k, n * 512:(n + 1) * 512], start=(j == 0 and k == 0),
                                      stop=(j == 2 and k == KD - 1))
                last.then_inc(h_ready, 1)

            def turn_h(t):
                pe.wait_ge(hq_ready, t + 1)
                if t >= 2:
                    pe.wait_ge(hqT_copied, t - 1)
                for k in range(KH):
                    last = nc.tensor.transpose(ps[:, 4 + t % 2, :].bitcast(BF16)[:, k * P:(k + 1) * P],
                                               hid_q[:, t % 2, k * P:(k + 1) * P], ident_bf[:])
                last.then_inc(hq_turned, 1)

            def down_f(t):
                pe.wait_ge(hqT_copied, t + 1)
                if t >= 2:
                    pe.wait_ge(f_added, t - 1)
                for k in range(KH):
                    last = mm(ps[:, 6 + t % 2, 0:D], hid_q[:, 2 + t % 2, k * P:(k + 1) * P], q_out[:, k, :],
                              start=(k == 0), stop=(k == KH - 1))
                last.then_inc(f_out_ready, 1)

            up(0)
            for t in range(TILES):
                if t < TILES - 1:
                    up(t + 1)
                turn_h(t)
                down_f(t)

        @block.gpsimd
        def _(pool):
            nc.gpsimd.memset(x_pad[:, :, :, 0:DC - 1], 0.0).then_inc(pool_set, 1)
            nc.gpsimd.memset(blank[:], 0.0).then_inc(pool_set, 1)
            G = nc.gpsimd
            pool.sem_inc(y_added, 2)
            pool.wait_ge(u_ready, 4)

            def steps(i):
                def drive_of(n):
                    j, e = n // 2, n % 2
                    pool.wait_ge(bc_loaded[j], at(i, 32, 32))
                    pool.wait_ge(scanned, at(i, 4, n + 1))
                    G.tensor_tensor(drive[:, n % 2], du[:, e], b_row[:, j], ALU.mult).then_inc(drive_ready, 1)

                def read_of(n):
                    j, e = n // 2, n % 2
                    pool.wait_ge(scanned, at(i, 4, n + 3))
                    G.tensor_tensor(state[:, n % 2], state[:, n % 2], c_row[:, j], ALU.mult).then_inc(read_out, 1)
                    pool.wait_ge(read_out, at(i, 4, n + 1))
                    pool.wait_ge(y_added, at(i, 4, n + 1))
                    G.tensor_tensor(y[:, e], y[:, e], state[:, n % 2], ALU.add).then_inc(y_added, 1)

                drive_of(0)
                drive_of(1)
                read_of(0)
                drive_of(2)
                read_of(1)
                drive_of(3)
                read_of(2)
                read_of(3)

            steps(0)
            with pool.Fori(1, PAIRS) as i:
                steps(i)
            pool.wait_ge(y_turned, 4)
            G.memset(ones_bf[:], 1.0).then_inc(pool_set, 1)
            pool.wait_ge(tok_known, 1)
            pool.wait_ge(x_stored, 16)

            def gather(i, j, first):
                if not first:
                    pool.wait_ge(xg_turned, at(i - 1, NJ, j + 1))
                    pool.wait_ge(gathered[j], at(i, 16, 0))
                G.tensor_copy(tok_cur[:, j:j + 1], tok_of[:, bass.ds(i * NJ + j, 1)]).then_inc(tok_picked, 1)
                pool.wait_ge(tok_picked, at(i, NJ, j + 1))
                pool.sem_inc(gather_due, 1)
                G.indirect_dma_start(xg[:, j, :], None, x_dram, bass.IndirectOffsetOnAxis(ap=tok_cur[:, j:j + 1], axis=0)
                                     ).then_inc(gathered[j], 16)

            for j in range(NJ):
                gather(0, j, True)
            used = used_groups(pool)
            with pool.Fori(1, used) as i:
                for j in range(NJ):
                    gather(i, j, False)
            for j in range(NJ):
                pool.wait_ge(y_stored[j], used * 16 + 16)
            pool.sem_inc(gather_due, 1)
            for n in range(TILES * TOPK):
                if n >= 8:
                    pool.wait_ge(combined, n - 7)
                G.indirect_dma_start(yg[:, n % 8, :], None, y_dram,
                                     bass.IndirectOffsetOnAxis(ap=slot_idx[:, n // TOPK, n % TOPK:n % TOPK + 1], axis=0)
                                     ).then_inc(back[n % 8], 16)
            pool.wait_ge(normed, 32)
            G.memset(q_st[:, :, :, SHIFT:SLOT], 0.0).then_inc(pool_set, 1)
            G.memset(k_st[:, :, :, SHIFT:SHIFT + 3], 1.0).then_inc(pool_set, 1)
            G.memset(k_st[:, :, :, SHIFT + 3:SLOT], 0.0).then_inc(pool_set, 1)
            G.memset(v_win[:], 0.0).then_inc(pool_set, 1)
            pool.wait_ge(pool_set, 7)
            for j in range(2):
                G.memset(v_win[:, j, :, :, 2 * GAP + XD_H:2 * GAP + 2 * XD_H], 1.0).then_inc(pool_set, 1)
            pool.wait_ge(xv_copied, TILES)
            pool.wait_ge(pool_set, 9)

            def place_v(g, it):
                b = it // GP
                pool.wait_ge(pv_ready, at(g, ITEMS, it + 1))
                G.tensor_copy(v_win[:, it % 2, :, :, GAP:GAP + XD_H],
                              x_v[:, 2 * b:2 * b + 2, bass.ds(g * (GP * 2 * XD_H) + it % GP * 2 * XD_H, 2 * XD_H)
                                  ].rearrange("p t (h d) -> p t h d", h=2)).then_inc(v_placed, 1)

            with pool.Fori(0, XGROUPS) as g:
                for it in range(ITEMS):
                    place_v(g, it)

        @block.scalar
        def _(act):
            def f(out, in_, func, **kw):
                return nc.scalar.activation(out, in_, func, **kw)

            act.wait_ge(const_loaded, 48)
            nc.scalar.mul(gn_half[:], gn_half[:], 0.5).then_inc(act_step, 1)

            def copy_qk(i, pieces):
                for n in pieces:
                    act.wait_ge(proj_ready, at(i, 14, n + 1))
                    dst = (qT, kT)[n // 2]
                    f(dst[:, (n % 2) * 512:(n % 2) * 512 + 512], bank(PJ + n % 2), ACT.Copy).then_inc(qk_copied, 1)

            def exp_slots(i):
                for n in range(2):
                    act.wait_ge(s_clipped, at(i, 2, n + 1))
                    f(eT[:, n * 512:(n + 1) * 512], sT[:, n * 512:(n + 1) * 512], ACT.Exp).then_inc(eT_ready, 1)

            def log_sums(i):
                act.wait_ge(zT_ready, at(i, 1, 1))
                f(zT[:], zT[:], ACT.Ln).then_inc(lnz_ready, 1)

            def rms(i):
                act.wait_ge(squares_read, at(i, 4, 4))
                f(lnv[:], ss[:], ACT.Ln, scale=1.0 / DV, bias=eps_col[:]).then_inc(act_step, 1)
                act.wait_ge(act_step, at(i, 1, 2))
                f(rstd[:], lnv[:], ACT.Exp, scale=-0.5).then_inc(rstd_ready, 1)

            def decay_of(i, n):
                j, e = n // 2, n % 2
                act.wait_ge(a_picked, at(i, 1, 1))
                act.wait_ge(scanned, at(i, 4, n + 1))
                f(decay[:, n % 2], delta[:, e], ACT.Exp, scale=a_cur[:, e, j:j + 1]).then_inc(decay_ready, 1)

            def step(i, last_pair):
                for n in range(2):
                    act.wait_ge(e_turned, at(i, 2, n + 1))
                    f(e_tok[:, 4 * n:4 * n + 4, :].rearrange("p a b -> p (a b)"), bank(X + n),
                      ACT.Copy).then_inc(e_copied, 1)
                for n in range(2):
                    act.wait_ge(z_turned, at(i, 2, n + 1))
                    f(zi[:, 4 * n:4 * n + 4, :].rearrange("p a b -> p (a b)"), bank(Y + n), ACT.Exp,
                      scale=-1.0).then_inc(zi_ready, 1)

                def values_and_gate(t):
                    act.wait_ge(proj_ready, at(i, 14, 7 + t))
                    f(v[:, t, :], bank(PJ + t % 2, 0, 256), ACT.Copy)
                    f(th[:, t, :], bank(PJ + t % 2, 256, 512), ACT.Tanh, scale=0.5).then_inc(tanh_ready, 1)

                decay_of(i, 0)
                for t in range(4):
                    values_and_gate(t)
                act.wait_ge(slots_shifted, at(i, 1, 1))
                f(pe_[:], okn[:], ACT.Exp, scale=DK ** -0.5).then_inc(slots_exp, 1)
                for t in range(4, 6):
                    values_and_gate(t)
                decay_of(i, 1)
                for t in range(6, TILES):
                    values_and_gate(t)
                for n in range(2):
                    act.wait_ge(w_turned, at(i, 2, n + 1))
                    f(wT[:, n * 512:(n + 1) * 512], bank(Y + n), ACT.Copy).then_inc(wT_copied, 1)
                decay_of(i, 2)
                for b in range(B):
                    act.wait_ge(o_ready, at(i, 4, b + 1))
                    if b >= 2:
                        act.wait_ge(squares_read, at(i, 4, b - 1))
                    f(sq[:, b % 2].rearrange("p a b -> p (a b)"), bank(X + b), ACT.Square).then_inc(squares_ready, 1)
                if not last_pair:
                    copy_qk(i + 1, range(2))
                nc.scalar.preload_act_table_set("natural_log_exp_and_others")
                rms(i)
                if not last_pair:
                    copy_qk(i + 1, range(2, 4))
                decay_of(i, 3)
                if not last_pair:
                    exp_slots(i + 1)
                for b in range(B):
                    act.wait_ge(o_turned, at(i, 4, b + 1))
                    f(oT[:, :, 2 * b * P:(2 * b + 2) * P], bank(AB + b % 2).rearrange("p (h t) -> p h t", h=2), ACT.Copy,
                      scale=gn_half[:]).then_inc(oT_copied, 1)
                if not last_pair:
                    log_sums(i + 1)

            act.wait_ge(act_step, 1)
            act.wait_ge(const_set, 2)
            nc.scalar.preload_act_table_set("natural_log_exp_and_others")
            copy_qk(0, range(4))
            exp_slots(0)
            log_sums(0)
            act.wait_ge(scan_consts, 96)
            f(a_neg[:], a_neg[:], ACT.Exp).then_inc(a_ready, 1)
            act.wait_ge(a_ready, 1)
            nc.scalar.mul(a_neg[:], a_neg[:], -1.0).then_inc(a_ready, 1)
            for e in range(ET):
                for half in range(2):
                    act.wait_ge(scan_mm, 2 * e + half + 1)
                    f(x_pad[:, e, 2 * half:2 * half + 2, DC - 1:DC - 1 + T],
                      bank(X + 2 * e + half).rearrange("p (b t) -> p b t", b=2), ACT.Copy).then_inc(inner_copied, 1)
            for e in range(ET):
                act.wait_ge(conv_step, 4 * e + 4)
                f(aux[:, e], conv[:, e], ACT.Tanh, scale=0.5).then_inc(scan_act, 1)
            for half in range(2):
                act.wait_ge(scan_mm, 4 + half + 1)
                f(x_dbl[:, half * 512:(half + 1) * 512], ps[0:XD, X + half, :], ACT.Copy).then_inc(x_dbl_copied, 1)
            act.wait_ge(u_ready, 2)
            for e in range(ET):
                for half in range(2):
                    c = slice(half * 512, (half + 1) * 512)
                    act.wait_ge(scan_mm, 6 + 2 * e + half + 1)
                    f(delta[:, e, c], bank(X + 2 * e + half), ACT.Relu, bias=s_cols[:, e, DC + 1:DC + 2]).then_inc(scan_act, 1)
                    f(conv[:, e, c], bank(X + 2 * e + half), ACT.Abs, bias=s_cols[:, e, DC + 1:DC + 2]).then_inc(scan_act, 1)
            act.wait_ge(scan_act, 10)
            f(conv[:], conv[:], ACT.Exp, scale=-1.0).then_inc(scan_act, 1)
            nc.scalar.preload_act_table_set("natural_log_exp_and_others")
            act.wait_ge(softplus_step, 1)
            f(aux2[:], aux[:], ACT.Ln).then_inc(scan_act, 1)
            act.wait_ge(u_ready, 4)
            with act.Fori(0, PAIRS - 1) as i:
                step(i, False)
            step(PAIRS - 1, True)

            def norm_scale(n):
                nc.scalar.preload_act_table_set("natural_log_exp_and_others")
                act.wait_ge(ln_moments, n + 1)
                f(ln_var[:], moments[:, :, 1], ACT.Ln, bias=eps_col[:]).then_inc(ln_scale, 1)
                act.wait_ge(ln_scale, 2 * n + 1)
                f(ln_rstd[:], ln_var[:], ACT.Exp, scale=-0.5).then_inc(ln_scale, 1)

            def copy_xT(n):
                for b in range(B):
                    act.wait_ge(x_turned, 4 * TURN[f"x{n}"] + b + 1)
                    f(xT[:, :, b * 256:(b + 1) * 256], bank(b).rearrange("p (k t) -> p k t", k=KD),
                      ACT.Copy).then_inc(xT_copied, 1)

            norm_scale(0)
            act.wait_ge(normed, 8)
            f(th[:], xres[:], ACT.Tanh, scale=0.5).then_inc(tanh_ready, 1)
            norm_scale(1)
            copy_xT(1)
            act.wait_ge(route_vec, 1)
            f(score[:, :, 0:E], score[:, :, 0:E], ACT.Exp).then_inc(route_act, 1)
            act.wait_ge(route_mm, 3)
            f(expert_row[:], ps[0:1, Y, 0:P], ACT.Copy).then_inc(route_act, 1)

            def g_tanh_of(n, j):
                act.wait_ge(gv_ready, n + 1)
                f(g_th[:, j, :], ps[:, 2 * j + 1, 0:F], ACT.Tanh, scale=0.5).then_inc(g_tanh, 1)

            def hidT_of(n, j):
                act.wait_ge(hid_turned, n + 1)
                f(hidT[:, j, :], ps[0:FH, 2 * j, 0:2 * P], ACT.Copy).then_inc(hidT_copied, 1)

            for r in range(TILES // NJ):
                for j in range(NJ):
                    g_tanh_of(r * NJ + j, j)
                for j in range(NJ):
                    hidT_of(r * NJ + j, j)
            with act.Fori(0, used_groups(act)) as i:
                for j in range(NJ):
                    act.wait_ge(xg_turned, at(i, NJ, j + 1))
                    f(xgT[:, j, :], ps[:, 2 * j, 0:KD * P], ACT.Copy).then_inc(xgT_copied, 1)
                for j in range(NJ):
                    g_tanh_of(i * NJ + j + TILES, j)
                for j in range(NJ):
                    hidT_of(i * NJ + j + TILES, j)

            def hqT_of(t):
                act.wait_ge(hq_turned, t + 1)
                if t >= 2:
                    act.wait_ge(f_out_ready, t - 1)
                f(hid_q[:, 2 + t % 2], ps[:, 4 + t % 2, :].bitcast(BF16), ACT.Copy).then_inc(hqT_copied, 1)

            norm_scale(2)
            copy_xT(2)
            for n in range(4):
                act.wait_ge(elu_split, 2 * n + 2)
                f(lq_low[:, n % 2, :], lq_low[:, n % 2, :], ACT.Exp).then_inc(elu_exp, 1)
            for t in range(TILES):
                act.wait_ge(elu_split, 8 + t + 1)
                f(lk_low[:, t % 2, :], lk_low[:, t % 2, :], ACT.Exp).then_inc(elu_exp, 1)

            def copy_attT(n):
                for b in range(B):
                    act.wait_ge(x_turned, 4 * TURN[f"att{n}"] + b + 1)
                    f(xT[:, :, b * 256:(b + 1) * 256], bank(4 + b).rearrange("p (k t) -> p k t", k=KD),
                      ACT.Copy).then_inc(xT_copied, 1)

            copy_attT(0)
            norm_scale(3)
            act.wait_ge(angle, 6)
            f(cos_sin[:], ang[:], ACT.Sin).then_inc(cos_sin_ready, 1)
            for t in range(TILES):
                act.wait_ge(xkv_ready, t + 1)
                f(x_v[:, t, :], bank(t % 4, 256, 512),
                  ACT.Copy).then_inc(xv_copied, 1)
            copy_xT(3)

            def cast_parts(n, src, count):
                act.wait_ge(rotated, count)
                for j in range(3):
                    if j:
                        act.wait_ge(part_rest, 2 * n + j)
                    elif n:
                        act.wait_ge(stacked, 6)
                    f(part[:, j], src[:], ACT.Copy).then_inc(part_cast, 1)

            cast_parts(0, k_rot, 2 * TILES)
            cast_parts(1, q_rot, 2 * TILES + 2 * B)
            act.sem_inc(qsT_copied, 1)
            act.sem_inc(ksT_copied, 1)
            act.sem_inc(prob_ready, 2)
            act.sem_inc(pv_ready, 2)

            def copy_q(m, j):
                act.wait_ge(heads_turned, at(m, 2, 1))
                f(qsT[:, j], bank(0).bitcast(BF16), ACT.Copy).then_inc(qsT_copied, 1)

            with act.Fori(0, XPAIRS // 2) as i:
                for j in range(2):
                    copy_q(i * 2 + j, j)
                    act.wait_ge(heads_turned, at(i * 2 + j, 2, 2))
                    f(ksT[:, j], bank(1).bitcast(BF16), ACT.Copy).then_inc(ksT_copied, 1)

            def probs(g, it):
                act.wait_ge(cols_ready, at(g, ITEMS, it + 1))
                f(probT[:, 2 * (it % 2):2 * (it % 2) + 2].rearrange("p a k n -> p (a k n)"), pair(4 + 2 * (it % 2)),
                  ACT.Exp, scale=XD_H ** -0.5).then_inc(prob_ready, 1)

            for jj in range(GP):
                copy_q(XPAIRS + jj, jj)
            with act.Fori(0, XGROUPS - 1) as g:
                for it in range(ITEMS):
                    probs(g, it)
                    if it > ITEMS - GP:
                        copy_q((g + 1) * GP + it - (ITEMS - GP + 1) + XPAIRS, it - (ITEMS - GP + 1))
                copy_q((g + 1) * GP + GP - 1 + XPAIRS, GP - 1)
            for it in range(ITEMS):
                probs(XGROUPS - 1, it)
            norm_scale(4)
            copy_xT(4)
            act.wait_ge(xT_copied, 4 * TURN["x4"] + 4)
            for j in range(3):
                if j:
                    act.wait_ge(part_rest, 4 + j)
                f(x_part[:, j], xT[:], ACT.Copy).then_inc(part_cast, 1)
            for t in range(TILES):
                act.wait_ge(h_ready, t + 1)
                if t >= 2:
                    act.wait_ge(hq_ready, t - 1)
                for n in range(2):
                    last = f(hid_f[:, t % 2, n * 512:(n + 1) * 512], bank(2 * (t % 2) + n), ACT.Relu, scale=f_scale[:, 0:1])
                last.then_inc(h_relu, 1)
                act.wait_ge(h_relu, t + 1)
                f(hid_f[:, t % 2], hid_f[:, t % 2], ACT.Square).then_inc(h_square, 1)
                if t:
                    hqT_of(t - 1)
            hqT_of(TILES - 1)
            norm_scale(5)

        @block.vector
        def _(dve):
            V = nc.vector
            V.memset(ones[:], 1.0).then_inc(const_set, 1)
            V.memset(eps_col[:], LN_EPS).then_inc(const_set, 1)
            dve.wait_ge(const_set, 2)
            CHAIN = 5
            dve.sem_inc(scanned, 2)
            dve.sem_inc(mixed_added, 1)
            dve.sem_inc(acc_free, 2)
            dve.sem_inc(rows_maxed, 2)
            steps = [0]

            def then(ins):
                steps[0] += 1
                ins.then_inc(chain, 1)
                dve.wait_ge(chain, steps[0])

            def head(i):
                for n in range(2):
                    dve.wait_ge(proj_ready, at(i, 14, 5 + n))
                    V.tensor_scalar(sT[:, n * 512:(n + 1) * 512], bank(PJ + n % 2), CLAMP, -CLAMP,
                                    ALU.min, ALU.max).then_inc(s_clipped, 1)
                dve.wait_ge(eT_ready, at(i, 2, 2))
                for b in range(B):
                    last = V.tensor_tensor_scan(zT[:, b * T:(b + 1) * T], ones[:], eT[:, b * T:(b + 1) * T], 0.0,
                                                ALU.mult, ALU.add)
                last.then_inc(zT_ready, 1)

            def scan(i, n):
                j, e = n // 2, n % 2
                dve.wait_ge(decay_ready, at(i, 4, n + 1))
                dve.wait_ge(drive_ready, at(i, 4, n + 1))
                dve.wait_ge(y_added, at(i, 4, n + 1))
                for b in range(B):
                    c = slice(b * T, (b + 1) * T)
                    last = V.tensor_tensor_scan(state[:, n % 2, c], decay[:, n % 2, c], drive[:, n % 2, c], 0.0,
                                                ALU.mult, ALU.add)
                last.then_inc(scanned, 1)

            def step(i, last_pair):
                for n in range(8):
                    dve.wait_ge(scores_ready, at(i, 8, n + 1))
                    V.tensor_tensor(aT[:, n, :], ps[:, AB + n % 2, 0:384], tri[:], ALU.mult).then_inc(scores_masked, 1)

                def gate(t):
                    dve.wait_ge(tanh_ready, at(i, 8, t + 1))
                    V.scalar_tensor_tensor(out=th[:, t, :], in0=th[:, t, :], scalar=1.0,
                                           in1=bank(PJ + t % 2, 256, 512), op0=ALU.add,
                                           op1=ALU.mult).then_inc(gate_ready, 1)

                gate(0)
                gate(1)
                dve.wait_ge(slots_ready, at(i, 1, 1))
                dve.wait_ge(zi_ready, at(i, 2, 2))
                okf = okn[:].rearrange("p a b -> p (a b)")
                zif = zi[:].rearrange("p a b -> p (a b)")
                V.tensor_tensor(okf, pair(X), zif, ALU.mult).then_inc(vec_step, 1)
                dve.wait_ge(vec_step, at(i, CHAIN, 1))
                V.tensor_reduce(okmax[:], okn[:], AX.X, ALU.max).then_inc(vec_step, 1)
                gate(2)
                dve.wait_ge(vec_step, at(i, CHAIN, 2))
                V.tensor_tensor(okn[:], okn[:], okmax[:].unsqueeze(2).to_broadcast([P, TILES * 2, M]),
                                ALU.subtract).then_inc(slots_shifted, 1)

                gate(3)
                dve.wait_ge(slots_exp, at(i, 1, 1))
                V.tensor_reduce(psum_[:], pe_[:], AX.X, ALU.add).then_inc(vec_step, 1)
                gate(4)
                dve.wait_ge(vec_step, at(i, CHAIN, 3))
                V.reciprocal(psum_[:], psum_[:]).then_inc(vec_step, 1)
                V.tensor_tensor(pe_[:].rearrange("p a b -> p (a b)"), pe_[:].rearrange("p a b -> p (a b)"), zif,
                                ALU.mult).then_inc(vec_step, 1)
                gate(5)
                dve.wait_ge(vec_step, at(i, CHAIN, 5))
                V.tensor_tensor(okn[:], pe_[:], psum_[:].unsqueeze(2).to_broadcast([P, TILES * 2, M]),
                                ALU.mult).then_inc(w_ready, 1)
                scan(i, 0)
                for t in range(6, TILES):
                    gate(t)
                scan(i, 1)
                for n in range(8):
                    dve.wait_ge(read_ready, at(i, 8, n + 1))
                    V.tensor_tensor(aT[:, n, :], ps[:, AB + n % 2, 0:384], tri[:], ALU.mult).then_inc(read_masked, 1)
                scan(i, 2)
                for b in range(B):
                    dve.wait_ge(squares_ready, at(i, 4, b + 1))
                    V.tensor_reduce(ss[:, 4 * b:4 * b + 4], sq[:, b % 2], AX.X, ALU.add).then_inc(squares_read, 1)
                dve.wait_ge(rstd_ready, at(i, 1, 1))
                for b in range(B):
                    r = slice(4 * b, 4 * b + 4)
                    V.tensor_tensor(on[:, r, :], bank(X + b).rearrange("p (a b) -> p a b", a=4),
                                    rstd[:, r].unsqueeze(2).to_broadcast([P, 4, DV]), ALU.mult).then_inc(o_scaled, 1)
                for b in range(B):
                    r = slice(4 * b, 4 * b + 4)
                    dve.wait_ge(o_scaled, at(i, 4, b + 1))
                    V.tensor_tensor(on[:, r, :].rearrange("p a b -> p (a b)"), on[:, r, :].rearrange("p a b -> p (a b)"),
                                    th[:, 2 * b:2 * b + 2, :].rearrange("p a b -> p (a b)"),
                                    ALU.mult).then_inc(o_gated, 1)
                if not last_pair:
                    dve.wait_ge(decay_ready, at(i, 4, 4))
                    V.tensor_copy(a_cur[:], a_neg[:, :, bass.ds(2 * i + 2, 2)]).then_inc(a_picked, 1)
                    head(i + 1)
                scan(i, 3)
                for b in range(B):
                    dve.wait_ge(mixed_ready, at(i, 4, b + 1))
                    r = xres[:, 2 * b:2 * b + 2, :].rearrange("p a b -> p (a b)")
                    if b == 0:
                        dve.wait_ge(mixed_added, at(i, 4, 1))
                    V.tensor_tensor(r, r, bank(X + b % 2), ALU.add).then_inc(mixed_added, 1)

            head(0)
            dve.wait_ge(pool_set, 1)
            dve.wait_ge(scan_consts, 96)
            for e in range(ET):
                dve.wait_ge(inner_copied, 2 * e + 2)
                out = conv[:, e].rearrange("p (b t) -> p b t", b=B)
                for tap in range(DC):
                    x_tap = x_pad[:, e, :, tap:tap + T]
                    if tap == 0:
                        ins = V.tensor_scalar(out, x_tap, s_cols[:, e, 0:1], s_cols[:, e, DC:DC + 1], ALU.mult, ALU.add)
                    else:
                        dve.wait_ge(conv_step, 4 * e + tap)
                        ins = V.scalar_tensor_tensor(out=out, in0=x_tap, scalar=s_cols[:, e, tap:tap + 1], in1=out,
                                                     op0=ALU.mult, op1=ALU.add)
                    ins.then_inc(conv_step, 1)
            for e in range(ET):
                dve.wait_ge(scan_act, e + 1)
                V.tensor_scalar(aux[:, e], aux[:, e], 0.5, 0.5, ALU.mult, ALU.add).then_inc(conv_step, 1)
                dve.wait_ge(conv_step, 9 + e)
                V.tensor_tensor(u[:, e], aux[:, e], conv[:, e], ALU.mult).then_inc(u_ready, 1)
            dve.wait_ge(scan_act, 11)
            V.tensor_scalar(aux[:], conv[:], 1.0, None, ALU.add).then_inc(softplus_step, 1)
            dve.wait_ge(softplus_step, 1)
            dve.wait_ge(scan_act, 12)
            V.scalar_tensor_tensor(out=conv[:], in0=aux[:], scalar=-1.0, in1=conv[:], op0=ALU.add,
                                   op1=ALU.subtract).then_inc(softplus_step, 1)
            V.tensor_tensor(delta[:], delta[:], aux2[:], ALU.add).then_inc(softplus_step, 1)
            dve.wait_ge(softplus_step, 3)
            V.tensor_tensor(delta[:], delta[:], conv[:], ALU.subtract).then_inc(softplus_step, 1)
            dve.wait_ge(softplus_step, 4)
            V.tensor_tensor(du[:], delta[:], u[:], ALU.mult).then_inc(u_ready, 1)
            for e in range(ET):
                last = V.tensor_scalar(y[:, e], u[:, e], s_cols[:, e, DC + 2:DC + 3], None, ALU.mult)
            last.then_inc(u_ready, 1)
            dve.wait_ge(a_ready, 2)
            V.tensor_copy(a_cur[:], a_neg[:, :, 0:2]).then_inc(a_picked, 1)
            dve.wait_ge(x_loaded, 32)
            with dve.Fori(0, PAIRS - 1) as i:
                step(i, False)
            step(PAIRS - 1, True)

            def norm(n):
                for t in range(TILES):
                    last = V.bn_stats(stats[:, t, :], xres[:, t, :])
                then(last)
                for t in range(TILES):
                    last = V.bn_aggr(moments[:, t, :], stats[:, t, :])
                last.then_inc(ln_moments, 1)
                dve.wait_ge(ln_scale, 2 * n + 2)
                then(V.scalar_tensor_tensor(out=ln_shift[:], in0=moments[:, :, 0], scalar=-1.0, in1=ln_rstd[:],
                                            op0=ALU.mult, op1=ALU.mult))
                for t in range(TILES):
                    V.tensor_scalar(xres[:, t, :], xres[:, t, :], ln_rstd[:, t:t + 1], ln_shift[:, t:t + 1],
                                    ALU.mult, ALU.add).then_inc(normed, 1)

            dve.wait_ge(mixed_added, 4 * PAIRS + 1)
            norm(0)
            dve.wait_ge(tanh_ready, TILES * PAIRS + 1)
            dve.wait_ge(y_added, 4 * PAIRS + 2)
            then(V.scalar_tensor_tensor(out=v[:], in0=th[:], scalar=1.0, in1=xres[:], op0=ALU.add, op1=ALU.mult))
            for b in range(B):
                V.tensor_tensor(v[:, 2 * b:2 * b + 2, :], v[:, 2 * b:2 * b + 2, :], y[:, :, b * T:(b + 1) * T],
                                ALU.mult).then_inc(y_gated, 1)
            for b in range(B):
                dve.wait_ge(y_turned, b + 1)
                r = xres[:, 2 * b:2 * b + 2, :].rearrange("p a b -> p (a b)")
                V.scalar_tensor_tensor(out=r, in0=bank(X + b), scalar=0.5, in1=r, op0=ALU.mult,
                                       op1=ALU.add).then_inc(y_residual, 1)
            dve.wait_ge(y_residual, 4)
            norm(1)
            dve.wait_ge(route_mm, 1)
            logits = bank(X).rearrange("p (t e) -> p t e", t=TILES)
            def per_tile(col, n):
                return col.unsqueeze(2).to_broadcast([P, TILES, n])

            then(V.tensor_reduce(top_logit[:], logits, AX.X, ALU.max))
            V.memset(score[:, :, E:SC], -7.0)
            V.tensor_tensor(score[:, :, 0:E], logits, per_tile(top_logit[:], E), ALU.subtract).then_inc(route_vec, 1)
            dve.wait_ge(route_act, 1)
            then(V.tensor_reduce(score_sum[:], score[:, :, 0:E], AX.X, ALU.add))
            then(V.reciprocal(score_sum[:], score_sum[:]))
            then(V.tensor_tensor(score[:, :, 0:E], score[:, :, 0:E], per_tile(score_sum[:], E), ALU.mult))
            for t in range(TILES):
                last = V.max(top8[:, t, :], score[:, t, 0:E])
            then(last)
            then(V.memset(top8[:, :, TOPK:8], -7.0))
            for t in range(TILES):
                last = V.match_replace(score_rest[:, t, :], top8[:, t, :], score[:, t, :], -9.0)
            then(last)
            then(V.tensor_tensor(chosen[:], score[:, :, 0:E], score_rest[:, :, 0:E], ALU.not_equal))
            V.tensor_copy(chosen_bf[:], chosen[:]).then_inc(route_vec, 1)
            dve.wait_ge(route_mm, 2)
            then(V.tensor_scalar(blocks[:], ps[:, Y, 0:E], P - 1.0, 1.0 / P, ALU.add, ALU.mult))
            then(V.tensor_scalar(blocks[:], blocks[:], -0.498, ROUND, ALU.add, ALU.add))
            then(V.tensor_scalar(blocks[:], blocks[:], -ROUND, None, ALU.add))
            then(V.tensor_tensor_scan(blk_end[:], ones[:, 0:E], blocks[:], 0.0, ALU.mult, ALU.add))
            then(V.tensor_tensor(blk_row[:], blk_end[:], blocks[:], ALU.subtract))
            then(V.tensor_scalar(late[:], blk_end[:], tok_id[:, 0:1], None, ALU.is_le))
            then(V.tensor_reduce(blk_expert[:], late[:], AX.X, ALU.add))
            V.tensor_scalar(blk_expert[:], blk_expert[:], E - 1.0, None, ALU.min).then_inc(route_vec, 1)
            then(V.tensor_scalar(groups_f[:], blk_end[0:1, E - 1:E], 1.0 / NJ, (NJ - 1.0) / NJ - 0.498, ALU.mult, ALU.add))
            then(V.tensor_scalar(groups_f[:], groups_f[:], ROUND, None, ALU.add))
            V.tensor_scalar(groups[:], groups_f[:], -ROUND, None, ALU.add).then_inc(groups_known, 1)
            then(V.tensor_scalar(blk_row[:], blk_row[:], float(P), 1.0, ALU.mult, ALU.add))
            then(V.tensor_tensor(place[:], bank(X + 1).rearrange("p (t e) -> p t e", t=TILES),
                                 blk_row[:].unsqueeze(1).to_broadcast([P, TILES, E]), ALU.add))
            then(V.tensor_tensor(place[:], place[:], chosen[:], ALU.mult))
            for t in range(TILES):
                last = V.max(place8[:, t, :], place[:, t, :])
            then(last)
            then(V.tensor_scalar(slot[:], place8[:, :, 0:TOPK], -1.0, None, ALU.add))
            then(V.tensor_copy(slot_idx[:], slot[:]))
            then(V.tensor_scalar(slot_blk[:], slot[:], 1.0 / P, -0.498, ALU.mult, ALU.add))
            then(V.tensor_scalar(slot_blk[:], slot_blk[:], ROUND, None, ALU.add))
            then(V.tensor_scalar(slot_blk[:], slot_blk[:], -ROUND, None, ALU.add))
            then(V.scalar_tensor_tensor(out=slot_row[:], in0=slot_blk[:], scalar=-float(P), in1=slot[:], op0=ALU.mult,
                                        op1=ALU.add))
            for n in range(TILES * TOPK):
                t, k = n // TOPK, n % TOPK
                if n >= 4:
                    dve.wait_ge(hot_used, n - 3)
                V.tensor_scalar(row_hot[:, n % 4, :], iota[:], slot_row[:, t, k:k + 1], tok_id[:, t:t + 1], ALU.is_equal,
                                ALU.mult).then_inc(hot_ready, 1)
                V.tensor_scalar(blk_hot[:, n % 4, :], iota[:, 0:NBLK], slot_blk[:, t, k:k + 1], None,
                                ALU.is_equal).then_inc(hot_ready, 1)
            dve.wait_ge(hot_used, TILES * TOPK)
            V.tensor_copy(tok_of[:], ps[:, Y + 1, 0:NBLK]).then_inc(tok_known, 1)

            def hidden(n, j):
                dve.wait_ge(g_tanh, n + 1)
                V.scalar_tensor_tensor(out=g_th[:, j, :], in0=g_th[:, j, :], scalar=1.0, in1=ps[:, 2 * j + 1, 0:F],
                                       op0=ALU.add, op1=ALU.mult).then_inc(g_silu, 1)
                dve.wait_ge(g_silu, n + 1)
                V.tensor_tensor(hid[:, j, :], g_th[:, j, :], ps[:, 2 * j + 1, F:2 * F], ALU.mult).then_inc(hid_ready, 1)

            for r in range(TILES // NJ):
                for j in range(NJ):
                    hidden(r * NJ + j, j)
                for j in range(NJ):
                    n = r * NJ + j
                    dve.wait_ge(down_ready, n + 1)
                    if n == 0:
                        dve.wait_ge(x_stored, 16)
                    V.scalar_tensor_tensor(out=xres[:, n, :], in0=ps[:, 2 * j, 256:512], scalar=0.5, in1=xres[:, n, :],
                                           op0=ALU.mult, op1=ALU.add).then_inc(down_copied, 1)
            with dve.Fori(0, used_groups(dve)) as i:
                for j in range(NJ):
                    hidden(i * NJ + j + TILES, j)
                for j in range(NJ):
                    dve.wait_ge(down_ready, i * NJ + j + TILES + 1)
                    dve.wait_ge(y_stored[j], at(i, 16, 16))
                    V.tensor_scalar(y_out[:, j, :], ps[:, 2 * j, 256:512], 0.5, None, ALU.mult).then_inc(down_copied, 1)
            for t in range(TILES):
                then(V.tensor_tensor(pick[:], place[:, t, :].unsqueeze(1).to_broadcast([P, TOPK, E]),
                                     place8[:, t, 0:TOPK].unsqueeze(2).to_broadcast([P, TOPK, E]), ALU.is_equal))
                then(V.tensor_tensor(pick[:], pick[:], score[:, t, 0:E].unsqueeze(1).to_broadcast([P, TOPK, E]),
                                     ALU.mult))
                then(V.tensor_reduce(pick_w[:, t, :], pick[:], AX.X, ALU.add))
            for n in range(TILES * TOPK):
                t, k = n // TOPK, n % TOPK
                dve.wait_ge(back[n % 8], 16 * (n // 8 + 1))
                if n:
                    dve.wait_ge(combined, n)
                V.scalar_tensor_tensor(out=xres[:, t, :], in0=yg[:, n % 8, :], scalar=pick_w[:, t, k:k + 1],
                                       in1=xres[:, t, :], op0=ALU.mult, op1=ALU.add).then_inc(combined, 1)
            dve.wait_ge(combined, TILES * TOPK)
            norm(2)
            dve.wait_ge(layer_loaded, 144)
            for t in range(TILES):
                if t % 2 == 0:
                    dve.wait_ge(x_turned, 4 * TURN["x2"] + t // 2 + 1)
                V.tensor_tensor(xres[:, t, :], xres[:, t, :], l_bo[:], ALU.add).then_inc(bias_added, 1)

            def add_exp(n):
                m, c = n // 2, slice((n % 2) * 512, (n % 2) * 512 + 512)
                dve.wait_ge(elu_exp, n + 1)
                V.tensor_tensor(lqT[:, m, c], lqT[:, m, c], lq_low[:, n % 2, :], ALU.add).then_inc(elu_done, 1)

            for n in range(4):
                m, c = n // 2, slice((n % 2) * 512, (n % 2) * 512 + 512)
                dve.wait_ge(lq_ready, n + 1)
                if n >= 2:
                    dve.wait_ge(elu_done, n - 1)
                V.tensor_scalar(lq_low[:, n % 2, :], bank(4 + n), l_bq[:, m:m + 1], 0.0, ALU.add, ALU.min).then_inc(elu_split, 1)
                V.tensor_scalar(lqT[:, m, c], bank(4 + n), l_bq[:, m:m + 1], 0.0, ALU.add, ALU.max).then_inc(elu_split, 1)
                if n:
                    add_exp(n - 1)
            add_exp(3)

            def finish_k(t):
                dve.wait_ge(elu_exp, 4 + t + 1)
                V.scalar_tensor_tensor(out=lk[:, t, :], in0=lk[:, t, :], scalar=0.0, in1=lk_low[:, t % 2, :], op0=ALU.max,
                                       op1=ALU.add).then_inc(elu_done, 1)

            for t in range(TILES):
                dve.wait_ge(lkv_ready, t + 1)
                V.tensor_tensor(lk[:, t, :], bank(t % 4, 0, 256), l_bkv[:, 0:D], ALU.add).then_inc(lkv_added, 1)
                V.tensor_tensor(lv[:, t, :], bank(t % 4, 256, 512), l_bkv[:, D:2 * D], ALU.add).then_inc(lkv_added, 1)
                dve.wait_ge(lkv_added, 2 * t + 1)
                if t >= 2:
                    dve.wait_ge(elu_done, 4 + t - 1)
                V.tensor_scalar(lk_low[:, t % 2, :], lk[:, t, :], 0.0, None, ALU.min).then_inc(elu_split, 1)
                if t:
                    finish_k(t - 1)
            finish_k(TILES - 1)
            for n in range(B * KD):
                dve.wait_ge(kv_ready, n + 1)
                V.tensor_tensor(kv[:, n, :], ps[:, 4 + n % 4, 0:KVW], head_mask[:], ALU.mult).then_inc(kv_masked, 1)
            for t in range(TILES):
                dve.wait_ge(num_ready, t + 1)
                src = ps[:, t % 4, 0:KD * KVW].rearrange("p (k n) -> p k n", k=KD)
                then(V.tensor_scalar(l_den[:, t], src[:, :, P:KVW], 1e-8, None, ALU.add))
                then(V.reciprocal(l_den[:, t], l_den[:, t]))
                for k in range(KD):
                    last = V.tensor_tensor(l_out[:, t, k * P:(k + 1) * P].rearrange("p (h d) -> p h d", h=LB),
                                           src[:, k, 0:P].rearrange("p (h d) -> p h d", h=LB),
                                           l_den[:, t, k, :].unsqueeze(2).to_broadcast([P, LB, P // LB]), ALU.mult)
                last.then_inc(att_ready, 1)

            def add_att(n):
                for t in range(TILES):
                    dve.wait_ge(proj_out_ready, 8 * n + t + 1)
                    dve.wait_ge(bias_added, 8 * n + t + 1)
                    V.tensor_tensor(xres[:, t, :], xres[:, t, :], ps[:, t % 4, 0:D], ALU.add).then_inc(attended, 1)
                dve.wait_ge(attended, 8 * n + 8)

            add_att(0)
            norm(3)
            dve.wait_ge(layer_loaded, 272)
            pi = float(np.pi)
            for half, freq in enumerate((1.0, 0.01)):
                for n in range(2):
                    out = ang[:, :, n, half::2]
                    last = V.tensor_scalar(out, pos[:], freq, (0.5 * pi, 0.0)[n], ALU.mult, ALU.add)
            last.then_inc(angle, 1)
            dve.wait_ge(angle, 1)
            V.tensor_scalar(turns[:], ang[:], 0.5 / pi, ROUND, ALU.mult, ALU.add).then_inc(angle, 1)
            dve.wait_ge(angle, 2)
            V.tensor_scalar(turns[:], turns[:], -ROUND, None, ALU.add).then_inc(angle, 1)
            dve.wait_ge(angle, 3)
            V.scalar_tensor_tensor(out=ang[:], in0=turns[:], scalar=-2.0 * pi, in1=ang[:], op0=ALU.mult,
                                   op1=ALU.add).then_inc(angle, 1)
            dve.wait_ge(angle, 4)
            in_pi = 3.1415925
            V.tensor_scalar(ang[:], ang[:], in_pi, -in_pi, ALU.min, ALU.max).then_inc(angle, 2)
            dve.wait_ge(cos_sin_ready, 1)

            def rotate(src, dst, tiles, n, size):
                pairs = src.rearrange("p (t h c two) -> p t h c two", t=tiles.stop - tiles.start, h=XH, two=2)
                out = dst[:, tiles, :].rearrange("p t (h c two) -> p t h c two", h=XH, two=2)
                shape = [P, tiles.stop - tiles.start, XH, 4]
                for turn in range(2):
                    for two in range(2):
                        w = cos_sin[:, tiles, turn ^ two, :].unsqueeze(2).to_broadcast(shape)
                        prod = rot[:, turn, two, 0:size].rearrange("p (t h c) -> p t h c", t=shape[1], h=XH)
                        V.tensor_tensor(prod, pairs[:, :, :, :, two], w, ALU.mult).then_inc(turns_done, 1)
                dve.wait_ge(turns_done, 4 * n + 4)
                for turn in range(2):
                    o = out[:, :, :, :, turn]
                    p0, p1 = (rot[:, turn, two, 0:size].rearrange("p (t h c) -> p t h c", t=shape[1], h=XH) for two in range(2))
                    V.tensor_tensor(o, p0, p1, (ALU.subtract, ALU.add)[turn]).then_inc(rotated, 1)
                dve.wait_ge(rotated, 2 * n + 2)

            for t in range(TILES):
                dve.wait_ge(xv_copied, t + 1)
                rotate(bank(t % 4, 0, 256), k_rot, slice(t, t + 1), t, P)

            def stack(n, src, dst, order):
                for j in range(2):
                    dve.wait_ge(part_cast, 3 * n + j + 1)
                    V.tensor_tensor(src[:], src[:], part[:, j], ALU.subtract).then_inc(part_rest, 1)
                    dve.wait_ge(part_rest, 2 * n + j + 1)
                dve.wait_ge(part_cast, 3 * n + 3)
                for slot_n, j in enumerate(order):
                    V.tensor_copy(dst[:, :, :, slot_n * XD_H:(slot_n + 1) * XD_H],
                                  part[:, j].rearrange("p t (h d) -> p t h d", h=XH)).then_inc(stacked, 1)

            stack(0, k_rot, k_st, (0, 1, 0, 2, 1, 0))
            for t in range(TILES):
                if t % 2 == 0:
                    dve.wait_ge(x_turned, 4 * TURN["x3"] + t // 2 + 1)
                V.tensor_tensor(xres[:, t, :], xres[:, t, :], x_bo[:], ALU.add).then_inc(bias_added, 1)
            for b in range(B):
                dve.wait_ge(xq_ready, b + 1)
                rotate(bank(4 + b), q_rot, slice(2 * b, 2 * b + 2), TILES + b, 256)
            stack(1, q_rot, q_st, (0, 0, 1, 0, 1, 2))
            with dve.Fori(0, XPAIRS) as i:
                for b in range(B):
                    dve.wait_ge(rows_ready, at(i, 4, b + 1))
                    V.tensor_reduce(row_max[:, bass.ds(i * 16 + 4 * b, 4)],
                                    pair(4 + 2 * (b % 2)).rearrange("p (a k) -> p a k", a=4), AX.X,
                                    ALU.max).then_inc(rows_maxed, 1)
            dve.wait_ge(rows_maxed, 4 * XPAIRS + 2)
            then(V.tensor_scalar(row_max[:], row_max[:], -1.0, None, ALU.mult))
            for j in range(3):
                then(V.tensor_copy(shift[:, j], row_max[:]))
                if j < 2:
                    then(V.tensor_tensor(row_max[:], row_max[:], shift[:, j], ALU.subtract))
                for b in range(B):
                    last = V.tensor_copy(
                        q_st[:, 2 * b:2 * b + 2, :, SHIFT + j].rearrange("p q (i h) -> p q i h", h=2),
                        shift[:, j].rearrange("p (i b h q) -> p b q i h", b=B, h=2, q=2)[:, b])
            last.then_inc(shifted, 1)

            def copy_k(n, j):
                dve.wait_ge(heads_turned, at(n + XPAIRS, 2, 2))
                V.tensor_copy(ksT[:, j], bank(1).bitcast(BF16)).then_inc(ksT_copied, 1)

            def divide(g, b):
                dve.wait_ge(pv_ready, at(g, ITEMS, (b + 1) * GP) + 2)
                then(V.reciprocal(x_den[:, b % 2], ps[P // 2:P, 2 + b % 2, 0:256]))
                rows = slice(P // 2 * (g % 2), P // 2 * (g % 2 + 1))
                V.tensor_tensor(xT[rows, g // 2, b * T:(b + 1) * T], ps[0:P // 2, 2 + b % 2, 0:256], x_den[:, b % 2],
                                ALU.mult).then_inc(acc_free, 1)

            for jj in range(GP):
                copy_k(jj, jj)
            for g in range(XGROUPS):
                for b in range(B - 1):
                    divide(g, b)
                if g < XGROUPS - 1:
                    for jj in range(GP):
                        copy_k((g + 1) * GP + jj, jj)
                divide(g, B - 1)
            add_att(1)
            norm(4)
            dve.wait_ge(acc_free, XGROUPS * B + 2)
            for n, w in enumerate((f_in, f_out)):
                V.tensor_reduce(f_sum[:, n:n + 1], w[:].rearrange("p a b -> p (a b)"), AX.X, ALU.add,
                                apply_absolute_value=True).then_inc(ternary, 1)
            dve.wait_ge(f_total, 1)
            then(V.tensor_scalar(f_scale[:], ps[:, 7, 0:2], 1.0 / (D * HF), 1e-5, ALU.mult, ALU.max))
            then(V.reciprocal(f_inv[:], f_scale[:]))
            for n, (w, q) in enumerate(((f_in, q_in), (f_out, q_out))):
                then(V.tensor_scalar(w[:], w[:], f_inv[:, n:n + 1], ROUND, ALU.mult, ALU.add))
                then(V.tensor_scalar(w[:], w[:], -ROUND, 1.0, ALU.add, ALU.min))
                V.tensor_scalar(q[:], w[:], -1.0, None, ALU.max).then_inc(ternary, 1)
            dve.wait_ge(xT_copied, 4 * TURN["x4"] + 4)
            for j in range(2):
                dve.wait_ge(part_cast, 6 + j + 1)
                V.tensor_tensor(xT[:], xT[:], x_part[:, j], ALU.subtract).then_inc(part_rest, 1)
                dve.wait_ge(part_rest, 4 + j + 1)

            def quantize(t):
                j = t % 2
                dve.wait_ge(h_square, t + 1)
                then(V.tensor_reduce(f_max[:, j:j + 1], hid_f[:, j], AX.X, ALU.max))
                then(V.tensor_scalar(f_max[:, j:j + 1], f_max[:, j:j + 1], 1e-5, None, ALU.max))
                V.reciprocal(f_rmax[:, j:j + 1], f_max[:, j:j + 1])
                then(V.tensor_scalar(f_back[:, j:j + 1], f_max[:, j:j + 1], f_scale[:, 1:2], 1.0 / 255, ALU.mult,
                                     ALU.mult))
                then(V.tensor_scalar(hid_f[:, j], hid_f[:, j], f_rmax[:, j:j + 1], 255.0, ALU.mult, ALU.mult))
                if t >= 2:
                    dve.wait_ge(hq_turned, t - 1)
                V.tensor_scalar(hid_q[:, j], hid_f[:, j], ROUND, -ROUND, ALU.add, ALU.add).then_inc(hq_ready, 1)

            def add_ffn(t):
                dve.wait_ge(f_out_ready, t + 1)
                V.scalar_tensor_tensor(out=xres[:, t, :], in0=ps[:, 6 + t % 2, 0:D], scalar=f_back[:, t % 2:t % 2 + 1],
                                       in1=xres[:, t, :], op0=ALU.mult, op1=ALU.add).then_inc(f_added, 1)

            for t in range(TILES):
                quantize(t)
                if t:
                    add_ffn(t - 1)
            add_ffn(TILES - 1)
            dve.wait_ge(f_added, TILES)
            norm(5)


def host_layout(inp):
    g = {k: np.asarray(v) for k, v in inp.items()}
    x = g["x"].reshape(TOK, D)

    def kp(w):
        return w.reshape(-1, P, w.shape[-1]).transpose(1, 0, 2)

    q, k, s = (kp(g["L0_attn_W" + n]).reshape(P, KD, PAIRS, P) for n in "qks")
    v, w = (kp(g["L0_attn_W" + n]).reshape(P, KD, PAIRS, 256) for n in "vg")
    t = np.triu(np.ones((P, P), np.float32))
    col = {n: g["L0_xattn_" + n].reshape(ET, P, -1) for n in ("conv_w", "conv_b", "dt_proj_b", "D", "A_log")}
    out = dict(
        x_tok=x.reshape(TILES, P, D).transpose(1, 0, 2), xT=kp(x.T),
        wqks=np.concatenate([q, k, s], 3).transpose(2, 0, 1, 3), wvg=np.concatenate([v, w], 3).transpose(2, 0, 1, 3),
        wo=g["L0_attn_Wo"].reshape(PAIRS, 2, DV, D).transpose(0, 2, 1, 3),
        gnorm=g["L0_attn_g_norm_weight"].reshape(P, 1),
        ident=np.eye(P, dtype=np.float32), tri=np.concatenate([t, np.ones((P, P), np.float32), t], 1),
        ctxT=g["ctx_1024"].reshape(TOK, CTX).T, w_in=g["L0_xattn_in_proj_w"].T, xp_w=kp(g["L0_xattn_x_proj_w"].T),
        dt_w=g["L0_xattn_dt_proj_w"].T,
        s_cols=np.concatenate([col[n] for n in ("conv_w", "conv_b", "dt_proj_b", "D")], 2).transpose(1, 0, 2),
        a_log=col["A_log"].transpose(1, 0, 2),
    )
    def ffn(gate, value, down):
        lead = gate.shape[:-2]
        gv = np.concatenate([gate, value], -1).reshape(*lead, KD, P, 2 * F)
        return np.moveaxis(gv, -3, -2), np.moveaxis(down.reshape(*lead, 2, FH, D), -3, -2)

    out["w_router"] = kp(g["L0_ffn_w_router"].T)
    out["w_gv"], out["w_dn"] = ffn(g["L0_ffn_wg"], g["L0_ffn_wv"], g["L0_ffn_wo"])
    out["sh_gv"], out["sh_dn"] = ffn(g["L0_ffn_swg"], g["L0_ffn_swv"], g["L0_ffn_swo"])
    bf16 = mybir.dt.np(BF16)
    out["iota"] = np.tile(np.arange(P, dtype=np.float32), (P, 1))
    out["tok_id"] = np.arange(TOK, dtype=np.float32).reshape(TILES, P).T
    out["tri_bf"] = np.triu(np.ones((P, P), np.float32), 1).astype(bf16)
    out["l_wq"], out["l_wo"] = kp(g["L1_attn_wq"].T), kp(g["L1_attn_wo"].T)
    out["l_wkv"] = np.concatenate([kp(g["L1_attn_wk"].T), kp(g["L1_attn_wv"].T)], 2)
    out["l_bq"] = g["L1_attn_bq"].reshape(KD, P).T
    out["l_bkv"] = np.concatenate([g["L1_attn_bk"], g["L1_attn_bv"]]).reshape(1, 2 * D)
    out["l_bo"] = g["L1_attn_bo"].reshape(1, D)
    same = np.arange(P)[:, None] // (P // LB)
    out["head_mask"] = np.concatenate([same == same.T, same == np.arange(LB)], 1).astype(np.float32)
    out["x_wq"], out["x_wo"] = kp(g["L1_xattn_Wq"]), kp(g["L1_xattn_Wout"])
    out["x_wkv"], out["x_bo"] = g["L1_xattn_Wkv"], g["L1_xattn_bout"].reshape(1, D)
    out["pos"] = kp(g["fside_BxSx2_0"].reshape(TOK, 2))
    out["ident_bf"] = np.eye(P, dtype=np.float32).astype(bf16)
    out["f_in"], out["f_out"] = kp(g["L1_ffn_c_fc"]), kp(g["L1_ffn_c_proj"].T)
    return {n: np.ascontiguousarray(m) for n, m in out.items()}


def kernel(**inputs):
    from concourse import bacc
    from concourse.bass_utils import run_bass_kernel_spmd

    nc = bacc.Bacc("TRN2", target_bir_lowering=False, num_devices=1)
    arrays = {"in_" + name: array for name, array in host_layout(inputs).items()}
    args = {name[3:]: nc.dram_tensor(name, m.shape, mybir.dt.from_np(m.dtype), kind="ExternalInput").ap()
            for name, m in arrays.items()}
    out = nc.dram_tensor("out", (B, T, D), F32, kind="ExternalOutput").ap()
    build(nc, args, out)
    return run_bass_kernel_spmd(nc, [arrays], core_ids=[0]).results[0]["out"]
```

```python
from contextlib import ExitStack

import numpy as np

import concourse.bass as bass
from concourse import mybir

F32 = mybir.dt.float32
BF16 = mybir.dt.bfloat16
ALU = mybir.AluOpType
ACT = mybir.ActivationFunctionType
AX = mybir.AxisListType

P = 128
B, T, D = 4, 256, 256
TOK = B * T
TILES = TOK // P
KD = D // P
LN_EPS = 1e-5
H, DK, DV, M = 16, 64, 128, 64
PAIRS = H // 2
CLAMP = 32.0
CTX = 128
DI, DS, DR, DC = 256, 16, 8, 4
ET = DI // P
XD = DR + 2 * DS
E, TOPK, F = 64, 6, 176
FH = F // 2
SC = E + 2
NJ = 4
NBLK = -(-((TOK * TOPK + E * (P - 1)) // P) // NJ) * NJ
LEAST_GROUPS = TOK * TOPK // P // NJ
ROUND = 1.5 * 2.0 ** 23
LH = 16
LB = P // (D // LH)
KVW = P + LB
XH, XD_H = 32, 8
XPAIRS = XH // 2
SLOT = 64
Q_PARTS, K_PARTS = (0, 0, 1, 0, 1, 2), (0, 1, 0, 2, 1, 0)
SHIFT = 6 * XD_H
GH = P // (2 * XD_H)
GAP = P // 2 - XD_H
VW = 3 * GAP + 2 * XD_H
XGROUPS = XH // GH
GP = GH // 2
ITEMS = B * GP
HF = 4 * D
KH = HF // P


TURN = dict(x1=0, x2=1, att0=2, x3=3, x4=4)


def at(i, per, c):
    return i * per + c


def build(nc, a, out):
    with ExitStack() as ctx:
        mem = [ctx]

        def sb(name, shape, dt=F32):
            return mem[-1].enter_context(nc.sbuf_tensor(name, shape, dt))

        def sem(name):
            return ctx.enter_context(nc.semaphore(name))

        ps = ctx.enter_context(nc.psum_tensor("ps", [P, 8, 512], F32))
        PJ, AB, X, Y = 0, 2, 4, 6

        xres = sb("xres", [P, TILES, D])
        xT = sb("xT", [P, KD, TOK])
        ident = sb("ident", [P, P])
        tri = sb("tri", [P, 384])
        ones = sb("ones", [P, 256])
        ctxT = sb("ctxT", [P, TOK])
        stats = sb("stats", [P, TILES, 6])
        moments = sb("moments", [P, TILES, 2])
        ln_var = sb("ln_var", [P, TILES])
        ln_rstd = sb("ln_rstd", [P, TILES])
        ln_shift = sb("ln_shift", [P, TILES])
        blank = sb("blank", [P, D])
        eps_col = sb("eps_col", [P, 1])
        attn_mem = ExitStack()
        mem.append(attn_mem)
        w_qks = sb("w_qks", [P, KD, 384])
        w_vg = sb("w_vg", [P, KD, 512])
        w_o = sb("w_o", [P, 2, D])
        gn_half = sb("gn_half", [P, 1])
        qT = sb("qT", [P, TOK])
        kT = sb("kT", [P, TOK])
        sT = sb("sT", [P, TOK])
        eT = sb("eT", [P, TOK])
        e_tok = sb("e_tok", [P, TILES, P])
        zT = sb("zT", [P, TOK])
        z_inv = sb("z_inv", [P, TILES, P])
        aT = sb("aT", [P, 8, 384])
        okn = sb("okn", [P, TILES * 2, M])
        slot_exp = sb("slot_exp", [P, TILES * 2, M])
        okmax = sb("okmax", [P, TILES * 2])
        slot_sum = sb("slot_sum", [P, TILES * 2])
        wT = sb("wT", [P, TOK])
        v = sb("v", [P, TILES, 256])
        th = sb("th", [P, TILES, 256])
        on = sb("on", [P, TILES * 2, DV])
        sq = sb("sq", [P, 2, 4, DV])
        ss = sb("ss", [P, TILES * 2])
        log_ms = sb("log_ms", [P, TILES * 2])
        rstd = sb("rstd", [P, TILES * 2])
        oT = sb("oT", [P, 2, TOK])
        w_in = sb("w_in", [P, DI])
        xp_w = sb("xp_w", [P, ET, XD])
        dt_w = sb("dt_w", [DR, DI])
        s_cols = sb("s_cols", [P, ET, DC + 3])
        a_neg = sb("a_neg", [P, ET, DS])
        a_cur = sb("a_cur", [P, ET, 2])
        x_dbl = sb("x_dbl", [XD, TOK])
        u = sb("u", [P, ET, TOK])
        delta = sb("delta", [P, ET, TOK])
        du = sb("du", [P, ET, TOK])
        y = sb("y", [P, ET, TOK])
        b_row = sb("b_row", [P, 2, TOK])
        c_row = sb("c_row", [P, 2, TOK])
        decay = sb("decay", [P, 2, TOK])
        drive = sb("drive", [P, 2, TOK])
        state = sb("state", [P, 2, TOK])
        x_pad = aT[:].rearrange("p a b -> p (a b)")[:, 0:ET * B * (T + 3)].rearrange(
            "p (e b t) -> p e b t", e=ET, b=B)
        conv = v[:].rearrange("p a b -> p (a b)").rearrange("p (e n) -> p e n", e=ET)
        aux = th[:].rearrange("p a b -> p (a b)").rearrange("p (e n) -> p e n", e=ET)
        aux2 = on[:].rearrange("p a b -> p (a b)").rearrange("p (e n) -> p e n", e=ET)
        mem.pop()
        attn_mem.close()

        x_wkv = sb("x_wkv", [P, 2 * D])
        x_wq = sb("x_wq", [P, KD, D])
        x_wo = sb("x_wo", [P, KD, D])
        x_bo = sb("x_bo", [P, D])
        ident_bf = sb("ident_bf", [P, P], BF16)
        pos = sb("pos", [P, TILES, 2])
        ang = sb("ang", [P, TILES, 2, 4])
        turns = sb("turns", [P, TILES, 2, 4])
        cos_sin = sb("cos_sin", [P, TILES, 2, 4])
        x_v = sb("x_v", [P, TILES, D])
        k_st = sb("k_st", [P, TILES, XH, SLOT], BF16)
        moe_mem = ExitStack()
        mem.append(moe_mem)
        U32 = mybir.dt.uint32
        w_router = sb("w_router", [P, KD, E])
        iota = sb("iota", [P, P])
        tok_id = sb("tok_id", [P, TILES])
        tri_bf = sb("tri_bf", [P, P], BF16)
        ones_bf = sb("ones_bf", [P, P], BF16)
        top_logit = sb("top_logit", [P, TILES])
        score_sum = sb("score_sum", [P, TILES])
        score = sb("score", [P, TILES, SC])
        score_rest = sb("score_rest", [P, TILES, SC])
        top8 = sb("top8", [P, TILES, 8])
        chosen = sb("chosen", [P, TILES, E])
        chosen_bf = sb("chosen_bf", [P, TILES, E], BF16)
        blocks = sb("blocks", [P, E])
        blk_end = sb("blk_end", [P, E])
        blk_row = sb("blk_row", [P, E])
        place = sb("place", [P, TILES, E])
        place8 = sb("place8", [P, TILES, 8])
        slot = sb("slot", [P, TILES, TOPK])
        slot_blk = sb("slot_blk", [P, TILES, TOPK])
        slot_row = sb("slot_row", [P, TILES, TOPK])
        slot_idx = sb("slot_idx", [P, TILES, TOPK], U32)
        pick = sb("pick", [P, TOPK, E])
        pick_w = sb("pick_w", [P, TILES, TOPK])
        late = sb("late", [P, E])
        blk_expert = sb("blk_expert", [P, 1])
        expert_row = sb("expert_row", [1, P], mybir.dt.int32)
        groups_f = sb("groups_f", [1, 1])
        groups = sb("groups", [1, 2], mybir.dt.int32)
        tok_of = sb("tok_of", [P, NBLK], U32)
        tok_cur = sb("tok_cur", [P, NJ], U32)
        xg = sb("xg", [P, NJ, D])
        xgT = sb("xgT", [P, NJ, KD * P])
        w_gv = sb("w_gv", [P, NJ, KD, 2 * F])
        w_dn = sb("w_dn", [FH, NJ, 2, D])
        sh_gv = sb("sh_gv", [P, KD, 2 * F])
        sh_dn = sb("sh_dn", [FH, 2, D])
        g_th = sb("g_th", [P, NJ, F])
        hid = sb("hid", [P, NJ, F])
        hidT = sb("hidT", [FH, NJ, 2 * P])
        y_out = sb("y_out", [P, NJ, D])
        yg = sb("yg", [P, 8, D])
        hot_mem = ExitStack()
        mem.append(hot_mem)
        row_hot = sb("row_hot", [P, 2, TOPK, P])
        blk_hot = sb("blk_hot", [P, 2, TOPK, NBLK])
        mem.pop()
        hot_mem.close()
        key_mem = ExitStack()
        mem.append(key_mem)
        key_rot = sb("key_rot", [P, 2, 2, 512])
        key_f32 = sb("key_f32", [P, TILES, D])
        key_part = sb("key_part", [P, 3, TILES, D], BF16)
        mem.pop()
        key_mem.close()
        l_wq = sb("l_wq", [P, KD, D])
        l_wkv = sb("l_wkv", [P, KD, 2 * D])
        l_wo = sb("l_wo", [P, KD, D])
        l_bq = sb("l_bq", [P, KD])
        l_bkv = sb("l_bkv", [P, 2 * D])
        l_bo = sb("l_bo", [P, D])
        head_mask = sb("head_mask", [P, KVW])
        lqT = sb("lqT", [P, KD, TOK])
        lq_low = sb("lq_low", [P, 2, 512])
        lk = sb("lk", [P, TILES, D])
        lk_low = sb("lk_low", [P, 2, D])
        lv = sb("lv", [P, TILES, D])
        kv = sb("kv", [P, B * KD, KVW])
        l_den = sb("l_den", [P, TILES, KD, LB])
        l_out = sb("l_out", [P, TILES, D])
        mem.pop()
        moe_mem.close()
        last_mem = ExitStack()
        mem.append(last_mem)
        rot = sb("rot", [P, 2, 2, 512])
        q_rot = sb("q_rot", [P, TILES, D])
        hid_int = sb("hid_int", [P, TILES, D])
        v_win = sb("v_win", [P, 2, 2, 2, VW])
        part = sb("part", [P, 3, TILES, D], BF16)
        q_st = sb("q_st", [P, TILES, XH, SLOT], BF16)
        qsT = sb("qsT", [P, GP, TOK], BF16)
        ksT = sb("ksT", [P, GP, TOK], BF16)
        row_max = sb("row_max", [P, XPAIRS * 16])
        shift = sb("shift", [P, 3, XPAIRS * 16], BF16)
        probT = sb("probT", [P, 4, 2, 2 * P])
        x_den = sb("x_den", [P // 2, 2, 256])
        f_in = sb("f_in", [P, KD, HF])
        f_out = sb("f_out", [P, KH, D])
        f_sum = sb("f_sum", [P, 2])
        f_scale = sb("f_scale", [P, 2])
        f_inv = sb("f_inv", [P, 2])
        q_in = sb("q_in", [P, KD, HF], BF16)
        q_out = sb("q_out", [P, KH, D], BF16)
        x_part = part[:].rearrange("p a b c -> p a (b c)").rearrange("p a (k n) -> p a k n", k=KD)
        hid_f = q_rot[:].rearrange("p a b -> p (a b)").rearrange("p (a b) -> p a b", a=2)
        hid_q = hid_int[:].rearrange("p a b -> p (a b)").bitcast(BF16).rearrange("p (a b) -> p a b", a=4)
        f_max = sb("f_max", [P, 2])
        f_rmax = sb("f_rmax", [P, 2])
        f_back = sb("f_back", [P, 2])
        mem.pop()
        last_mem.close()

        x_dram = nc.dram_tensor("x_dram", (TOK, D), F32).ap()
        y_dram = nc.dram_tensor("y_dram", (NBLK * P, D), F32).ap()
        x_dbl_dram = nc.dram_tensor("x_dbl_dram", (XD, TOK), F32).ap()

        x_loaded = sem("x_loaded")
        const_loaded = sem("const_loaded")
        const_set = sem("const_set")
        qks_loaded = sem("qks_loaded")
        vg_loaded = sem("vg_loaded")
        wo_loaded = sem("wo_loaded")
        proj_ready = sem("proj_ready")
        qk_copied = sem("qk_copied")
        s_clipped = sem("s_clipped")
        eT_ready = sem("eT_ready")
        zT_ready = sem("zT_ready")
        lnz_ready = sem("lnz_ready")
        scores_ready = sem("scores_ready")
        scores_masked = sem("scores_masked")
        e_turned = sem("e_turned")
        e_copied = sem("e_copied")
        z_turned = sem("z_turned")
        zi_ready = sem("zi_ready")
        slots_ready = sem("slots_ready")
        slots_shifted = sem("slots_shifted")
        slots_exp = sem("slots_exp")
        w_ready = sem("w_ready")
        tanh_ready = sem("tanh_ready")
        gate_ready = sem("gate_ready")
        w_turned = sem("w_turned")
        wT_copied = sem("wT_copied")
        read_ready = sem("read_ready")
        read_masked = sem("read_masked")
        o_ready = sem("o_ready")
        squares_ready = sem("squares_ready")
        squares_read = sem("squares_read")
        rstd_ready = sem("rstd_ready")
        o_scaled = sem("o_scaled")
        o_gated = sem("o_gated")
        o_turned = sem("o_turned")
        oT_copied = sem("oT_copied")
        mixed_ready = sem("mixed_ready")
        mixed_added = sem("mixed_added")
        vec_step = sem("vec_step")
        chain = sem("chain")
        act_step = sem("act_step")
        scan_consts = sem("scan_consts")
        scan_mm = sem("scan_mm")
        inner_copied = sem("inner_copied")
        pool_set = sem("pool_set")
        conv_step = sem("conv_step")
        u_ready = sem("u_ready")
        x_dbl_copied = sem("x_dbl_copied")
        x_dbl_stored = sem("x_dbl_stored")
        scan_act = sem("scan_act")
        softplus_step = sem("softplus_step")
        a_ready = sem("a_ready")
        bc_loaded = [sem(f"bc_loaded{j}") for j in range(2)]
        a_picked = sem("a_picked")
        decay_ready = sem("decay_ready")
        drive_ready = sem("drive_ready")
        scanned = sem("scanned")
        read_out = sem("read_out")
        y_added = sem("y_added")
        ln_moments = sem("ln_moments")
        ln_scale = sem("ln_scale")
        normed = sem("normed")
        x_turned = sem("x_turned")
        xT_copied = sem("xT_copied")
        y_gated = sem("y_gated")
        y_turned = sem("y_turned")
        y_residual = sem("y_residual")
        moe_consts = sem("moe_consts")
        route_mm = sem("route_mm")
        groups_known = sem("groups_known")
        route_vec = sem("route_vec")
        route_act = sem("route_act")
        hot_ready = sem("hot_ready")
        hot_used = sem("hot_used")
        tok_known = sem("tok_known")
        tok_picked = sem("tok_picked")
        gather_due = sem("gather_due")
        x_stored = sem("x_stored")
        gathered = [sem(f"gathered{j}") for j in range(NJ)]
        w_loaded = [sem(f"w_loaded{j}") for j in range(NJ)]
        dn_loaded = [sem(f"dn_loaded{j}") for j in range(NJ)]
        y_stored = [sem(f"y_stored{j}") for j in range(NJ)]
        xg_turned = sem("xg_turned")
        xgT_copied = sem("xgT_copied")
        gv_ready = sem("gv_ready")
        g_tanh = sem("g_tanh")
        g_silu = sem("g_silu")
        hid_ready = sem("hid_ready")
        hid_turned = sem("hid_turned")
        hidT_copied = sem("hidT_copied")
        down_ready = sem("down_ready")
        down_copied = sem("down_copied")
        y_blank = sem("y_blank")
        back = [sem(f"back{j}") for j in range(8)]
        combined = sem("combined")
        lproj_ready = sem("lproj_ready")
        elu_split = sem("elu_split")
        elu_exp = sem("elu_exp")
        elu_done = sem("elu_done")
        lkv_added = sem("lkv_added")
        kv_ready = sem("kv_ready")
        kv_masked = sem("kv_masked")
        proj_out_ready = sem("proj_out_ready")
        bias_added = sem("bias_added")
        attended = sem("attended")
        layer_loaded = sem("layer_loaded")
        angle = sem("angle")
        cos_sin_ready = sem("cos_sin_ready")
        xproj_ready = sem("xproj_ready")
        xv_copied = sem("xv_copied")
        turns_done = sem("turns_done")
        rotated = sem("rotated")
        part_cast = sem("part_cast")
        part_rest = sem("part_rest")
        stacked = sem("stacked")
        heads_turned = sem("heads_turned")
        qsT_copied = sem("qsT_copied")
        ksT_copied = sem("ksT_copied")
        rows_ready = sem("rows_ready")
        rows_maxed = sem("rows_maxed")
        shifted = sem("shifted")
        cols_ready = sem("cols_ready")
        prob_ready = sem("prob_ready")
        pv_ready = sem("pv_ready")
        acc_free = sem("acc_free")
        v_placed = sem("v_placed")
        f_total = sem("f_total")
        ternary = sem("ternary")
        h_ready = sem("h_ready")
        h_relu = sem("h_relu")
        hq_ready = sem("hq_ready")
        hq_turned = sem("hq_turned")
        hqT_copied = sem("hqT_copied")
        f_out_ready = sem("f_out_ready")
        f_added = sem("f_added")

        block = ctx.enter_context(nc.Block())

        def bank(n, a=0, b=512):
            return ps[:, n, a:b]

        def pair(n):
            return ps[:, n:n + 2, :].rearrange("p a b -> p (a b)")

        def used_groups(engine):
            engine.wait_ge(groups_known, 1)
            return engine.value_load(groups[0:1, 0:1], min_val=LEAST_GROUPS, max_val=NBLK // NJ)

        def last_used_group(engine):
            engine.wait_ge(groups_known, 1)
            return engine.value_load(groups[0:1, 1:2], min_val=LEAST_GROUPS - 1, max_val=NBLK // NJ - 1)

        @block.sync
        def _(sp):
            for dst, src in ((w_in, "w_in"), (ctxT, "ctxT"), (s_cols, "s_cols")):
                sp.dma_start(dst[:], a[src]).then_inc(scan_consts, 16)
            sp.dma_start(xT[:], a["xT"]).then_inc(x_loaded, 16)
            sp.dma_start(w_qks[:], a["wqks"][0]).then_inc(qks_loaded, 16)
            sp.wait_ge(scan_consts, 48)
            for dst, src in ((xp_w, "xp_w"), (dt_w, "dt_w"), (a_neg, "a_log")):
                sp.dma_start(dst[:], a[src]).then_inc(scan_consts, 16)
            for dst, src in ((ident, "ident"), (tri, "tri"), (gn_half, "gnorm")):
                sp.dma_start(dst[:], a[src]).then_inc(const_loaded, 16)
            sp.dma_start(w_vg[:], a["wvg"][0]).then_inc(vg_loaded, 16)
            sp.dma_start(w_o[:], a["wo"][0]).then_inc(wo_loaded, 16)
            sp.wait_ge(x_loaded, 16)
            sp.dma_start(xres[:], a["x_tok"]).then_inc(x_loaded, 16)
            sp.wait_ge(proj_ready, 6)
            sp.dma_start(w_qks[:], a["wqks"][1]).then_inc(qks_loaded, 16)
            sp.wait_ge(x_dbl_copied, 2)
            sp.dma_start(x_dbl_dram, x_dbl[:]).then_inc(x_dbl_stored, 16)
            sp.wait_ge(x_dbl_stored, 16)

            def scan_rows(i, j):
                row = DR + 2 * i + j
                for dst, r in ((b_row, row), (c_row, row + DS)):
                    src = x_dbl_dram[bass.ds(r, 1), :].to_broadcast([P, TOK])
                    sp.dma_start(dst[:, j, :], src).then_inc(bc_loaded[j], 16)

            for j in range(2):
                scan_rows(0, j)

            sp.wait_ge(pool_set, 2)
            chunk = NBLK // NJ
            for r in range(LEAST_GROUPS * NJ, NBLK, chunk):
                n = min(chunk, NBLK - r)
                sp.dma_start(y_dram[r * P:(r + n) * P, :].rearrange("(n p) d -> p n d", p=P),
                             blank[:].unsqueeze(1).to_broadcast([P, n, D])).then_inc(y_blank, 16)

            def loads(i, last):
                sp.wait_ge(proj_ready, at(i, 14, 14))
                sp.dma_start(w_vg[:], a["wvg"][bass.ds(i + 1, 1)].rearrange("a p k n -> (a p) k n")).then_inc(vg_loaded, 16)
                if not last:
                    sp.wait_ge(proj_ready, at(i, 14, 20))
                    sp.dma_start(w_qks[:], a["wqks"][bass.ds(i + 2, 1)].rearrange("a p k n -> (a p) k n")).then_inc(qks_loaded, 16)
                sp.wait_ge(mixed_ready, at(i, 4, 4))
                sp.dma_start(w_o[:], a["wo"][bass.ds(i + 1, 1)].rearrange("a p k n -> (a p) k n")).then_inc(wo_loaded, 16)
                for j in range(2):
                    sp.wait_ge(read_out, at(i, 4, 2 * j + 2))
                    scan_rows(i + 1, j)

            with sp.Fori(0, PAIRS - 2) as i:
                loads(i, False)
            loads(PAIRS - 2, True)
            sp.wait_ge(y_turned, 4)
            for dst, src in ((w_router, "w_router"), (iota, "iota"), (tok_id, "tok_id"), (tri_bf, "tri_bf")):
                sp.dma_start(dst[:], a[src]).then_inc(moe_consts, 16)
            for dst, src in ((sh_gv, "sh_gv"), (sh_dn, "sh_dn"), (x_wkv, "x_wkv"), (pos, "pos"), (ident_bf, "ident_bf"),
                             (x_wq, "x_wq"), (x_wo, "x_wo")):
                sp.dma_start(dst[:], a[src]).then_inc(layer_loaded, 16)
            sp.dma_start(x_bo[:], a["x_bo"].to_broadcast([P, D])).then_inc(layer_loaded, 16)
            sp.wait_ge(normed, 16)
            sp.dma_start(x_dram.rearrange("(t p) d -> p t d", p=P), xres[:]).then_inc(x_stored, 16)
            sp.wait_ge(route_act, 2)
            sp.wait_ge(y_blank, 16 * -(-(NBLK - LEAST_GROUPS * NJ) // (NBLK // NJ)))
            for j in range(NJ):
                sp.sem_inc(y_stored[j], 16)

            def store_y(i, j):
                sp.wait_ge(down_copied, at(i, NJ, j + 1) + TILES)
                rows = y_dram[bass.ds((i * NJ + j) * P, P), :]
                sp.dma_start(rows, y_out[:, j, :]).then_inc(y_stored[j], 16)

            def expert_of(i, j):
                return sp.value_load(expert_row[0:1, bass.ds(i * NJ + j, 1)], min_val=0, max_val=E - 1)

            def load_up(e, j):
                sp.dma_start(w_gv[:, j], a["w_gv"][bass.ds(e, 1)].rearrange("a p k n -> (a p) k n")).then_inc(w_loaded[j], 16)

            def load_down(e, j):
                sp.dma_start(w_dn[:, j], a["w_dn"][bass.ds(e, 1)].rearrange("a p k n -> (a p) k n")).then_inc(dn_loaded[j], 16)

            for j in range(NJ):
                e = expert_of(0, j)
                load_up(e, j)
                load_down(e, j)
            used = used_groups(sp)
            with sp.Fori(1, used) as i:
                for j in range(NJ):
                    sp.wait_ge(gv_ready, at(i, NJ, j + 1) + TILES - NJ)
                    load_up(expert_of(i, j), j)
                for j in range(NJ):
                    store_y(i - 1, j)
                    load_down(expert_of(i, j), j)
            for j in range(NJ):
                store_y(used - 1, j)
            sp.wait_ge(normed, 24)
            for dst, src in ((l_wq, "l_wq"), (l_wkv, "l_wkv"), (l_wo, "l_wo"), (l_bq, "l_bq"), (head_mask, "head_mask")):
                sp.dma_start(dst[:], a[src]).then_inc(layer_loaded, 16)
            sp.dma_start(l_bkv[:], a["l_bkv"].to_broadcast([P, 2 * D])).then_inc(layer_loaded, 16)
            sp.dma_start(l_bo[:], a["l_bo"].to_broadcast([P, D])).then_inc(layer_loaded, 16)
            sp.wait_ge(normed, 32)
            for dst, src in ((f_in, "f_in"), (f_out, "f_out")):
                sp.dma_start(dst[:], a[src]).then_inc(layer_loaded, 16)
            sp.wait_ge(normed, 48)
            sp.dma_start(out.rearrange("b (t p) d -> p (b t) d", p=P), xres[:]).then_inc(x_stored, 16)
            sp.wait_ge(x_stored, 32)

        @block.tensor
        def _(pe):
            mm = nc.tensor.matmul

            def project_qks(i, first, pieces):
                pe.wait_ge(qks_loaded, at(i, 16, 16))
                for n in pieces:
                    part, half = n // 2, n % 2
                    if n < 2:
                        if not first:
                            pe.wait_ge(gate_ready, at(i - 1, 8, 7 + n))
                    elif n < 4:
                        pe.wait_ge(qk_copied, at(i, 4, n - 1))
                    else:
                        pe.wait_ge(qk_copied, at(i, 4, n - 1))
                    for k in range(KD):
                        last = mm(bank(PJ + n % 2), w_qks[:, k, part * P:(part + 1) * P],
                                  xT[:, k, half * 512:(half + 1) * 512], start=(k == 0), stop=(k == KD - 1))
                    last.then_inc(proj_ready, 1)

            def scores(i, which):
                pe.wait_ge(qk_copied, at(i, 4, 4))
                for n in which:
                    b, h = n // 2, n % 2
                    if n >= 2:
                        pe.wait_ge(scores_masked, at(i, 8, n - 1))
                    r = slice(64 * h, 64 * h + 64)
                    c = b * T
                    mm(ps[:, AB + n % 2, 0:256], kT[r, c:c + P], qT[r, c:c + 256], start=True, stop=True)
                    mm(ps[:, AB + n % 2, 256:384], kT[r, c + P:c + 256], qT[r, c + P:c + 256],
                       start=True, stop=True).then_inc(scores_ready, 1)

            def step(i, last_pair):
                pe.wait_ge(eT_ready, at(i, 2, 2))
                pe.wait_ge(const_loaded, 48)
                pe.wait_ge(mixed_added, at(i, 4, 1))
                for n in range(2):
                    for t in range(4):
                        c = (4 * n + t) * P
                        last = nc.tensor.transpose(ps[:, X + n, t * P:(t + 1) * P], eT[:, c:c + P], ident[:])
                    last.then_inc(e_turned, 1)
                pe.wait_ge(lnz_ready, at(i, 1, 1))
                for n in range(2):
                    for t in range(4):
                        c = (4 * n + t) * P
                        last = nc.tensor.transpose(ps[:, Y + n, t * P:(t + 1) * P], zT[:, c:c + P], ident[:])
                    last.then_inc(z_turned, 1)
                pe.wait_ge(vg_loaded, at(i, 16, 16))

                def project_vg(t):
                    if t < 2:
                        pe.wait_ge(s_clipped, at(i, 2, t + 1))
                    else:
                        pe.wait_ge(gate_ready, at(i, 8, t - 1))
                    for k in range(KD):
                        last = mm(bank(PJ + t % 2), xT[:, k, t * P:(t + 1) * P], w_vg[:, k, :],
                                  start=(k == 0), stop=(k == KD - 1))
                    last.then_inc(proj_ready, 1)

                project_vg(0)
                project_vg(1)
                pe.wait_ge(e_copied, at(i, 2, 2))
                pe.wait_ge(scores_masked, at(i, 8, 8))
                for b in range(B):
                    for h in range(2):
                        n = 2 * b + h
                        m = slice(M * h, M * h + M)
                        o0 = ps[:, X + b // 2, (b % 2) * 256 + M * h:(b % 2) * 256 + M * h + M]
                        o1 = ps[:, X + b // 2, (b % 2) * 256 + P + M * h:(b % 2) * 256 + P + M * h + M]
                        mm(o0, aT[:, n, 0:P], e_tok[:, 2 * b, m], start=True, stop=True)
                        mm(o1, aT[:, n, P:256], e_tok[:, 2 * b, m], start=True, stop=False)
                        last = mm(o1, aT[:, n, 256:384], e_tok[:, 2 * b + 1, m], start=False, stop=True)
                last.then_inc(slots_ready, 1)
                for t in range(2, TILES):
                    project_vg(t)
                pe.wait_ge(w_ready, at(i, 1, 1))
                pe.wait_ge(zi_ready, at(i, 2, 2))
                for n in range(2):
                    for t in range(4):
                        r = 4 * n + t
                        last = nc.tensor.transpose(ps[:, Y + n, t * P:(t + 1) * P],
                                                   okn[:, 2 * r:2 * r + 2, :].rearrange("p a b -> p (a b)"), ident[:])
                    last.then_inc(w_turned, 1)
                def read(n):
                    b, h = n // 2, n % 2
                    if n % 4 == 0:
                        pe.wait_ge(wT_copied, at(i, 2, n // 4 + 1))
                    if n >= 2:
                        pe.wait_ge(read_masked, at(i, 8, n - 1))
                    r = slice(64 * h, 64 * h + 64)
                    c = b * T
                    mm(ps[:, AB + n % 2, 0:256], eT[r, c:c + P], wT[r, c:c + 256], start=True, stop=True)
                    mm(ps[:, AB + n % 2, 256:384], eT[r, c + P:c + 256], wT[r, c + P:c + 256],
                       start=True, stop=True).then_inc(read_ready, 1)

                def mix(n):
                    b, h = n // 2, n % 2
                    pe.wait_ge(read_masked, at(i, 8, n + 1))
                    vh = slice(DV * h, DV * h + DV)
                    o0 = ps[:, X + b, DV * h:DV * h + DV]
                    o1 = ps[:, X + b, 256 + DV * h:256 + DV * h + DV]
                    mm(o0, aT[:, n, 0:P], v[:, 2 * b, vh], start=True, stop=True)
                    mm(o1, aT[:, n, P:256], v[:, 2 * b, vh], start=True, stop=False)
                    last = mm(o1, aT[:, n, 256:384], v[:, 2 * b + 1, vh], start=False, stop=True)
                    if h == 1:
                        last.then_inc(o_ready, 1)

                read(0)
                for n in range(8):
                    if n < 7:
                        read(n + 1)
                    mix(n)
                if not last_pair:
                    project_qks(i + 1, False, range(4))

                def turn(b):
                    pe.wait_ge(o_gated, at(i, 4, b + 1))
                    if b >= 2:
                        pe.wait_ge(oT_copied, at(i, 4, b - 1))
                    for h in range(2):
                        for t in range(2):
                            last = nc.tensor.transpose(ps[:, AB + b % 2, (2 * h + t) * P:(2 * h + t + 1) * P],
                                                       on[:, 2 * (2 * b + t) + h, :], ident[:])
                    last.then_inc(o_turned, 1)

                def project_out(b):
                    pe.wait_ge(oT_copied, at(i, 4, b + 1))
                    if b >= 2:
                        pe.wait_ge(mixed_added, at(i, 4, b))
                    for t in range(2):
                        for h in range(2):
                            c = (2 * b + t) * P
                            last = mm(ps[:, X + b % 2, 256 * t:256 * t + 256], oT[:, h, c:c + P], w_o[:, h, :],
                                      start=(h == 0), stop=(h == 1))
                    last.then_inc(mixed_ready, 1)

                turn(0)
                turn(1)
                if not last_pair:
                    project_qks(i + 1, False, range(4, 6))
                pe.wait_ge(wo_loaded, at(i, 16, 16))
                for b in range(B):
                    project_out(b)
                    if b + 2 < B:
                        turn(b + 2)
                if not last_pair:
                    scores(i + 1, range(8))

            pe.wait_ge(scan_consts, 48)
            for e in range(ET):
                for half in range(2):
                    mm(bank(X + 2 * e + half), w_in[:, e * P:(e + 1) * P], ctxT[:, half * 512:(half + 1) * 512],
                       start=True, stop=True).then_inc(scan_mm, 1)
            pe.wait_ge(x_loaded, 16)
            project_qks(0, True, range(6))
            pe.wait_ge(scan_consts, 96)
            pe.wait_ge(u_ready, 2)
            for half in range(2):
                for e in range(ET):
                    last = mm(ps[0:XD, X + half, :], xp_w[:, e, :], u[:, e, half * 512:(half + 1) * 512],
                              start=(e == 0), stop=(e == ET - 1))
                last.then_inc(scan_mm, 1)
            pe.wait_ge(const_loaded, 48)
            scores(0, range(2))
            pe.wait_ge(x_dbl_copied, 2)
            for e in range(ET):
                for half in range(2):
                    mm(bank(X + 2 * e + half), dt_w[:, e * P:(e + 1) * P], x_dbl[0:DR, half * 512:(half + 1) * 512],
                       start=True, stop=True).then_inc(scan_mm, 1)
            scores(0, range(2, 8))
            pe.wait_ge(scan_act, 10)
            with pe.Fori(0, PAIRS - 1) as i:
                step(i, False)
            step(PAIRS - 1, True)

            def turn_x(n):
                for b in range(B):
                    pe.wait_ge(normed, 8 * n + 2 * b + 2)
                    for k in range(KD):
                        for t in range(2):
                            last = nc.tensor.transpose(ps[:, b, k * 256 + t * P:k * 256 + (t + 1) * P],
                                                       xres[:, 2 * b + t, k * P:(k + 1) * P], ident[:])
                    last.then_inc(x_turned, 1)

            for b in range(B):
                pe.wait_ge(y_gated, b + 1)
                for t in range(2):
                    for e in range(ET):
                        last = nc.tensor.transpose(ps[:, X + b, t * 256 + e * P:t * 256 + (e + 1) * P],
                                                   v[:, 2 * b + e, t * P:(t + 1) * P], ident[:])
                last.then_inc(y_turned, 1)
            turn_x(1)
            pe.wait_ge(moe_consts, 64)
            for t in range(TILES):
                if t % 2 == 0:
                    pe.wait_ge(xT_copied, t // 2 + 1)
                if t == 0:
                    pe.wait_ge(y_residual, 1)
                for k in range(KD):
                    last = mm(ps[:, X, t * E:(t + 1) * E], xT[:, k, t * P:(t + 1) * P], w_router[:, k, :],
                              start=(k == 0), stop=(k == KD - 1))
            last.then_inc(route_mm, 1)
            pe.wait_ge(route_vec, 2)
            pe.wait_ge(pool_set, 3)
            for t in range(TILES):
                for q in range(t + 1):
                    last = mm(ps[:, X + 1, t * E:(t + 1) * E], ones_bf[:] if q < t else tri_bf[:], chosen_bf[:, q, :],
                              start=(q == 0), stop=(q == t))
            for t in range(TILES):
                last = mm(ps[:, Y, 0:E], ones_bf[:], chosen_bf[:, t, :], start=(t == 0), stop=(t == TILES - 1))
            last.then_inc(route_mm, 1)
            pe.wait_ge(route_vec, 3)
            nc.tensor.transpose(ps[0:1, Y, 0:P], blk_expert[:], ident[:]).then_inc(route_mm, 1)
            for n in range(TILES * TOPK):
                t, k = n // TOPK, n % TOPK
                if k == 0:
                    pe.wait_ge(hot_ready, t + 1)
                last = mm(ps[:, Y + 1, 0:NBLK], row_hot[:, t % 2, k, :], blk_hot[:, t % 2, k, :], start=(n == 0),
                          stop=(n == TILES * TOPK - 1))
                if k == TOPK - 1:
                    last.then_inc(hot_used, 1)

            def gate_up(n, j, x_of, w):
                for k in range(KD):
                    last = mm(ps[:, 2 * j + 1, 0:2 * F], x_of(k), w[:, k, :], start=(k == 0), stop=(k == KD - 1))
                last.then_inc(gv_ready, 1)

            def turn_hid(n, j):
                pe.wait_ge(hid_ready, n + 1)
                for f in range(2):
                    last = nc.tensor.transpose(ps[0:FH, 2 * j + 1, f * P:(f + 1) * P], hid[:, j, f * FH:(f + 1) * FH], ident[:])
                last.then_inc(hid_turned, 1)

            def down(n, j, w):
                pe.wait_ge(hidT_copied, n + 1)
                for f in range(2):
                    last = mm(ps[:, 2 * j + 1, 256:512], hidT[:, j, f * P:(f + 1) * P], w[:, f, :], start=(f == 0),
                              stop=(f == 1))
                last.then_inc(down_ready, 1)

            pe.wait_ge(layer_loaded, 128)
            pe.wait_ge(tok_known, 1)
            for r in range(TILES // NJ):
                for j in range(NJ):
                    n = r * NJ + j
                    if r:
                        pe.wait_ge(down_copied, n - NJ + 1)
                    gate_up(n, j, lambda k: xT[:, k, n * P:(n + 1) * P], sh_gv)
                for j in range(NJ):
                    turn_hid(r * NJ + j, j)
                for j in range(NJ):
                    down(r * NJ + j, j, sh_dn)
            def turn_g(i, j):
                pe.wait_ge(gathered[j], at(i, 16, 16))
                for k in range(KD):
                    last = nc.tensor.transpose(ps[:, 2 * j, k * P:(k + 1) * P], xg[:, j, k * P:(k + 1) * P], ident[:])
                last.then_inc(xg_turned, 1)

            def group(i, last_group):
                def up_g(j):
                    pe.wait_ge(xgT_copied, at(i, NJ, j + 1))
                    pe.wait_ge(w_loaded[j], at(i, 16, 16))
                    pe.wait_ge(down_copied, at(i, NJ, j + 1) + TILES - NJ)
                    gate_up(i * NJ + (j + TILES), j, lambda k: xgT[:, j, k * P:(k + 1) * P], w_gv[:, j])

                def down_g(j):
                    pe.wait_ge(dn_loaded[j], at(i, 16, 16))
                    down(i * NJ + (j + TILES), j, w_dn[:, j])
                    if not last_group:
                        turn_g(i + 1, j)

                for j in range(NJ):
                    up_g(j)
                    if j >= 2:
                        turn_hid(i * NJ + (j - 2 + TILES), j - 2)
                for j in range(NJ):
                    down_g(j)
                    if j + 2 < NJ:
                        turn_hid(i * NJ + (j + 2 + TILES), j + 2)

            for j in range(NJ):
                turn_g(0, j)
            final = last_used_group(pe)
            with pe.Fori(0, final) as i:
                group(i, False)
            group(final, True)

            def copy_x_wait(n):
                pe.wait_ge(xT_copied, 4 * TURN[f"x{n}"] + 4)

            pe.wait_ge(down_copied, at(final, NJ, NJ) + TILES)
            for t in range(TILES):
                if t >= 4:
                    pe.wait_ge(turns_done, 4 * (t - 3))
                mm(bank(t % 4), ctxT[:, t * P:(t + 1) * P], x_wkv[:], start=True, stop=True).then_inc(xproj_ready, 1)
            pe.wait_ge(turns_done, 4 * TILES)
            turn_x(2)
            copy_x_wait(2)
            pe.wait_ge(layer_loaded, 240)
            for n in range(4):
                m, half = n // 2, n % 2
                for k in range(KD):
                    last = mm(bank(4 + n), l_wq[:, k, m * P:(m + 1) * P], xT[:, k, half * 512:(half + 1) * 512],
                              start=(k == 0), stop=(k == KD - 1))
                last.then_inc(lproj_ready, 1)
            for t in range(TILES):
                if t >= 4:
                    pe.wait_ge(lkv_added, 2 * (t - 3))
                for k in range(KD):
                    last = mm(bank(t % 4), xT[:, k, t * P:(t + 1) * P], l_wkv[:, k, :], start=(k == 0), stop=(k == KD - 1))
                last.then_inc(lproj_ready, 1)
            pe.wait_ge(elu_split, 8)
            for n in range(B * KD):
                b, m = n // KD, n % KD
                pe.wait_ge(elu_done, 4 + 2 * b + 2)
                if n >= 4:
                    pe.wait_ge(kv_masked, n - 3)
                c = slice(m * P, (m + 1) * P)
                for t in range(2):
                    mm(ps[:, 4 + n % 4, 0:P], lk[:, 2 * b + t, c], lv[:, 2 * b + t, c], start=(t == 0), stop=(t == 1))
                for t in range(2):
                    last = mm(ps[:, 4 + n % 4, P:KVW], lk[:, 2 * b + t, c], ones[:, 0:LB], start=(t == 0), stop=(t == 1))
                last.then_inc(kv_ready, 1)
            pe.wait_ge(elu_done, 4)
            for t in range(TILES):
                b = t // 2
                pe.wait_ge(kv_masked, KD * (b + 1))
                if t < 4:
                    pe.wait_ge(lkv_added, 2 * TILES)
                else:
                    pe.wait_ge(kv_masked, B * KD + t - 3)
                for m in range(KD):
                    last = mm(ps[:, t % 4, m * KVW:(m + 1) * KVW], lqT[:, m, t * P:(t + 1) * P], kv[:, KD * b + m, :],
                              start=True, stop=True)
                last.then_inc(kv_ready, 1)

            def turn_att(src):
                for b in range(B):
                    pe.wait_ge(kv_masked, B * KD + 2 * b + 2)
                    for k in range(KD):
                        for t in range(2):
                            last = nc.tensor.transpose(ps[:, 4 + b, k * 256 + t * P:k * 256 + (t + 1) * P],
                                                       src[:, 2 * b + t, k * P:(k + 1) * P], ident[:])
                    last.then_inc(x_turned, 1)

            def project_att(n, w):
                for t in range(TILES):
                    if n == 0:
                        pe.wait_ge(xT_copied, 4 * TURN["att0"] + t // 2 + 1)
                    if t >= 4:
                        pe.wait_ge(attended, 8 * n + t - 3)
                    for k in range(KD):
                        last = mm(ps[:, t % 4, 0:D], xT[:, k, t * P:(t + 1) * P], w[:, k, :], start=(k == 0),
                                  stop=(k == KD - 1))
                    last.then_inc(proj_out_ready, 1)

            pe.wait_ge(kv_masked, B * KD)
            turn_att(l_out)
            project_att(0, l_wo)

            turn_x(3)
            copy_x_wait(3)
            for b in range(B):
                for t in range(2):
                    for k in range(KD):
                        c = (2 * b + t) * P
                        last = mm(ps[:, 4 + b, t * 256:(t + 1) * 256], xT[:, k, c:c + P], x_wq[:, k, :], start=(k == 0),
                                  stop=(k == KD - 1))
                last.then_inc(xproj_ready, 1)
            pe.wait_ge(stacked, 12)
            pe.wait_ge(pool_set, 9)
            pe.wait_ge(turns_done, 48)

            def turn_heads(n, m, sides=(0, 1)):
                for bank_n in sides:
                    src, copied = ((q_st, qsT_copied), (k_st, ksT_copied))[bank_n]
                    pe.wait_ge(copied, at(m, 1, 1))
                    for t in range(TILES):
                        last = nc.tensor.transpose(bank(bank_n).bitcast(BF16)[:, t * P:(t + 1) * P],
                                                   src[:, t, bass.ds(n * 2, 2), :].rearrange("p a b -> p (a b)"),
                                                   ident_bf[:])
                    last.then_inc(heads_turned, 1)

            def rows(n, j, batches):
                pe.wait_ge(qsT_copied, at(n, 1, 2))
                pe.wait_ge(ksT_copied, at(n, 1, 2))
                for b in batches:
                    pe.wait_ge(rows_maxed, at(n, 4, b + 1))
                    for h in range(2):
                        r = slice(SLOT * h, SLOT * h + SLOT)
                        for q in range(2):
                            c = b * T + q * P
                            last = mm(ps[:, 4 + 2 * (b % 2) + h, q * 256:(q + 1) * 256], qsT[r, j, c:c + P],
                                      ksT[r, j, b * T:(b + 1) * T], start=True, stop=True)
                    last.then_inc(rows_ready, 1)

            def columns(g, it):
                b, jj = it // GP, it % GP
                if b == 0:
                    pe.wait_ge(qsT_copied, at(g, GP, jj + 2) + XPAIRS)
                    pe.wait_ge(ksT_copied, at(g, GP, jj + 2) + XPAIRS)
                pe.wait_ge(prob_ready, at(g, ITEMS, it + 1))
                for h in range(2):
                    r = slice(SLOT * h, SLOT * h + SLOT)
                    for k in range(2):
                        last = mm(ps[:, 4 + 2 * (it % 2) + h, k * 256:(k + 1) * 256],
                                  ksT[r, jj, b * T + k * P:b * T + (k + 1) * P], qsT[r, jj, b * T:(b + 1) * T],
                                  start=True, stop=True)
                last.then_inc(cols_ready, 1)

            def values(g, it):
                b, jj = it // GP, it % GP
                pe.wait_ge(prob_ready, at(g, ITEMS, it + 3))
                pe.wait_ge(v_placed, at(g, ITEMS, it + 1))
                if jj == 0:
                    pe.wait_ge(acc_free, at(g, B, b + 1))
                for h in range(2):
                    hh = 2 * jj + h
                    for k in range(2):
                        last = mm(ps[:, 2 + b % 2, 0:256],
                                  v_win[:, it % 2, k, h, GAP - XD_H * hh:GAP - XD_H * hh + P],
                                  probT[:, 2 * (it % 2) + h, k, :], start=(hh == 0 and k == 0),
                                  stop=(hh == GH - 1 and k == 1))
                last.then_inc(pv_ready, 1)

            def attend(g, last_group):
                for it in range(ITEMS):
                    if it < ITEMS - 1:
                        columns(g, it + 1)
                    elif not last_group:
                        columns(g + 1, 0)
                    if last_group and it == GP:
                        pe.wait_ge(ternary, 2)
                        mm(ps[:, 0, 0:2], ones[:, 0:P], f_sum[:], start=True, stop=True).then_inc(f_total, 1)
                    values(g, it)
                    if it // GP == B - 1 and not last_group:
                        turn_heads((g + 1) * GP + it % GP, (g + 1) * GP + it % GP + XPAIRS)

            def pair_rows(n, j, turn_ahead):
                rows(n, j, (0, 1))
                if turn_ahead:
                    turn_heads(n + 2, n + 2, (0,))
                rows(n, j, (2,))
                if turn_ahead:
                    turn_heads(n + 2, n + 2, (1,))
                rows(n, j, (3,))

            turn_heads(0, 0)
            turn_heads(1, 1)
            with pe.Fori(0, XPAIRS // GP - 1) as i:
                for j in range(GP):
                    pair_rows(i * GP + j, j, True)
            for j in range(GP):
                pair_rows(XPAIRS - GP + j, j, j + 2 < GP)
            pe.wait_ge(shifted, 1)
            for jj in range(GP):
                turn_heads(jj, XPAIRS + jj)
            columns(0, 0)
            with pe.Fori(0, XGROUPS - 1) as g:
                attend(g, False)
            attend(XGROUPS - 1, True)
            pe.wait_ge(acc_free, XGROUPS * B + 2)
            project_att(1, x_wo)

            turn_x(4)
            pe.wait_ge(ternary, 4)

            def up(t):
                if t % 2 == 0:
                    pe.wait_ge(part_cast, 9 + 2 * B + t // 2 + 1)
                if t >= 2:
                    pe.wait_ge(h_relu, 2 * t - 3)
                for n in range(2):
                    for j in range(3):
                        for k in range(KD):
                            last = mm(bank(2 * (t % 2) + n), x_part[:, j, k, t * P:(t + 1) * P],
                                      q_in[:, k, n * 512:(n + 1) * 512], start=(j == 0 and k == 0),
                                      stop=(j == 2 and k == KD - 1))
                last.then_inc(h_ready, 1)

            def turn_h(t):
                pe.wait_ge(hq_ready, t + 1)
                if t >= 2:
                    pe.wait_ge(hqT_copied, t - 1)
                for k in range(KH):
                    last = nc.tensor.transpose(ps[:, 4 + t % 2, :].bitcast(BF16)[:, k * P:(k + 1) * P],
                                               hid_q[:, t % 2, k * P:(k + 1) * P], ident_bf[:])
                last.then_inc(hq_turned, 1)

            def down_f(t):
                pe.wait_ge(hqT_copied, t + 1)
                if t >= 2:
                    pe.wait_ge(f_added, t - 1)
                for k in range(KH):
                    last = mm(ps[:, 6 + t % 2, 0:D], hid_q[:, 2 + t % 2, k * P:(k + 1) * P], q_out[:, k, :],
                              start=(k == 0), stop=(k == KH - 1))
                last.then_inc(f_out_ready, 1)

            up(0)
            up(1)
            for t in range(TILES):
                turn_h(t)
                if t + 2 < TILES:
                    up(t + 2)
                down_f(t)

        @block.gpsimd
        def _(pool):
            nc.gpsimd.memset(x_pad[:, :, :, 0:DC - 1], 0.0).then_inc(pool_set, 1)
            nc.gpsimd.memset(blank[:], 0.0).then_inc(pool_set, 1)
            G = nc.gpsimd
            pool.sem_inc(y_added, 2)
            pool.wait_ge(u_ready, 4)

            def steps(i):
                def drive_of(n):
                    j, e = n // 2, n % 2
                    pool.wait_ge(bc_loaded[j], at(i, 32, 32))
                    pool.wait_ge(scanned, at(i, 4, n + 1))
                    G.tensor_tensor(drive[:, n % 2], du[:, e], b_row[:, j], ALU.mult).then_inc(drive_ready, 1)

                def read_of(n):
                    j, e = n // 2, n % 2
                    pool.wait_ge(scanned, at(i, 4, n + 3))
                    G.tensor_tensor(state[:, n % 2], state[:, n % 2], c_row[:, j], ALU.mult).then_inc(read_out, 1)
                    pool.wait_ge(read_out, at(i, 4, n + 1))
                    pool.wait_ge(y_added, at(i, 4, n + 1))
                    G.tensor_tensor(y[:, e], y[:, e], state[:, n % 2], ALU.add).then_inc(y_added, 1)

                drive_of(0)
                drive_of(1)
                read_of(0)
                drive_of(2)
                read_of(1)
                drive_of(3)
                read_of(2)
                read_of(3)

            steps(0)
            with pool.Fori(1, PAIRS) as i:
                steps(i)
            pool.wait_ge(y_turned, 4)
            G.memset(ones_bf[:], 1.0).then_inc(pool_set, 1)
            G.memset(k_st[:, :, :, SHIFT:SHIFT + 3], 1.0).then_inc(pool_set, 1)
            G.memset(k_st[:, :, :, SHIFT + 3:SLOT], 0.0).then_inc(pool_set, 1)
            pool.wait_ge(tok_known, 1)
            pool.wait_ge(x_stored, 16)

            def gather(i, j, first):
                if not first:
                    pool.wait_ge(xg_turned, at(i - 1, NJ, j + 1))
                    pool.wait_ge(gathered[j], at(i, 16, 0))
                G.tensor_copy(tok_cur[:, j:j + 1], tok_of[:, bass.ds(i * NJ + j, 1)]).then_inc(tok_picked, 1)
                pool.wait_ge(tok_picked, at(i, NJ, j + 1))
                pool.sem_inc(gather_due, 1)
                G.indirect_dma_start(xg[:, j, :], None, x_dram, bass.IndirectOffsetOnAxis(ap=tok_cur[:, j:j + 1], axis=0)
                                     ).then_inc(gathered[j], 16)

            for j in range(NJ):
                gather(0, j, True)
            used = used_groups(pool)
            with pool.Fori(1, used) as i:
                for j in range(NJ):
                    gather(i, j, False)
            for j in range(NJ):
                pool.wait_ge(y_stored[j], used * 16 + 16)
            pool.sem_inc(gather_due, 1)
            for n in range(TILES * TOPK):
                if n >= 8:
                    pool.wait_ge(combined, n - 7)
                G.indirect_dma_start(yg[:, n % 8, :], None, y_dram,
                                     bass.IndirectOffsetOnAxis(ap=slot_idx[:, n // TOPK, n % TOPK:n % TOPK + 1], axis=0)
                                     ).then_inc(back[n % 8], 16)
            pool.wait_ge(normed, 32)
            G.memset(q_st[:, :, :, SHIFT:SLOT], 0.0).then_inc(pool_set, 1)
            G.memset(v_win[:], 0.0).then_inc(pool_set, 1)
            pool.wait_ge(pool_set, 7)
            for j in range(2):
                G.memset(v_win[:, j, :, :, 2 * GAP + XD_H:2 * GAP + 2 * XD_H], 1.0).then_inc(pool_set, 1)
            pool.wait_ge(xv_copied, TILES)
            pool.wait_ge(pool_set, 9)

            def place_v(g, it):
                b = it // GP
                pool.wait_ge(pv_ready, at(g, ITEMS, it + 1))
                G.tensor_copy(v_win[:, it % 2, :, :, GAP:GAP + XD_H],
                              x_v[:, 2 * b:2 * b + 2, bass.ds(g * (GP * 2 * XD_H) + it % GP * 2 * XD_H, 2 * XD_H)
                                  ].rearrange("p t (h d) -> p t h d", h=2)).then_inc(v_placed, 1)

            with pool.Fori(0, XGROUPS) as g:
                for it in range(ITEMS):
                    place_v(g, it)

        @block.scalar
        def _(act):
            def f(out, in_, func, **kw):
                return nc.scalar.activation(out, in_, func, **kw)

            def copy_qk(i, pieces):
                for n in pieces:
                    act.wait_ge(proj_ready, at(i, 14, n + 1))
                    dst = (qT, kT)[n // 2]
                    f(dst[:, (n % 2) * 512:(n % 2) * 512 + 512], bank(PJ + n % 2), ACT.Copy).then_inc(qk_copied, 1)

            def exp_slots(i):
                for n in range(2):
                    act.wait_ge(s_clipped, at(i, 2, n + 1))
                    f(eT[:, n * 512:(n + 1) * 512], sT[:, n * 512:(n + 1) * 512], ACT.Exp).then_inc(eT_ready, 1)

            def log_sums(i):
                act.wait_ge(zT_ready, at(i, 1, 1))
                f(zT[:], zT[:], ACT.Ln).then_inc(lnz_ready, 1)

            def rms(i):
                act.wait_ge(squares_read, at(i, 4, 4))
                f(log_ms[:], ss[:], ACT.Ln, scale=1.0 / DV, bias=eps_col[:]).then_inc(act_step, 1)
                act.wait_ge(act_step, at(i, 1, 2))
                f(rstd[:], log_ms[:], ACT.Exp, scale=-0.5).then_inc(rstd_ready, 1)

            def decay_of(i, n):
                j, e = n // 2, n % 2
                act.wait_ge(a_picked, at(i, 1, 1))
                act.wait_ge(scanned, at(i, 4, n + 1))
                f(decay[:, n % 2], delta[:, e], ACT.Exp, scale=a_cur[:, e, j:j + 1]).then_inc(decay_ready, 1)

            def step(i, last_pair):
                for n in range(2):
                    act.wait_ge(e_turned, at(i, 2, n + 1))
                    f(e_tok[:, 4 * n:4 * n + 4, :].rearrange("p a b -> p (a b)"), bank(X + n),
                      ACT.Copy).then_inc(e_copied, 1)
                for n in range(2):
                    act.wait_ge(z_turned, at(i, 2, n + 1))
                    f(z_inv[:, 4 * n:4 * n + 4, :].rearrange("p a b -> p (a b)"), bank(Y + n), ACT.Exp,
                      scale=-1.0).then_inc(zi_ready, 1)

                def values_and_gate(t):
                    act.wait_ge(proj_ready, at(i, 14, 7 + t))
                    f(v[:, t, :], bank(PJ + t % 2, 0, 256), ACT.Copy)
                    f(th[:, t, :], bank(PJ + t % 2, 256, 512), ACT.Tanh, scale=0.5).then_inc(tanh_ready, 1)

                decay_of(i, 0)
                for t in range(4):
                    values_and_gate(t)
                act.wait_ge(slots_shifted, at(i, 1, 1))
                f(slot_exp[:], okn[:], ACT.Exp, scale=DK ** -0.5).then_inc(slots_exp, 1)
                for t in range(4, 6):
                    values_and_gate(t)
                decay_of(i, 1)
                for t in range(6, TILES):
                    values_and_gate(t)
                for n in range(2):
                    act.wait_ge(w_turned, at(i, 2, n + 1))
                    f(wT[:, n * 512:(n + 1) * 512], bank(Y + n), ACT.Copy).then_inc(wT_copied, 1)
                decay_of(i, 2)
                nc.scalar.preload_act_table_set("natural_log_exp_and_others")
                for b in range(B):
                    act.wait_ge(o_ready, at(i, 4, b + 1))
                    if b >= 2:
                        act.wait_ge(squares_read, at(i, 4, b - 1))
                    f(sq[:, b % 2].rearrange("p a b -> p (a b)"), bank(X + b), ACT.Square).then_inc(squares_ready, 1)
                if not last_pair:
                    copy_qk(i + 1, range(2))
                rms(i)
                if not last_pair:
                    copy_qk(i + 1, range(2, 4))
                decay_of(i, 3)
                for b in range(B):
                    if b == 2 and not last_pair:
                        exp_slots(i + 1)
                    act.wait_ge(o_turned, at(i, 4, b + 1))
                    f(oT[:, :, 2 * b * P:(2 * b + 2) * P], bank(AB + b % 2).rearrange("p (h t) -> p h t", h=2), ACT.Copy,
                      scale=gn_half[:]).then_inc(oT_copied, 1)
                if not last_pair:
                    log_sums(i + 1)

            act.wait_ge(const_set, 2)
            for e in range(ET):
                for half in range(2):
                    act.wait_ge(scan_mm, 2 * e + half + 1)
                    f(x_pad[:, e, 2 * half:2 * half + 2, DC - 1:DC - 1 + T],
                      bank(X + 2 * e + half).rearrange("p (b t) -> p b t", b=2), ACT.Copy).then_inc(inner_copied, 1)
            copy_qk(0, range(4))
            act.wait_ge(scan_consts, 96)
            f(a_neg[:], a_neg[:], ACT.Exp).then_inc(a_ready, 1)
            act.wait_ge(a_ready, 1)
            nc.scalar.mul(a_neg[:], a_neg[:], -1.0).then_inc(a_ready, 1)
            for e in range(ET):
                act.wait_ge(conv_step, 4 * e + 4)
                f(aux[:, e], conv[:, e], ACT.Tanh, scale=0.5).then_inc(scan_act, 1)
            exp_slots(0)
            act.wait_ge(const_loaded, 48)
            nc.scalar.mul(gn_half[:], gn_half[:], 0.5).then_inc(act_step, 1)

            for half in range(2):
                act.wait_ge(scan_mm, 4 + half + 1)
                f(x_dbl[:, half * 512:(half + 1) * 512], ps[0:XD, X + half, :], ACT.Copy).then_inc(x_dbl_copied, 1)
            act.wait_ge(u_ready, 2)
            for e in range(ET):
                for half in range(2):
                    c = slice(half * 512, (half + 1) * 512)
                    act.wait_ge(scan_mm, 6 + 2 * e + half + 1)
                    f(delta[:, e, c], bank(X + 2 * e + half), ACT.Relu, bias=s_cols[:, e, DC + 1:DC + 2]).then_inc(scan_act, 1)
                    f(conv[:, e, c], bank(X + 2 * e + half), ACT.Abs, bias=s_cols[:, e, DC + 1:DC + 2]).then_inc(scan_act, 1)
            act.wait_ge(scan_act, 10)
            f(conv[:], conv[:], ACT.Exp, scale=-1.0).then_inc(scan_act, 1)
            nc.scalar.preload_act_table_set("natural_log_exp_and_others")
            act.wait_ge(softplus_step, 1)
            f(aux2[:], aux[:], ACT.Ln).then_inc(scan_act, 1)
            log_sums(0)
            act.wait_ge(u_ready, 4)
            with act.Fori(0, PAIRS - 1) as i:
                step(i, False)
            step(PAIRS - 1, True)

            def norm_scale(n):
                nc.scalar.preload_act_table_set("natural_log_exp_and_others")
                act.wait_ge(ln_moments, n + 1)
                f(ln_var[:], moments[:, :, 1], ACT.Ln, bias=eps_col[:]).then_inc(ln_scale, 1)
                act.wait_ge(ln_scale, 2 * n + 1)
                f(ln_rstd[:], ln_var[:], ACT.Exp, scale=-0.5).then_inc(ln_scale, 1)

            def copy_xT(n):
                for b in range(B):
                    act.wait_ge(x_turned, 4 * TURN[f"x{n}"] + b + 1)
                    f(xT[:, :, b * 256:(b + 1) * 256], bank(b).rearrange("p (k t) -> p k t", k=KD),
                      ACT.Copy).then_inc(xT_copied, 1)

            norm_scale(0)
            for b in range(B):
                act.wait_ge(normed, 2 * b + 2)
                f(th[:, 2 * b:2 * b + 2, :], xres[:, 2 * b:2 * b + 2, :], ACT.Tanh, scale=0.5).then_inc(tanh_ready, 1)
            norm_scale(1)
            copy_xT(1)
            act.wait_ge(route_vec, 1)
            f(score[:, :, 0:E], score[:, :, 0:E], ACT.Exp).then_inc(route_act, 1)
            act.wait_ge(route_mm, 3)
            f(expert_row[:], ps[0:1, Y, 0:P], ACT.Copy).then_inc(route_act, 1)

            def g_tanh_of(n, j):
                act.wait_ge(gv_ready, n + 1)
                f(g_th[:, j, :], ps[:, 2 * j + 1, 0:F], ACT.Tanh, scale=0.5).then_inc(g_tanh, 1)

            def hidT_of(n, j):
                act.wait_ge(hid_turned, n + 1)
                f(hidT[:, j, :], ps[0:FH, 2 * j + 1, 0:2 * P], ACT.Copy).then_inc(hidT_copied, 1)

            for r in range(TILES // NJ):
                for j in range(NJ):
                    g_tanh_of(r * NJ + j, j)
                for j in range(NJ):
                    hidT_of(r * NJ + j, j)
            def xgT_of(i, j, first):
                act.wait_ge(xg_turned, at(i, NJ, j + 1))
                if not first:
                    act.wait_ge(gv_ready, at(i, NJ, j + 1) + TILES - NJ)
                f(xgT[:, j, :], ps[:, 2 * j, 0:KD * P], ACT.Copy).then_inc(xgT_copied, 1)

            def group(i, last_group):
                for j in range(NJ):
                    g_tanh_of(i * NJ + (j + TILES), j)
                    if j >= 2:
                        hidT_of(i * NJ + (j - 2 + TILES), j - 2)
                for j in range(NJ):
                    if j + 2 < NJ:
                        hidT_of(i * NJ + (j + 2 + TILES), j + 2)
                    if not last_group:
                        xgT_of(i + 1, j, False)

            for j in range(NJ):
                xgT_of(0, j, True)
            final = last_used_group(act)
            with act.Fori(0, final) as i:
                group(i, False)
            group(final, True)

            def hqT_of(t):
                act.wait_ge(hq_turned, t + 1)
                if t >= 2:
                    act.wait_ge(f_out_ready, t - 1)
                f(hid_q[:, 2 + t % 2], ps[:, 4 + t % 2, :].bitcast(BF16), ACT.Copy).then_inc(hqT_copied, 1)

            act.wait_ge(angle, 6)
            f(cos_sin[:], ang[:], ACT.Sin).then_inc(cos_sin_ready, 1)
            for t in range(TILES):
                act.wait_ge(xproj_ready, t + 1)
                f(x_v[:, t, :], bank(t % 4, 256, 512),
                  ACT.Copy).then_inc(xv_copied, 1)
            act.wait_ge(rotated, 2 * TILES)
            for j in range(3):
                if j:
                    act.wait_ge(part_rest, j)
                f(key_part[:, j], key_f32[:], ACT.Copy).then_inc(part_cast, 1)
            act.wait_ge(part_cast, 3)
            for slot_n in range(3, 6):
                f(k_st[:, :, :, slot_n * XD_H:(slot_n + 1) * XD_H],
                  key_part[:, K_PARTS[slot_n]].rearrange("p t (h d) -> p t h d", h=XH), ACT.Copy).then_inc(stacked, 1)
            norm_scale(2)
            copy_xT(2)
            for n in range(4):
                act.wait_ge(elu_split, 2 * n + 2)
                f(lq_low[:, n % 2, :], lq_low[:, n % 2, :], ACT.Exp).then_inc(elu_exp, 1)
            for t in range(TILES):
                act.wait_ge(elu_split, 8 + t + 1)
                f(lk_low[:, t % 2, :], lk_low[:, t % 2, :], ACT.Exp).then_inc(elu_exp, 1)

            def copy_attT(n):
                for b in range(B):
                    act.wait_ge(x_turned, 4 * TURN[f"att{n}"] + b + 1)
                    f(xT[:, :, b * 256:(b + 1) * 256], bank(4 + b).rearrange("p (k t) -> p k t", k=KD),
                      ACT.Copy).then_inc(xT_copied, 1)

            copy_attT(0)
            norm_scale(3)
            copy_xT(3)

            for j in range(3):
                for half in range(2):
                    r = slice(4 * half, 4 * half + 4)
                    if j:
                        act.wait_ge(part_rest, 2 + 2 * (j - 1) + half + 1)
                    else:
                        act.wait_ge(rotated, 2 * TILES + 4 * (half + 1))
                    f(part[:, j, r], q_rot[:, r], ACT.Copy).then_inc(part_cast, 1)
            act.sem_inc(qsT_copied, 1)
            act.sem_inc(ksT_copied, 1)
            act.sem_inc(prob_ready, 2)
            act.sem_inc(pv_ready, 2)

            def copy_q(m, j):
                act.wait_ge(heads_turned, at(m, 2, 1))
                f(qsT[:, j], bank(0).bitcast(BF16), ACT.Copy).then_inc(qsT_copied, 1)

            with act.Fori(0, XPAIRS // GP) as i:
                for j in range(GP):
                    copy_q(i * GP + j, j)
                    act.wait_ge(heads_turned, at(i * GP + j, 2, 2))
                    f(ksT[:, j], bank(1).bitcast(BF16), ACT.Copy).then_inc(ksT_copied, 1)

            def probs(g, it):
                act.wait_ge(cols_ready, at(g, ITEMS, it + 1))
                f(probT[:, 2 * (it % 2):2 * (it % 2) + 2].rearrange("p a k n -> p (a k n)"), pair(4 + 2 * (it % 2)),
                  ACT.Exp, scale=XD_H ** -0.5).then_inc(prob_ready, 1)

            for jj in range(GP):
                copy_q(XPAIRS + jj, jj)
            with act.Fori(0, XGROUPS - 1) as g:
                for it in range(ITEMS):
                    probs(g, it)
                    if it > ITEMS - GP:
                        copy_q((g + 1) * GP + it - (ITEMS - GP + 1) + XPAIRS, it - (ITEMS - GP + 1))
                copy_q((g + 1) * GP + GP - 1 + XPAIRS, GP - 1)
            for it in range(ITEMS):
                probs(XGROUPS - 1, it)
            norm_scale(4)
            copy_xT(4)
            for j in range(3):
                for b in range(B):
                    c = slice(b * T, (b + 1) * T)
                    if j:
                        act.wait_ge(part_rest, 6 + B * (j - 1) + b + 1)
                    else:
                        act.wait_ge(xT_copied, 4 * TURN["x4"] + b + 1)
                    f(x_part[:, j, :, c], xT[:, :, c], ACT.Copy).then_inc(part_cast, 1)
            for t in range(TILES):
                act.wait_ge(h_ready, t + 1)
                if t >= 2:
                    act.wait_ge(hq_ready, t - 1)
                for n in range(2):
                    last = f(hid_f[:, t % 2, n * 512:(n + 1) * 512], bank(2 * (t % 2) + n), ACT.Relu, scale=f_scale[:, 0:1])
                last.then_inc(h_relu, 1)
                act.wait_ge(h_relu, 2 * t + 1)
                f(hid_f[:, t % 2], hid_f[:, t % 2], ACT.Square).then_inc(h_relu, 1)
                if t:
                    hqT_of(t - 1)
            hqT_of(TILES - 1)
            norm_scale(5)

        @block.vector
        def _(dve):
            V = nc.vector
            V.memset(ones[:], 1.0).then_inc(const_set, 1)
            V.memset(eps_col[:], LN_EPS).then_inc(const_set, 1)
            dve.wait_ge(const_set, 2)
            CHAIN = 5
            dve.sem_inc(scanned, 2)
            dve.sem_inc(mixed_added, 1)
            dve.sem_inc(acc_free, 2)
            dve.sem_inc(rows_maxed, 2)
            steps = [0]

            def then(ins):
                steps[0] += 1
                ins.then_inc(chain, 1)
                dve.wait_ge(chain, steps[0])

            def clip_slots(i):
                for n in range(2):
                    dve.wait_ge(proj_ready, at(i, 14, 5 + n))
                    V.tensor_scalar(sT[:, n * 512:(n + 1) * 512], bank(PJ + n % 2), CLAMP, -CLAMP,
                                    ALU.min, ALU.max).then_inc(s_clipped, 1)

            def sum_slots(i):
                dve.wait_ge(eT_ready, at(i, 2, 2))
                for b in range(B):
                    last = V.tensor_tensor_scan(zT[:, b * T:(b + 1) * T], ones[:], eT[:, b * T:(b + 1) * T], 0.0,
                                                ALU.mult, ALU.add)
                last.then_inc(zT_ready, 1)

            def scan(i, n):
                j, e = n // 2, n % 2
                dve.wait_ge(decay_ready, at(i, 4, n + 1))
                dve.wait_ge(drive_ready, at(i, 4, n + 1))
                dve.wait_ge(y_added, at(i, 4, n + 1))
                for b in range(B):
                    c = slice(b * T, (b + 1) * T)
                    last = V.tensor_tensor_scan(state[:, n % 2, c], decay[:, n % 2, c], drive[:, n % 2, c], 0.0,
                                                ALU.mult, ALU.add)
                last.then_inc(scanned, 1)

            def stats_of(t):
                then(V.bn_stats(stats[:, t, :], xres[:, t, :]))
                ins = V.bn_aggr(moments[:, t, :], stats[:, t, :])
                if t == TILES - 1:
                    ins.then_inc(ln_moments, 1)

            def mask_scores(i):
                for n in range(8):
                    dve.wait_ge(scores_ready, at(i, 8, n + 1))
                    V.tensor_tensor(aT[:, n, :], ps[:, AB + n % 2, 0:384], tri[:], ALU.mult).then_inc(scores_masked, 1)

            def step(i, last_pair):
                def gate(t):
                    dve.wait_ge(tanh_ready, at(i, 8, t + 1))
                    V.scalar_tensor_tensor(out=th[:, t, :], in0=th[:, t, :], scalar=1.0,
                                           in1=bank(PJ + t % 2, 256, 512), op0=ALU.add,
                                           op1=ALU.mult).then_inc(gate_ready, 1)

                gate(0)
                gate(1)
                dve.wait_ge(slots_ready, at(i, 1, 1))
                dve.wait_ge(zi_ready, at(i, 2, 2))
                okf = okn[:].rearrange("p a b -> p (a b)")
                zif = z_inv[:].rearrange("p a b -> p (a b)")
                V.tensor_tensor(okf, pair(X), zif, ALU.mult).then_inc(vec_step, 1)
                dve.wait_ge(vec_step, at(i, CHAIN, 1))
                V.tensor_reduce(okmax[:], okn[:], AX.X, ALU.max).then_inc(vec_step, 1)
                gate(2)
                dve.wait_ge(vec_step, at(i, CHAIN, 2))
                V.tensor_tensor(okn[:], okn[:], okmax[:].unsqueeze(2).to_broadcast([P, TILES * 2, M]),
                                ALU.subtract).then_inc(slots_shifted, 1)

                gate(3)
                dve.wait_ge(slots_exp, at(i, 1, 1))
                V.tensor_reduce(slot_sum[:], slot_exp[:], AX.X, ALU.add).then_inc(vec_step, 1)
                gate(4)
                dve.wait_ge(vec_step, at(i, CHAIN, 3))
                V.reciprocal(slot_sum[:], slot_sum[:]).then_inc(vec_step, 1)
                V.tensor_tensor(slot_exp[:].rearrange("p a b -> p (a b)"), slot_exp[:].rearrange("p a b -> p (a b)"), zif,
                                ALU.mult).then_inc(vec_step, 1)
                gate(5)
                dve.wait_ge(vec_step, at(i, CHAIN, 5))
                V.tensor_tensor(okn[:], slot_exp[:], slot_sum[:].unsqueeze(2).to_broadcast([P, TILES * 2, M]),
                                ALU.mult).then_inc(w_ready, 1)
                scan(i, 0)
                for t in range(6, TILES):
                    gate(t)
                scan(i, 1)
                for n in range(8):
                    dve.wait_ge(read_ready, at(i, 8, n + 1))
                    V.tensor_tensor(aT[:, n, :], ps[:, AB + n % 2, 0:384], tri[:], ALU.mult).then_inc(read_masked, 1)
                scan(i, 2)
                for b in range(B):
                    dve.wait_ge(squares_ready, at(i, 4, b + 1))
                    V.tensor_reduce(ss[:, 4 * b:4 * b + 4], sq[:, b % 2], AX.X, ALU.add).then_inc(squares_read, 1)
                dve.wait_ge(rstd_ready, at(i, 1, 1))
                def scale_o(b):
                    r = slice(4 * b, 4 * b + 4)
                    V.tensor_tensor(on[:, r, :], bank(X + b).rearrange("p (a b) -> p a b", a=4),
                                    rstd[:, r].unsqueeze(2).to_broadcast([P, 4, DV]), ALU.mult).then_inc(o_scaled, 1)

                def gate_o(b):
                    r = slice(4 * b, 4 * b + 4)
                    dve.wait_ge(o_scaled, at(i, 4, b + 1))
                    V.tensor_tensor(on[:, r, :].rearrange("p a b -> p (a b)"), on[:, r, :].rearrange("p a b -> p (a b)"),
                                    th[:, 2 * b:2 * b + 2, :].rearrange("p a b -> p (a b)"),
                                    ALU.mult).then_inc(o_gated, 1)

                scale_o(0)
                for b in range(B):
                    if b < B - 1:
                        scale_o(b + 1)
                    gate_o(b)
                if not last_pair:
                    dve.wait_ge(decay_ready, at(i, 4, 4))
                    V.tensor_copy(a_cur[:], a_neg[:, :, bass.ds(2 * i + 2, 2)]).then_inc(a_picked, 1)
                    clip_slots(i + 1)
                    sum_slots(i + 1)
                scan(i, 3)
                for b in range(B):
                    dve.wait_ge(mixed_ready, at(i, 4, b + 1))
                    r = xres[:, 2 * b:2 * b + 2, :].rearrange("p a b -> p (a b)")
                    if b == 0:
                        dve.wait_ge(mixed_added, at(i, 4, 1))
                    V.tensor_tensor(r, r, bank(X + b % 2), ALU.add).then_inc(mixed_added, 1)
                    if last_pair:
                        dve.wait_ge(mixed_added, at(i, 4, b + 2))
                        stats_of(2 * b)
                        stats_of(2 * b + 1)
                if not last_pair:
                    mask_scores(i + 1)

            dve.wait_ge(pool_set, 1)
            dve.wait_ge(scan_consts, 48)
            for e in range(ET):
                dve.wait_ge(inner_copied, 2 * e + 2)
                out = conv[:, e].rearrange("p (b t) -> p b t", b=B)
                for tap in range(DC):
                    x_tap = x_pad[:, e, :, tap:tap + T]
                    if tap == 0:
                        ins = V.tensor_scalar(out, x_tap, s_cols[:, e, 0:1], s_cols[:, e, DC:DC + 1], ALU.mult, ALU.add)
                    else:
                        dve.wait_ge(conv_step, 4 * e + tap)
                        ins = V.scalar_tensor_tensor(out=out, in0=x_tap, scalar=s_cols[:, e, tap:tap + 1], in1=out,
                                                     op0=ALU.mult, op1=ALU.add)
                    ins.then_inc(conv_step, 1)
            clip_slots(0)
            for e in range(ET):
                dve.wait_ge(scan_act, e + 1)
                V.tensor_scalar(aux[:, e], aux[:, e], 0.5, 0.5, ALU.mult, ALU.add).then_inc(conv_step, 1)
                dve.wait_ge(conv_step, 9 + e)
                V.tensor_tensor(u[:, e], aux[:, e], conv[:, e], ALU.mult).then_inc(u_ready, 1)
            sum_slots(0)
            dve.wait_ge(const_loaded, 48)
            mask_scores(0)
            dve.wait_ge(scan_act, 11)
            V.tensor_scalar(aux[:], conv[:], 1.0, None, ALU.add).then_inc(softplus_step, 1)
            dve.wait_ge(softplus_step, 1)
            dve.wait_ge(scan_act, 12)
            V.scalar_tensor_tensor(out=conv[:], in0=aux[:], scalar=-1.0, in1=conv[:], op0=ALU.add,
                                   op1=ALU.subtract).then_inc(softplus_step, 1)
            V.tensor_tensor(delta[:], delta[:], aux2[:], ALU.add).then_inc(softplus_step, 1)
            dve.wait_ge(softplus_step, 3)
            V.tensor_tensor(delta[:], delta[:], conv[:], ALU.subtract).then_inc(softplus_step, 1)
            dve.wait_ge(softplus_step, 4)
            V.tensor_tensor(du[:], delta[:], u[:], ALU.mult).then_inc(u_ready, 1)
            for e in range(ET):
                last = V.tensor_scalar(y[:, e], u[:, e], s_cols[:, e, DC + 2:DC + 3], None, ALU.mult)
            last.then_inc(u_ready, 1)
            dve.wait_ge(a_ready, 2)
            V.tensor_copy(a_cur[:], a_neg[:, :, 0:2]).then_inc(a_picked, 1)
            dve.wait_ge(x_loaded, 32)
            with dve.Fori(0, PAIRS - 1) as i:
                step(i, False)
            step(PAIRS - 1, True)

            def norm(n):
                dve.wait_ge(ln_scale, 2 * n + 2)
                then(V.scalar_tensor_tensor(out=ln_shift[:], in0=moments[:, :, 0], scalar=-1.0, in1=ln_rstd[:],
                                            op0=ALU.mult, op1=ALU.mult))
                for t in range(TILES):
                    V.tensor_scalar(xres[:, t, :], xres[:, t, :], ln_rstd[:, t:t + 1], ln_shift[:, t:t + 1],
                                    ALU.mult, ALU.add).then_inc(normed, 1)

            norm(0)
            dve.wait_ge(y_added, 4 * PAIRS + 2)
            for b in range(B):
                r = slice(2 * b, 2 * b + 2)
                dve.wait_ge(tanh_ready, TILES * PAIRS + b + 1)
                then(V.scalar_tensor_tensor(out=v[:, r, :], in0=th[:, r, :], scalar=1.0, in1=xres[:, r, :], op0=ALU.add,
                                            op1=ALU.mult))
                V.tensor_tensor(v[:, r, :], v[:, r, :], y[:, :, b * T:(b + 1) * T], ALU.mult).then_inc(y_gated, 1)
            for b in range(B):
                dve.wait_ge(y_turned, b + 1)
                r = xres[:, 2 * b:2 * b + 2, :].rearrange("p a b -> p (a b)")
                V.scalar_tensor_tensor(out=r, in0=bank(X + b), scalar=0.5, in1=r, op0=ALU.mult,
                                       op1=ALU.add).then_inc(y_residual, 1)
                dve.wait_ge(y_residual, b + 1)
                for t in range(2):
                    stats_of(2 * b + t)
            norm(1)
            dve.wait_ge(route_mm, 1)
            logits = bank(X).rearrange("p (t e) -> p t e", t=TILES)
            def per_tile(col, n):
                return col.unsqueeze(2).to_broadcast([P, TILES, n])

            then(V.tensor_reduce(top_logit[:], logits, AX.X, ALU.max))
            V.memset(score[:, :, E:SC], -7.0)
            V.tensor_tensor(score[:, :, 0:E], logits, per_tile(top_logit[:], E), ALU.subtract).then_inc(route_vec, 1)
            dve.wait_ge(route_act, 1)
            then(V.tensor_reduce(score_sum[:], score[:, :, 0:E], AX.X, ALU.add))
            then(V.reciprocal(score_sum[:], score_sum[:]))
            then(V.tensor_tensor(score[:, :, 0:E], score[:, :, 0:E], per_tile(score_sum[:], E), ALU.mult))
            for t in range(TILES):
                last = V.max(top8[:, t, :], score[:, t, 0:E])
            then(last)
            then(V.memset(top8[:, :, TOPK:8], -7.0))
            for t in range(TILES):
                last = V.match_replace(score_rest[:, t, :], top8[:, t, :], score[:, t, :], -9.0)
            then(last)
            then(V.tensor_tensor(chosen[:], score[:, :, 0:E], score_rest[:, :, 0:E], ALU.not_equal))
            V.tensor_copy(chosen_bf[:], chosen[:]).then_inc(route_vec, 1)
            dve.wait_ge(route_mm, 2)
            then(V.tensor_scalar(blocks[:], ps[:, Y, 0:E], P - 1.0, 1.0 / P, ALU.add, ALU.mult))
            then(V.tensor_scalar(blocks[:], blocks[:], -0.498, ROUND, ALU.add, ALU.add))
            then(V.tensor_scalar(blocks[:], blocks[:], -ROUND, None, ALU.add))
            then(V.tensor_tensor_scan(blk_end[:], ones[:, 0:E], blocks[:], 0.0, ALU.mult, ALU.add))
            then(V.tensor_tensor(blk_row[:], blk_end[:], blocks[:], ALU.subtract))
            then(V.tensor_scalar(late[:], blk_end[:], tok_id[:, 0:1], None, ALU.is_le))
            then(V.tensor_reduce(blk_expert[:], late[:], AX.X, ALU.add))
            V.tensor_scalar(blk_expert[:], blk_expert[:], E - 1.0, None, ALU.min).then_inc(route_vec, 1)
            then(V.tensor_scalar(groups_f[:], blk_end[0:1, E - 1:E], 1.0 / NJ, (NJ - 1.0) / NJ - 0.498, ALU.mult, ALU.add))
            then(V.tensor_scalar(groups_f[:], groups_f[:], ROUND, None, ALU.add))
            V.tensor_scalar(groups[:, 0:1], groups_f[:], -ROUND, None, ALU.add)
            V.tensor_scalar(groups[:, 1:2], groups_f[:], -ROUND, -1.0, ALU.add, ALU.add).then_inc(groups_known, 1)
            then(V.tensor_scalar(blk_row[:], blk_row[:], float(P), 1.0, ALU.mult, ALU.add))
            then(V.tensor_tensor(place[:], bank(X + 1).rearrange("p (t e) -> p t e", t=TILES),
                                 blk_row[:].unsqueeze(1).to_broadcast([P, TILES, E]), ALU.add))
            then(V.tensor_tensor(place[:], place[:], chosen[:], ALU.mult))
            for t in range(TILES):
                last = V.max(place8[:, t, :], place[:, t, :])
            then(last)
            then(V.tensor_scalar(slot[:], place8[:, :, 0:TOPK], -1.0, None, ALU.add))
            then(V.tensor_copy(slot_idx[:], slot[:]))
            then(V.tensor_scalar(slot_blk[:], slot[:], 1.0 / P, -0.498, ALU.mult, ALU.add))
            then(V.tensor_scalar(slot_blk[:], slot_blk[:], ROUND, None, ALU.add))
            then(V.tensor_scalar(slot_blk[:], slot_blk[:], -ROUND, None, ALU.add))
            then(V.scalar_tensor_tensor(out=slot_row[:], in0=slot_blk[:], scalar=-float(P), in1=slot[:], op0=ALU.mult,
                                        op1=ALU.add))
            for t in range(TILES):
                if t >= 2:
                    dve.wait_ge(hot_used, t - 1)
                V.tensor_tensor(row_hot[:, t % 2], iota[:].unsqueeze(1).to_broadcast([P, TOPK, P]),
                                slot_row[:, t, :].unsqueeze(2).to_broadcast([P, TOPK, P]), ALU.is_equal)
                then(V.tensor_tensor(blk_hot[:, t % 2], iota[:, 0:NBLK].unsqueeze(1).to_broadcast([P, TOPK, NBLK]),
                                     slot_blk[:, t, :].unsqueeze(2).to_broadcast([P, TOPK, NBLK]), ALU.is_equal))
                V.tensor_scalar(blk_hot[:, t % 2], blk_hot[:, t % 2], tok_id[:, t:t + 1], None,
                                ALU.mult).then_inc(hot_ready, 1)
            dve.wait_ge(hot_used, TILES)
            V.tensor_copy(tok_of[:], ps[:, Y + 1, 0:NBLK]).then_inc(tok_known, 1)

            def hidden(n, j):
                dve.wait_ge(g_tanh, n + 1)
                V.scalar_tensor_tensor(out=g_th[:, j, :], in0=g_th[:, j, :], scalar=1.0, in1=ps[:, 2 * j + 1, 0:F],
                                       op0=ALU.add, op1=ALU.mult).then_inc(g_silu, 1)
                dve.wait_ge(g_silu, n + 1)
                V.tensor_tensor(hid[:, j, :], g_th[:, j, :], ps[:, 2 * j + 1, F:2 * F], ALU.mult).then_inc(hid_ready, 1)

            for r in range(TILES // NJ):
                for j in range(NJ):
                    hidden(r * NJ + j, j)
                for j in range(NJ):
                    n = r * NJ + j
                    dve.wait_ge(down_ready, n + 1)
                    if n == 0:
                        dve.wait_ge(x_stored, 16)
                    V.scalar_tensor_tensor(out=xres[:, n, :], in0=ps[:, 2 * j + 1, 256:512], scalar=0.5, in1=xres[:, n, :],
                                           op0=ALU.mult, op1=ALU.add).then_inc(down_copied, 1)
            dve.wait_ge(layer_loaded, 128)
            pi = float(np.pi)
            for half, freq in enumerate((1.0, 0.01)):
                for n in range(2):
                    out = ang[:, :, n, half::2]
                    last = V.tensor_scalar(out, pos[:], freq, (0.5 * pi, 0.0)[n], ALU.mult, ALU.add)
            last.then_inc(angle, 1)
            dve.wait_ge(angle, 1)
            V.tensor_scalar(turns[:], ang[:], 0.5 / pi, ROUND, ALU.mult, ALU.add).then_inc(angle, 1)
            dve.wait_ge(angle, 2)
            V.tensor_scalar(turns[:], turns[:], -ROUND, None, ALU.add).then_inc(angle, 1)
            dve.wait_ge(angle, 3)
            V.scalar_tensor_tensor(out=ang[:], in0=turns[:], scalar=-2.0 * pi, in1=ang[:], op0=ALU.mult,
                                   op1=ALU.add).then_inc(angle, 1)
            dve.wait_ge(angle, 4)
            in_pi = 3.1415925
            V.tensor_scalar(ang[:], ang[:], in_pi, -in_pi, ALU.min, ALU.max).then_inc(angle, 2)
            def group(i):
                for j in range(NJ):
                    hidden(i * NJ + (j + TILES), j)
                for j in range(NJ):
                    dve.wait_ge(down_ready, i * NJ + (j + TILES + 1))
                    dve.wait_ge(y_stored[j], at(i, 16, 16))
                    V.tensor_scalar(y_out[:, j, :], ps[:, 2 * j + 1, 256:512], 0.5, None, ALU.mult).then_inc(down_copied, 1)

            def pick_weights(t):
                def step_done(c):
                    dve.wait_ge(vec_step, at(t, 3, c) + CHAIN * PAIRS)

                def row(m, n):
                    return m[:, bass.ds(t, 1), 0:n].rearrange("p a n -> p (a n)")

                step_done(0)
                V.tensor_tensor(pick[:], row(place, E).unsqueeze(1).to_broadcast([P, TOPK, E]),
                                row(place8, TOPK).unsqueeze(2).to_broadcast([P, TOPK, E]), ALU.is_equal).then_inc(vec_step, 1)
                step_done(1)
                V.tensor_tensor(pick[:], pick[:], row(score, E).unsqueeze(1).to_broadcast([P, TOPK, E]),
                                ALU.mult).then_inc(vec_step, 1)
                step_done(2)
                V.tensor_reduce(row(pick_w, TOPK), pick[:], AX.X, ALU.add).then_inc(vec_step, 1)

            with dve.Fori(0, TILES) as i:
                group(i)
                pick_weights(i)
            with dve.Fori(TILES, used_groups(dve)) as i:
                group(i)
            dve.wait_ge(vec_step, 3 * TILES + CHAIN * PAIRS)
            def rotate(src, dst, prods, tiles, n, size):
                pairs = src.rearrange("p (t h c two) -> p t h c two", t=tiles.stop - tiles.start, h=XH, two=2)
                out = dst[:, tiles, :].rearrange("p t (h c two) -> p t h c two", h=XH, two=2)
                shape = [P, tiles.stop - tiles.start, XH, 4]
                for turn in range(2):
                    for two in range(2):
                        w = cos_sin[:, tiles, turn ^ two, :].unsqueeze(2).to_broadcast(shape)
                        prod = prods[:, turn, two, 0:size].rearrange("p (t h c) -> p t h c", t=shape[1], h=XH)
                        V.tensor_tensor(prod, pairs[:, :, :, :, two], w, ALU.mult).then_inc(turns_done, 1)
                dve.wait_ge(turns_done, 4 * n + 4)
                for turn in range(2):
                    o = out[:, :, :, :, turn]
                    p0, p1 = (prods[:, turn, two, 0:size].rearrange("p (t h c) -> p t h c", t=shape[1], h=XH) for two in range(2))
                    V.tensor_tensor(o, p0, p1, (ALU.subtract, ALU.add)[turn]).then_inc(rotated, 1)
                dve.wait_ge(rotated, 2 * n + 2)

            def rotate_key(t):
                dve.wait_ge(xv_copied, t + 1)
                rotate(bank(t % 4, 0, 256), key_f32, key_rot, slice(t, t + 1), t, P)

            def rest(j):
                dve.wait_ge(part_cast, j + 1)
                V.tensor_tensor(key_f32[:], key_f32[:], key_part[:, j], ALU.subtract).then_inc(part_rest, 1)

            def stack(slot_n, j, parts, dst):
                V.tensor_copy(dst[:, :, :, slot_n * XD_H:(slot_n + 1) * XD_H],
                              parts[:, j].rearrange("p t (h d) -> p t h d", h=XH)).then_inc(stacked, 1)

            for n in range(TILES * TOPK):
                t, k = n // TOPK, n % TOPK
                dve.wait_ge(back[n % 8], 16 * (n // 8 + 1))
                if n:
                    dve.wait_ge(combined, n)
                V.scalar_tensor_tensor(out=xres[:, t, :], in0=yg[:, n % 8, :], scalar=pick_w[:, t, k:k + 1],
                                       in1=xres[:, t, :], op0=ALU.mult, op1=ALU.add).then_inc(combined, 1)
                if k == TOPK - 1:
                    dve.wait_ge(combined, n + 1)
                    stats_of(t)
                if t < 4 and k % 3 == 2:
                    rotate_key(2 * t + k // 3)
                elif t in (4, 5) and k == 5:
                    rest(t - 4)
                elif t == 6 and k % 2 == 1:
                    dve.wait_ge(part_cast, 3)
                    slot_n = k // 2
                    stack(slot_n, K_PARTS[slot_n], key_part, k_st)
            norm(2)
            dve.wait_ge(layer_loaded, 240)
            for t in range(TILES):
                if t % 2 == 0:
                    dve.wait_ge(x_turned, 4 * TURN["x2"] + t // 2 + 1)
                V.tensor_tensor(xres[:, t, :], xres[:, t, :], l_bo[:], ALU.add).then_inc(bias_added, 1)

            def add_exp(n):
                m, c = n // 2, slice((n % 2) * 512, (n % 2) * 512 + 512)
                dve.wait_ge(elu_exp, n + 1)
                V.tensor_tensor(lqT[:, m, c], lqT[:, m, c], lq_low[:, n % 2, :], ALU.add).then_inc(elu_done, 1)

            for n in range(4):
                m, c = n // 2, slice((n % 2) * 512, (n % 2) * 512 + 512)
                dve.wait_ge(lproj_ready, n + 1)
                if n >= 2:
                    dve.wait_ge(elu_done, n - 1)
                V.tensor_scalar(lq_low[:, n % 2, :], bank(4 + n), l_bq[:, m:m + 1], 0.0, ALU.add, ALU.min).then_inc(elu_split, 1)
                V.tensor_scalar(lqT[:, m, c], bank(4 + n), l_bq[:, m:m + 1], 0.0, ALU.add, ALU.max).then_inc(elu_split, 1)
                if n:
                    add_exp(n - 1)
            add_exp(3)

            def finish_k(t):
                dve.wait_ge(elu_exp, 4 + t + 1)
                V.scalar_tensor_tensor(out=lk[:, t, :], in0=lk[:, t, :], scalar=0.0, in1=lk_low[:, t % 2, :], op0=ALU.max,
                                       op1=ALU.add).then_inc(elu_done, 1)

            for t in range(TILES):
                dve.wait_ge(lproj_ready, 4 + t + 1)
                V.tensor_tensor(lk[:, t, :], bank(t % 4, 0, 256), l_bkv[:, 0:D], ALU.add).then_inc(lkv_added, 1)
                V.tensor_tensor(lv[:, t, :], bank(t % 4, 256, 512), l_bkv[:, D:2 * D], ALU.add).then_inc(lkv_added, 1)
                dve.wait_ge(lkv_added, 2 * t + 1)
                if t >= 2:
                    dve.wait_ge(elu_done, 4 + t - 1)
                V.tensor_scalar(lk_low[:, t % 2, :], lk[:, t, :], 0.0, None, ALU.min).then_inc(elu_split, 1)
                if t:
                    finish_k(t - 1)
            finish_k(TILES - 1)
            for n in range(B * KD):
                dve.wait_ge(kv_ready, n + 1)
                V.tensor_tensor(kv[:, n, :], ps[:, 4 + n % 4, 0:KVW], head_mask[:], ALU.mult).then_inc(kv_masked, 1)
            for t in range(TILES):
                dve.wait_ge(kv_ready, B * KD + t + 1)
                src = ps[:, t % 4, 0:KD * KVW].rearrange("p (k n) -> p k n", k=KD)
                then(V.tensor_scalar(l_den[:, t], src[:, :, P:KVW], 1e-8, None, ALU.add))
                then(V.reciprocal(l_den[:, t], l_den[:, t]))
                for k in range(KD):
                    last = V.tensor_tensor(l_out[:, t, k * P:(k + 1) * P].rearrange("p (h d) -> p h d", h=LB),
                                           src[:, k, 0:P].rearrange("p (h d) -> p h d", h=LB),
                                           l_den[:, t, k, :].unsqueeze(2).to_broadcast([P, LB, P // LB]), ALU.mult)
                last.then_inc(kv_masked, 1)

            def add_att(n):
                for t in range(TILES):
                    dve.wait_ge(proj_out_ready, 8 * n + t + 1)
                    dve.wait_ge(bias_added, 8 * n + t + 1)
                    V.tensor_tensor(xres[:, t, :], xres[:, t, :], ps[:, t % 4, 0:D], ALU.add).then_inc(attended, 1)
                    dve.wait_ge(attended, 8 * n + t + 1)
                    stats_of(t)

            add_att(0)
            norm(3)
            for t in range(TILES):
                if t % 2 == 0:
                    dve.wait_ge(x_turned, 4 * TURN["x3"] + t // 2 + 1)
                V.tensor_tensor(xres[:, t, :], xres[:, t, :], x_bo[:], ALU.add).then_inc(bias_added, 1)
            for b in range(B):
                dve.wait_ge(xproj_ready, TILES + b + 1)
                rotate(bank(4 + b), q_rot, rot, slice(2 * b, 2 * b + 2), TILES + b, 256)
            for j in range(3):
                if j < 2:
                    for half in range(2):
                        r = slice(4 * half, 4 * half + 4)
                        dve.wait_ge(part_cast, 3 + 2 * j + half + 1)
                        V.tensor_tensor(q_rot[:, r], q_rot[:, r], part[:, j, r], ALU.subtract).then_inc(part_rest, 1)
                dve.wait_ge(part_cast, 3 + 2 * j + 2)
                for slot_n in range(6):
                    if Q_PARTS[slot_n] == j:
                        stack(slot_n, j, part, q_st)
            with dve.Fori(0, XPAIRS) as i:
                for b in range(B):
                    dve.wait_ge(rows_ready, at(i, 4, b + 1))
                    V.tensor_reduce(row_max[:, bass.ds(i * 16 + 4 * b, 4)],
                                    pair(4 + 2 * (b % 2)).rearrange("p (a k) -> p a k", a=4), AX.X,
                                    ALU.max).then_inc(rows_maxed, 1)
            dve.wait_ge(rows_maxed, 4 * XPAIRS + 2)
            then(V.tensor_scalar(row_max[:], row_max[:], -1.0, None, ALU.mult))
            for j in range(3):
                then(V.tensor_copy(shift[:, j], row_max[:]))
                if j < 2:
                    then(V.tensor_tensor(row_max[:], row_max[:], shift[:, j], ALU.subtract))
                for b in range(B):
                    last = V.tensor_copy(
                        q_st[:, 2 * b:2 * b + 2, :, SHIFT + j].rearrange("p q (i h) -> p q i h", h=2),
                        shift[:, j].rearrange("p (i b h q) -> p b q i h", b=B, h=2, q=2)[:, b])
            last.then_inc(shifted, 1)

            def copy_k(n, j):
                dve.wait_ge(heads_turned, at(n + XPAIRS, 2, 2))
                V.tensor_copy(ksT[:, j], bank(1).bitcast(BF16)).then_inc(ksT_copied, 1)

            def divide(g, b):
                dve.wait_ge(pv_ready, at(g, ITEMS, (b + 1) * GP) + 2)
                then(V.reciprocal(x_den[:, b % 2], ps[P // 2:P, 2 + b % 2, 0:256]))
                rows = slice(P // 2 * (g % 2), P // 2 * (g % 2 + 1))
                V.tensor_tensor(xT[rows, g // 2, b * T:(b + 1) * T], ps[0:P // 2, 2 + b % 2, 0:256], x_den[:, b % 2],
                                ALU.mult).then_inc(acc_free, 1)

            def size_of(w, n):
                dve.wait_ge(layer_loaded, 272)
                V.tensor_reduce(f_sum[:, n:n + 1], w[:].rearrange("p a b -> p (a b)"), AX.X, ALU.add,
                                apply_absolute_value=True).then_inc(ternary, 1)

            def ternary_step(b):
                if b == 0:
                    dve.wait_ge(f_total, 1)
                    then(V.tensor_scalar(f_scale[:], ps[:, 0, 0:2], 1.0 / (D * HF), 1e-5, ALU.mult, ALU.max))
                    then(V.reciprocal(f_inv[:], f_scale[:]))
                    return
                n, w, q = ((0, f_in, q_in), (1, f_out, q_out))[b - 1]
                then(V.tensor_scalar(w[:], w[:], f_inv[:, n:n + 1], ROUND, ALU.mult, ALU.add))
                then(V.tensor_scalar(w[:], w[:], -ROUND, 1.0, ALU.add, ALU.min))
                V.tensor_scalar(q[:], w[:], -1.0, None, ALU.max).then_inc(ternary, 1)

            for jj in range(GP):
                copy_k(jj, jj)
            for g in range(XGROUPS):
                for b in range(B - 1):
                    divide(g, b)
                    if g == 1 and b < 2:
                        size_of((f_in, f_out)[b], b)
                    if g == XGROUPS - 1:
                        ternary_step(b)
                if g < XGROUPS - 1:
                    for jj in range(GP):
                        copy_k((g + 1) * GP + jj, jj)
                divide(g, B - 1)
            add_att(1)
            norm(4)
            for j in range(2):
                for b in range(B):
                    c = slice(b * T, (b + 1) * T)
                    dve.wait_ge(part_cast, 9 + B * j + b + 1)
                    V.tensor_tensor(xT[:, :, c], xT[:, :, c], x_part[:, j, :, c], ALU.subtract).then_inc(part_rest, 1)

            def quantize(t):
                j = t % 2
                dve.wait_ge(h_relu, 2 * t + 2)
                then(V.tensor_reduce(f_max[:, j:j + 1], hid_f[:, j], AX.X, ALU.max))
                then(V.tensor_scalar(f_max[:, j:j + 1], f_max[:, j:j + 1], 1e-5, None, ALU.max))
                V.reciprocal(f_rmax[:, j:j + 1], f_max[:, j:j + 1])
                then(V.tensor_scalar(f_back[:, j:j + 1], f_max[:, j:j + 1], f_scale[:, 1:2], 1.0 / 255, ALU.mult,
                                     ALU.mult))
                then(V.tensor_scalar(hid_f[:, j], hid_f[:, j], f_rmax[:, j:j + 1], 255.0, ALU.mult, ALU.mult))
                if t >= 2:
                    dve.wait_ge(hq_turned, t - 1)
                V.tensor_scalar(hid_q[:, j], hid_f[:, j], ROUND, -ROUND, ALU.add, ALU.add).then_inc(hq_ready, 1)

            def add_ffn(t):
                dve.wait_ge(f_out_ready, t + 1)
                V.scalar_tensor_tensor(out=xres[:, t, :], in0=ps[:, 6 + t % 2, 0:D], scalar=f_back[:, t % 2:t % 2 + 1],
                                       in1=xres[:, t, :], op0=ALU.mult, op1=ALU.add).then_inc(f_added, 1)
                dve.wait_ge(f_added, t + 1)
                stats_of(t)

            for t in range(TILES):
                quantize(t)
                if t:
                    add_ffn(t - 1)
            add_ffn(TILES - 1)
            norm(5)


def host_layout(inp):
    g = {k: np.asarray(v) for k, v in inp.items()}
    x = g["x"].reshape(TOK, D)

    def kp(w):
        return w.reshape(-1, P, w.shape[-1]).transpose(1, 0, 2)

    q, k, s = (kp(g["L0_attn_W" + n]).reshape(P, KD, PAIRS, P) for n in "qks")
    v, w = (kp(g["L0_attn_W" + n]).reshape(P, KD, PAIRS, 256) for n in "vg")
    t = np.triu(np.ones((P, P), np.float32))
    col = {n: g["L0_xattn_" + n].reshape(ET, P, -1) for n in ("conv_w", "conv_b", "dt_proj_b", "D", "A_log")}
    out = dict(
        x_tok=x.reshape(TILES, P, D).transpose(1, 0, 2), xT=kp(x.T),
        wqks=np.concatenate([q, k, s], 3).transpose(2, 0, 1, 3), wvg=np.concatenate([v, w], 3).transpose(2, 0, 1, 3),
        wo=g["L0_attn_Wo"].reshape(PAIRS, 2, DV, D).transpose(0, 2, 1, 3),
        gnorm=g["L0_attn_g_norm_weight"].reshape(P, 1),
        ident=np.eye(P, dtype=np.float32), tri=np.concatenate([t, np.ones((P, P), np.float32), t], 1),
        ctxT=g["ctx_1024"].reshape(TOK, CTX).T, w_in=g["L0_xattn_in_proj_w"].T, xp_w=kp(g["L0_xattn_x_proj_w"].T),
        dt_w=g["L0_xattn_dt_proj_w"].T,
        s_cols=np.concatenate([col[n] for n in ("conv_w", "conv_b", "dt_proj_b", "D")], 2).transpose(1, 0, 2),
        a_log=col["A_log"].transpose(1, 0, 2),
    )
    def ffn(gate, value, down):
        lead = gate.shape[:-2]
        gv = np.concatenate([gate, value], -1).reshape(*lead, KD, P, 2 * F)
        return np.moveaxis(gv, -3, -2), np.moveaxis(down.reshape(*lead, 2, FH, D), -3, -2)

    out["w_router"] = kp(g["L0_ffn_w_router"].T)
    out["w_gv"], out["w_dn"] = ffn(g["L0_ffn_wg"], g["L0_ffn_wv"], g["L0_ffn_wo"])
    out["sh_gv"], out["sh_dn"] = ffn(g["L0_ffn_swg"], g["L0_ffn_swv"], g["L0_ffn_swo"])
    bf16 = mybir.dt.np(BF16)
    out["iota"] = np.tile(np.arange(P, dtype=np.float32), (P, 1))
    out["tok_id"] = np.arange(TOK, dtype=np.float32).reshape(TILES, P).T
    out["tri_bf"] = np.triu(np.ones((P, P), np.float32), 1).astype(bf16)
    out["l_wq"], out["l_wo"] = kp(g["L1_attn_wq"].T), kp(g["L1_attn_wo"].T)
    out["l_wkv"] = np.concatenate([kp(g["L1_attn_wk"].T), kp(g["L1_attn_wv"].T)], 2)
    out["l_bq"] = g["L1_attn_bq"].reshape(KD, P).T
    out["l_bkv"] = np.concatenate([g["L1_attn_bk"], g["L1_attn_bv"]]).reshape(1, 2 * D)
    out["l_bo"] = g["L1_attn_bo"].reshape(1, D)
    same = np.arange(P)[:, None] // (P // LB)
    out["head_mask"] = np.concatenate([same == same.T, same == np.arange(LB)], 1).astype(np.float32)
    out["x_wq"], out["x_wo"] = kp(g["L1_xattn_Wq"]), kp(g["L1_xattn_Wout"])
    out["x_wkv"], out["x_bo"] = g["L1_xattn_Wkv"], g["L1_xattn_bout"].reshape(1, D)
    out["pos"] = kp(g["fside_BxSx2_0"].reshape(TOK, 2))
    out["ident_bf"] = np.eye(P, dtype=np.float32).astype(bf16)
    out["f_in"], out["f_out"] = kp(g["L1_ffn_c_fc"]), kp(g["L1_ffn_c_proj"].T)
    return {n: np.ascontiguousarray(m) for n, m in out.items()}


def kernel(**inputs):
    from concourse import bacc
    from concourse.bass_utils import run_bass_kernel_spmd

    nc = bacc.Bacc("TRN2", target_bir_lowering=False, num_devices=1)
    arrays = {"in_" + name: array for name, array in host_layout(inputs).items()}
    args = {name[3:]: nc.dram_tensor(name, m.shape, mybir.dt.from_np(m.dtype), kind="ExternalInput").ap()
            for name, m in arrays.items()}
    out = nc.dram_tensor("out", (B, T, D), F32, kind="ExternalOutput").ap()
    build(nc, args, out)
    return run_bass_kernel_spmd(nc, [arrays], core_ids=[0]).results[0]["out"]
```
